# Optimizing a Trainium2 kernel written in Bass

```python
import numpy as np
import jax
import jax.numpy as jnp

def _softmax(x, axis=-1):
    return jax.nn.softmax(x, axis=axis)

def _gelu(x):
    return jax.nn.gelu(x, approximate=True)

def _silu(x):
    return jax.nn.silu(x)

def _sigmoid(x):
    return jax.nn.sigmoid(x)

def _layernorm(x, axis=-1, eps=1e-05):
    m = jnp.mean(x, axis=axis, keepdims=True)
    v = jnp.var(x, axis=axis, keepdims=True)
    return (x - m) / jnp.sqrt(v + eps)

def _scatter_add(tgt, idx, src, axis=0):
    return tgt.at[idx].add(src)

def _segment_sum(src, seg, n):
    return jax.ops.segment_sum(src, seg, n)
kernel_name = 'mk_prb_d1_jaxref_r4_a27d94'

def setup_inputs(seed: int=0):
    np.random.seed(seed)
    _w = jnp.asarray

    def _L0_attn_setup():
        import jax, jax.numpy as jnp
        import numpy as np
        B, L, D_MODEL = (2, 256, 256)
        EXPAND = 2
        D_INNER = EXPAND * D_MODEL
        D_STATE = 16
        D_CONV = 4
        DT_RANK = D_MODEL // 16

        def _mamba(x, W_in, conv_w, conv_b, W_xproj, W_dt, b_dt, A_log, D_skip, W_out):
            b, l, _ = x.shape
            xz = jnp.einsum('bld,de->ble', x, W_in)
            x_in, z = jnp.split(xz, 2, axis=-1)
            xt = jnp.transpose(x_in, (0, 2, 1))
            xt = jnp.pad(xt, ((0, 0), (0, 0), (D_CONV - 1, 0)))
            conv = jax.lax.conv_general_dilated(xt, conv_w, window_strides=(1,), padding='VALID', dimension_numbers=('NCH', 'OIH', 'NCH'), feature_group_count=D_INNER)
            conv = conv + conv_b[None, :, None]
            u = jax.nn.silu(jnp.transpose(conv, (0, 2, 1)))
            x_dbl = jnp.einsum('bld,de->ble', u, W_xproj)
            dt_lr = x_dbl[..., :DT_RANK]
            Bm = x_dbl[..., DT_RANK:DT_RANK + D_STATE]
            Cm = x_dbl[..., DT_RANK + D_STATE:]
            delta = jax.nn.softplus(jnp.einsum('blr,rd->bld', dt_lr, W_dt) + b_dt)
            A = -jnp.exp(A_log)
            dA = jnp.exp(jnp.einsum('bld,dn->bldn', delta, A))
            dBu = (delta * u)[..., None] * Bm[:, :, None, :]

            def step(h, inp):
                dA_t, dBu_t, C_t = inp
                h = dA_t * h + dBu_t
                y_t = jnp.einsum('bdn,bn->bd', h, C_t)
                return (h, y_t)
            h0 = jnp.zeros((b, D_INNER, D_STATE), x.dtype)
            _, ys = jax.lax.scan(step, h0, (jnp.swapaxes(dA, 0, 1), jnp.swapaxes(dBu, 0, 1), jnp.swapaxes(Cm, 0, 1)))
            y = jnp.swapaxes(ys, 0, 1)
            y = y + D_skip * u
            y = y * jax.nn.silu(z)
            out = jnp.einsum('bld,de->ble', y, W_out)
            return out
        key = jax.random.key(seed)
        ks = jax.random.split(key, 8)
        s = 0.02
        x = jax.random.normal(ks[0], (B, L, D_MODEL), jnp.float32)
        W_in = jax.random.normal(ks[1], (D_MODEL, 2 * D_INNER), jnp.float32) * s
        conv_w = jax.random.normal(ks[2], (D_INNER, 1, D_CONV), jnp.float32) * 0.2
        conv_b = jnp.zeros((D_INNER,), jnp.float32)
        W_xproj = jax.random.normal(ks[3], (D_INNER, DT_RANK + 2 * D_STATE), jnp.float32) * s
        W_dt = jax.random.normal(ks[4], (DT_RANK, D_INNER), jnp.float32) * DT_RANK ** (-0.5)
        b_dt = jnp.full((D_INNER,), -4.6, jnp.float32)
        A_log = jnp.log(jnp.broadcast_to(jnp.arange(1, D_STATE + 1, dtype=jnp.float32), (D_INNER, D_STATE)))
        D_skip = jnp.ones((D_INNER,), jnp.float32)
        W_out = jax.random.normal(ks[5], (D_INNER, D_MODEL), jnp.float32) * s
        return dict(x=x, W_in=W_in, conv_w=conv_w, conv_b=conv_b, W_xproj=W_xproj, W_dt=W_dt, b_dt=b_dt, A_log=A_log, D_skip=D_skip, W_out=W_out)
    _L0_attn_in = _L0_attn_setup()

    def _L0_ffn_setup():
        import jax, jax.numpy as jnp
        import numpy as np
        IN_DIM = 256
        HIDDEN = 256
        OUT_DIM = 256
        NUM_EXPERTS = 16
        TOP_K = 2
        ROUTER_TEMP = 1.0
        LN_EPS = 1e-05

        def _layernorm(h, g, b):
            mu = jnp.mean(h, axis=-1, keepdims=True)
            var = jnp.mean(jnp.square(h - mu), axis=-1, keepdims=True)
            return (h - mu) * jax.lax.rsqrt(var + LN_EPS) * g + b
        key = jax.random.key(seed)
        ks = jax.random.split(key, 8)
        s_in = 1.0 / np.sqrt(IN_DIM)
        s_h = 1.0 / np.sqrt(HIDDEN)
        x = jax.random.normal(ks[0], (4, 512, IN_DIM), dtype=jnp.float32)
        Wr = jax.random.uniform(ks[1], (IN_DIM, NUM_EXPERTS), jnp.float32, -s_in, s_in)
        br = jax.random.uniform(ks[2], (NUM_EXPERTS,), jnp.float32, -s_in, s_in)
        W1 = jax.random.uniform(ks[3], (NUM_EXPERTS, IN_DIM, HIDDEN), jnp.float32, -s_in, s_in)
        b1 = jax.random.uniform(ks[4], (NUM_EXPERTS, HIDDEN), jnp.float32, -s_in, s_in)
        g1 = jnp.ones((NUM_EXPERTS, HIDDEN), jnp.float32)
        be1 = jnp.zeros((NUM_EXPERTS, HIDDEN), jnp.float32)
        W2 = jax.random.uniform(ks[5], (NUM_EXPERTS, HIDDEN, OUT_DIM), jnp.float32, -s_h, s_h)
        b2 = jax.random.uniform(ks[6], (NUM_EXPERTS, OUT_DIM), jnp.float32, -s_h, s_h)
        return {'x': x, 'Wr': Wr, 'br': br, 'W1': W1, 'b1': b1, 'g1': g1, 'be1': be1, 'W2': W2, 'b2': b2}
    _L0_ffn_in = _L0_ffn_setup()
    _d = {'L0_attn_x': _L0_attn_in['x'], 'L0_attn_W_in': _L0_attn_in['W_in'], 'L0_attn_conv_w': _L0_attn_in['conv_w'], 'L0_attn_conv_b': _L0_attn_in['conv_b'], 'L0_attn_W_xproj': _L0_attn_in['W_xproj'], 'L0_attn_W_dt': _L0_attn_in['W_dt'], 'L0_attn_b_dt': _L0_attn_in['b_dt'], 'L0_attn_A_log': _L0_attn_in['A_log'], 'L0_attn_D_skip': _L0_attn_in['D_skip'], 'L0_attn_W_out': _L0_attn_in['W_out'], 'L0_ffn_Wr': _L0_ffn_in['Wr'], 'L0_ffn_br': _L0_ffn_in['br'], 'L0_ffn_W1': _L0_ffn_in['W1'], 'L0_ffn_b1': _L0_ffn_in['b1'], 'L0_ffn_g1': _L0_ffn_in['g1'], 'L0_ffn_be1': _L0_ffn_in['be1'], 'L0_ffn_W2': _L0_ffn_in['W2'], 'L0_ffn_b2': _L0_ffn_in['b2']}
    _x0 = _d['L0_attn_x']
    _d['L0_attn_x'] = jax.random.normal(jax.random.fold_in(jax.random.key(seed), 1), (2, 2048, 256), dtype=_x0.dtype)
    del _x0
    return _d

def reference(L0_attn_x, L0_attn_W_in, L0_attn_conv_w, L0_attn_conv_b, L0_attn_W_xproj, L0_attn_W_dt, L0_attn_b_dt, L0_attn_A_log, L0_attn_D_skip, L0_attn_W_out, L0_ffn_Wr, L0_ffn_br, L0_ffn_W1, L0_ffn_b1, L0_ffn_g1, L0_ffn_be1, L0_ffn_W2, L0_ffn_b2):

    def _L0_attn_ref(x, W_in, conv_w, conv_b, W_xproj, W_dt, b_dt, A_log, D_skip, W_out):
        import jax, jax.numpy as jnp
        import numpy as np
        B, L, D_MODEL = (2, 256, 256)
        EXPAND = 2
        D_INNER = EXPAND * D_MODEL
        D_STATE = 16
        D_CONV = 4
        DT_RANK = D_MODEL // 16

        def _mamba(x, W_in, conv_w, conv_b, W_xproj, W_dt, b_dt, A_log, D_skip, W_out):
            b, l, _ = x.shape
            xz = jnp.einsum('bld,de->ble', x, W_in)
            x_in, z = jnp.split(xz, 2, axis=-1)
            xt = jnp.transpose(x_in, (0, 2, 1))
            xt = jnp.pad(xt, ((0, 0), (0, 0), (D_CONV - 1, 0)))
            conv = jax.lax.conv_general_dilated(xt, conv_w, window_strides=(1,), padding='VALID', dimension_numbers=('NCH', 'OIH', 'NCH'), feature_group_count=D_INNER)
            conv = conv + conv_b[None, :, None]
            u = jax.nn.silu(jnp.transpose(conv, (0, 2, 1)))
            x_dbl = jnp.einsum('bld,de->ble', u, W_xproj)
            dt_lr = x_dbl[..., :DT_RANK]
            Bm = x_dbl[..., DT_RANK:DT_RANK + D_STATE]
            Cm = x_dbl[..., DT_RANK + D_STATE:]
            delta = jax.nn.softplus(jnp.einsum('blr,rd->bld', dt_lr, W_dt) + b_dt)
            A = -jnp.exp(A_log)
            dA = jnp.exp(jnp.einsum('bld,dn->bldn', delta, A))
            dBu = (delta * u)[..., None] * Bm[:, :, None, :]

            def step(h, inp):
                dA_t, dBu_t, C_t = inp
                h = dA_t * h + dBu_t
                y_t = jnp.einsum('bdn,bn->bd', h, C_t)
                return (h, y_t)
            h0 = jnp.zeros((b, D_INNER, D_STATE), x.dtype)
            _, ys = jax.lax.scan(step, h0, (jnp.swapaxes(dA, 0, 1), jnp.swapaxes(dBu, 0, 1), jnp.swapaxes(Cm, 0, 1)))
            y = jnp.swapaxes(ys, 0, 1)
            y = y + D_skip * u
            y = y * jax.nn.silu(z)
            out = jnp.einsum('bld,de->ble', y, W_out)
            return out
        return _mamba(x, W_in, conv_w, conv_b, W_xproj, W_dt, b_dt, A_log, D_skip, W_out)

    def _L0_ffn_ref(x, Wr, br, W1, b1, g1, be1, W2, b2):
        import jax, jax.numpy as jnp
        import numpy as np
        IN_DIM = 256
        HIDDEN = 256
        OUT_DIM = 256
        NUM_EXPERTS = 16
        TOP_K = 2
        ROUTER_TEMP = 1.0
        LN_EPS = 1e-05

        def _layernorm(h, g, b):
            mu = jnp.mean(h, axis=-1, keepdims=True)
            var = jnp.mean(jnp.square(h - mu), axis=-1, keepdims=True)
            return (h - mu) * jax.lax.rsqrt(var + LN_EPS) * g + b
        orig_shape = x.shape[:-1]
        x_flat = x.reshape(-1, x.shape[-1])
        logits = (x_flat @ Wr + br) / max(ROUTER_TEMP, 1e-06)
        probs = jax.nn.softmax(logits, axis=-1)
        topk_w, topk_idx = jax.lax.top_k(probs, TOP_K)
        topk_w = topk_w / jnp.clip(jnp.sum(topk_w, axis=-1, keepdims=True), 1e-09)
        h = jnp.einsum('nc,ech->neh', x_flat, W1) + b1
        h = _layernorm(h, g1, be1)
        h = jax.nn.gelu(h, approximate=False)
        expert_out = jnp.einsum('neh,eho->neo', h, W2) + b2
        sel = jnp.take_along_axis(expert_out, topk_idx[:, :, None], axis=1)
        y_flat = jnp.sum(sel * topk_w[:, :, None], axis=1)
        return y_flat.reshape(*orig_shape, y_flat.shape[-1])
    x = L0_attn_x
    xn = _layernorm(x, axis=-1)
    x = x + _L0_attn_ref(xn, L0_attn_W_in, L0_attn_conv_w, L0_attn_conv_b, L0_attn_W_xproj, L0_attn_W_dt, L0_attn_b_dt, L0_attn_A_log, L0_attn_D_skip, L0_attn_W_out) + _L0_ffn_ref(xn, L0_ffn_Wr, L0_ffn_br, L0_ffn_W1, L0_ffn_b1, L0_ffn_g1, L0_ffn_be1, L0_ffn_W2, L0_ffn_b2)
    return x

_drawn_inputs = setup_inputs


def setup_inputs(seed=0):
    import zlib

    import numpy as np

    out = dict(_drawn_inputs(seed))
    spreads = {'L0_attn_conv_b': (0.0, 0.1),
     'L0_attn_b_dt': (-4.599999904632568, 0.2),
     'L0_attn_D_skip': (1.0, 0.2),
     'L0_ffn_g1': (1.0, 0.2),
     'L0_ffn_be1': (0.0, 0.1)}
    factors = {}
    for name, (base, spread) in spreads.items():
        noise = np.random.default_rng([zlib.crc32(name.encode()), seed]).standard_normal(out[name].shape)
        drawn = base * np.exp(spread * noise) if base else spread * noise
        out[name] = jnp.asarray(drawn.astype(out[name].dtype))
    for name, factor in factors.items():
        out[name] = (out[name] * factor).astype(out[name].dtype)
    return out
```

```python
from contextlib import ExitStack

import concourse.bass as bass
from concourse import mybir

F32, BF16, I32 = mybir.dt.float32, mybir.dt.bfloat16, mybir.dt.int32
ALU, ACT, AX = mybir.AluOpType, mybir.ActivationFunctionType, mybir.AxisListType

P = 128
NB, L, D = 2, 2048, 256
DI, NS, R = 512, 16, 16
KW = 4
E = 16
NT = NB * L
TILES = NT // P
T = 512
TT = T // P
NC = NT // T
CPB = L // T
DC = DI // P
KC = D // P
UN = DC * NS
GT = 4
NG = 3
MT = 80
EPS = 1e-5
LAG = 4
LEAD_B = 1
LEAD_A = 3
HR = 8
GR = 4
BIG = 1e38
assert UN % 3 == 1
assert MT >= 2 * NT // P + E - 1 and MT % GT == 0


def build(nc, x, W_in, conv_w, conv_b, W_xproj, W_dt, b_dt, A_log, D_skip, W_out,
          Wr, br, W1, b1, g1, be1, W2, b2, out):
    ctx = ExitStack()
    with ctx:
        def sb(name, shape, dt=F32):
            return ctx.enter_context(nc.sbuf_tensor(name, shape, dt))

        def psum(name):
            return ctx.enter_context(nc.psum_tensor(name, [P, 512], F32))

        def sem(name):
            return ctx.enter_context(nc.semaphore(name))

        def dram(name, shape, dt=F32):
            return nc.dram_tensor(name, shape, dt, kind="Internal").ap()

        xn_d = dram("xn_d", (NT, D))
        xnT_d = dram("xnT_d", (NC, P, KC, T))
        xs_d = dram("xs_d", (MT * P, D))
        ys_d = dram("ys_d", (MT * P, D))
        om_d = dram("om_d", (NT, D))
        b_d = dram("b_d", (6, E * D), BF16)

        w1 = sb("w1", [P, E, KC, D])
        w2r = sb("w2r", [P, GT, KC, D])
        win = sb("win", [P, KC, 2 * DI])
        wout = sb("wout", [P, DC, D])
        wxd = sb("wxd", [P, DC, P])
        wdt = sb("wdt", [P, DI])
        wr = sb("wr", [P, KC, E])
        brr = sb("brr", [1, E])
        cw = sb("cw", [P, DC, KW])
        cb = sb("cb", [P, DC])
        bdt = sb("bdt", [P, DC])
        dsk = sb("dsk", [P, DC])
        aneg = sb("aneg", [P, DC, NS])
        g1t = sb("g1t", [P, E, KC])
        be1t = sb("be1t", [P, E, KC])
        bias6 = sb("bias6", [6, E * D], BF16)
        ident = sb("ident", [P, P])
        upper = sb("upper", [P, P], BF16)
        onesb = sb("onesb", [P, P], BF16)
        ones1 = sb("ones1", [1, P])
        pick6 = sb("pick6", [6, 2, P], BF16)
        sel = sb("sel", [P, 2 * NS], BF16)
        keep = sb("keep", [P, NC + 1])
        mhalf = sb("mhalf", [P, TT])
        xnT = sb("xnT", [P, KC, T])
        xin = sb("xin", [P, 2, T + KW - 1])
        halo = sb("halo", [P, DC, KW - 1])
        u = sb("u", [P, DC, T])
        Du = sb("Du", [P, DC, T])
        delta = sb("delta", [P, DC, T])
        du = sb("du", [P, DC, T])
        tmpA = sb("tmpA", [P, 2, T])
        xr = sb("xr", [P, T])
        stackN = sb("stackN", [P, T], BF16)
        stack = sb("stack", [P, T], BF16)
        Cb = sb("Cb", [P, NS, T])
        hb = sb("hb", [P, HR, T])
        hc = sb("hc", [P, GR, T])
        carry = sb("carry", [P, UN])
        zs = sb("zs", [P, TT, DI])
        ygT = sb("ygT", [P, 2, DC, P])
        om = sb("om", [P, TT, D])
        xg = sb("xg", [P, GT, D])
        xgT = sb("xgT", [P, 2, KC, P])
        hn = sb("hn", [P, 2, D])
        hnT = sb("hnT", [P, GT, KC, P])
        yo = sb("yo", [P, GT, D])
        st = sb("st", [P, 2, TT, 6])
        mv = sb("mv", [P, 2, TT, 2])
        ve = sb("ve", [P, 2, TT])
        rstd = sb("rstd", [P, 2, TT])
        slots = sb("slots", [P, 2, TILES], I32)
        wk = sb("wk", [P, 2, TILES])
        etab = sb("etab", [P, MT], I32)
        small = sb("small", [P, 12, TILES])
        idx = sb("idx", [P, 2, 2 * TT], I32)

        def half(t, k):
            return t[:, 2 * k:2 * k + 2, :].rearrange("p a (b d) -> p (a b) d", d=D)

        xraw = [half(delta, k) for k in range(2)]
        xnb = [half(du, k) for k in range(2)]
        xnTg = [u[:, 2 * k:2 * k + 2, :] for k in range(2)]
        lg = zs[:, 3, :]
        iotaE, reset, iotaJ = zs[:, 0, :], zs[:, 1, :], zs[:, 2, :]
        Du_flat = Du[:, :, :].rearrange("p a b -> p (a b)")
        iotaT = Du_flat[:, 0:MT * E]
        Cb_flat = Cb[:, :, :].rearrange("p a b -> p (a b)")
        bparts = [om[:, 1, 32 * k:32 * k + 32].bitcast(BF16) for k in range(3)]
        xsrc = xg

        psB = [psum(f"psB{i}") for i in range(3)]
        psY = [psum(f"psY{i}") for i in range(2)]
        psP = [psum(f"psP{i}") for i in range(2)]
        psE = psum("psE")

        s_w = {k: sem(f"s_w_{k}") for k in ("early", "w1", "bias", "bst", "big")}
        s_plain = sem("s_plain")
        s_zero, s_wz = sem("s_zero"), sem("s_wz")
        s_const, s_cdve, s_a = sem("s_const"), sem("s_cdve"), sem("s_a")
        s_xl = [sem(f"s_xl{k}") for k in range(2)]
        s_xst = [sem(f"s_xst{k}") for k in range(2)]
        s_tst = [sem(f"s_tst{k}") for k in range(2)]
        s_bn, s_mv, s_ve, s_rs, s_xn = sem("s_bn"), sem("s_mv"), sem("s_ve"), sem("s_rs"), sem("s_xn")
        s_tp, s_te, s_lm, s_lg = sem("s_tp"), sem("s_te"), sem("s_lm"), sem("s_lg")
        s_rt, s_rtd, s_rte, s_rank = sem("s_rt"), sem("s_rtd"), sem("s_rte"), sem("s_rank")
        s_route = sem("s_route")
        s_bbc, s_dbu, s_exp, s_scan, s_carry, s_g, s_tr = (sem(n) for n in (
            "s_bbc", "s_dbu", "s_exp", "s_scan", "s_carry", "s_g", "s_tr"))
        s_xT, s_xp, s_xe, s_cv, s_halo, s_u, s_xd, s_stk, s_stack = (sem(n) for n in (
            "s_xT", "s_xp", "s_xe", "s_cv", "s_halo", "s_u", "s_xd", "s_stk", "s_stack"))
        s_dm, s_dl, s_ab, s_ln, s_dadd, s_delta, s_Du = (sem(n) for n in (
            "s_dm", "s_dl", "s_ab", "s_ln", "s_dadd", "s_delta", "s_Du"))
        s_cm, s_cb = sem("s_cm"), sem("s_cb")
        s_zm, s_zc, s_z, s_gate = sem("s_zm"), sem("s_zc"), sem("s_z"), sem("s_gate")
        s_etm, s_et, s_eom, s_eo, s_om = sem("s_etm"), sem("s_et"), sem("s_eom"), sem("s_eo"), sem("s_om")
        s_scl = [sem(f"s_scl{k}") for k in range(4)]
        s_sc = [sem(f"s_sc{k}") for k in range(4)]
        s_xg, s_w2, s_ys = sem("s_xg"), sem("s_w2"), sem("s_ys")
        s_t1, s_mx, s_m1, s_mbn, s_mag, s_mve, s_mrs, s_mh, s_t2, s_mn, s_mg, s_m2, s_my = (sem(n) for n in (
            "s_t1", "s_mx", "s_m1", "s_mbn", "s_mag", "s_mve", "s_mrs", "s_mh", "s_t2", "s_mn", "s_mg",
            "s_m2", "s_my"))
        s_fx = [sem(f"s_fx{k}") for k in range(2)]
        s_fg = [sem(f"s_fg{k}") for k in range(2)]
        s_fo = [sem(f"s_fo{k}") for k in range(2)]
        s_fi, s_fa = sem("s_fi"), sem("s_fa")

        ahead = [s_carry, s_eom, s_fa, s_lg, s_m2, s_my, s_om, s_t1, s_te, s_tp, s_ys,
                 *s_fo, *s_tst, *s_xst]

        def wait(eng, s, value):
            if isinstance(value, int) and value <= 0:
                return
            value = value + 1 if any(s is a for a in ahead) else value
            assert isinstance(value, int) or value.min_val > 0
            eng.wait_ge(s, value)

        def col(ap, i):
            return ap[:, i:i + 1]

        def plain(eng):
            eng.sem_inc(s_plain, 1)

        FIRST, MID, LAST = "first", "mid", "last"

        def ring3(s):
            return s % 3 if s < UN - 1 else 1

        def before3(s):
            return {0: -4, 1: -1, 2: -2, UN - 1: UN - 3}.get(s, s - 3)

        jobs = {e: [[] for _ in range(UN)] for e in ("pe", "act", "dve", "pool", "sp")}

        def job(engine, slot, family):
            def add(fn):
                jobs[engine][slot].append((family, fn))
            return add

        def present(family, kind):
            return {"P": kind in ("pre", FIRST, MID), "W": kind in (FIRST, MID, LAST),
                    "Z": kind in (FIRST, MID, LAST), "E": kind in (MID, LAST, "post"),
                    "M": kind in (MID, LAST), "S": kind == FIRST}[family]

        uses = []

        def use(name, family, released):
            uses.append((name, family, released))

        for n in (13, 14, 15):
            use(f"C{n}", "W", lambda it, n=n: (s_cb, it * NS + n + 1))
        for dc in (2, 3):
            use(f"D{dc}", "W", lambda it, dc=dc: (s_dl, it * DC + dc + 1))
        for tt in range(TT):
            use(f"ET{tt}", "E", lambda it, tt=tt: (s_et, (it - 1) * TT + tt + 1))
            use(f"EO{tt}", "E", lambda it, tt=tt: (s_eo, (it - 1) * TT + tt + 1))
        for tt in range(TT):
            use(f"Z{tt}", "Z", lambda it, tt=tt: (s_zc, it * TT + tt + 1))
        for dc in range(DC):
            use(f"X{dc}", "P", lambda it, dc=dc: (s_cv, ((it + 1) * DC + dc) * 3 + 3))
        use("XD", "P", lambda it: (s_stk, (it + 1) * 6 + 3))
        for dc in (0, 1):
            use(f"D{dc}", "P", lambda it, dc=dc: (s_dl, (it + 1) * DC + dc + 1))
        for n in range(13):
            use(f"C{n}", "P", lambda it, n=n: (s_cb, (it + 1) * NS + n + 1))
        place = {}
        for k, (name, family, _) in enumerate(uses):
            place[name, family] = k
        order = ["pre", FIRST, MID, LAST, "post"]

        def bank(name, family):
            return psP[place[name, family] % 2]

        def claim(pe, name, family, it, kind):
            k = place[name, family]
            back = list(range(k - 2, -1, -2))
            same = [j for j in range(k) if j % 2 == k % 2 and present(uses[j][1], kind)]
            if same:
                s, v = uses[same[-1]][2](it)
            else:
                if kind == "pre":
                    return bank(name, family)
                prev = order[order.index(kind) - 1]
                js = [j for j in range(len(uses)) if j % 2 == k % 2 and present(uses[j][1], prev)]
                s, v = uses[js[-1]][2](it - 1)
            wait(pe, s, v)
            return bank(name, family)

        def bcast(pe, dst, st_, r):
            return pe.matmul(dst, sel[:, r:r + 1].to_broadcast([P, P]), st_[:, :], start=True, stop=True)

        def pe_unit(pe, it, s):
            if s == 0:
                wait(pe, s_stack, it + 1)
            wait(pe, s_scan, it * UN + before3(s) + 1)
            bcast(pe, psB[ring3(s)][:, :], stack, s % NS).then_inc(s_bbc, 1)

        def pe_sum(pe, it, s):
            dc, n = divmod(s, NS)
            y = psY[dc % 2]
            if n == 0:
                wait(pe, s_Du, it * DC + dc + 1)
                wait(pe, s_gate, it * DC + dc - 1)
                for tt in range(TT):
                    pe.matmul(y[:, tt * P:(tt + 1) * P], Du[:, dc, tt * P:(tt + 1) * P], ident[:, :],
                              start=(tt == 0), stop=False, is_transpose=True, skip_group_check=True)
            wait(pe, s_g, it * UN + s + 1)
            for tt in range(TT):
                mm = pe.matmul(y[:, tt * P:(tt + 1) * P], hc[:, s % GR, tt * P:(tt + 1) * P], ident[:, :],
                               start=False, stop=(n == NS - 1), is_transpose=True, skip_group_check=True)
            mm.then_inc(s_tr, 1)

        def act_unit(act, it, s):
            dc, n = divmod(s, NS)
            if n == 0:
                wait(act, s_delta, it * 2 + dc // 2 + 1)
            wait(act, s_g, it * UN + s - HR + 1)
            act.activation(hb[:, s % HR, :], delta[:, dc, :], ACT.Exp, scale=aneg[:, dc, n:n + 1]).then_inc(s_exp, 1)

        def dve_product(dve, it, s):
            dc, n = divmod(s, NS)
            if n == 0:
                wait(dve, s_delta, it * 2 + dc // 2 + 1)
            wait(dve, s_bbc, it * UN + s + 1)
            b = psB[ring3(s)][:, :]
            dve.tensor_tensor(b, du[:, dc, :], b, ALU.mult).then_inc(s_dbu, 1)

        def dve_scan(dve, it, s):
            wait(dve, s_dbu, it * UN + s + 1)
            wait(dve, s_exp, it * UN + s + 1)
            wait(dve, s_carry, (it - 1) * UN + s + 1)
            h = hb[:, s % HR, :]
            dve.tensor_tensor_scan(h, h, psB[ring3(s)][:, :], col(carry, s), ALU.mult, ALU.add).then_inc(s_scan, 1)

        def pool_unit(pool, it, s):
            dc, n = divmod(s, NS)
            wait(pool, s_scan, it * UN + s + 1)
            if dc == 0:
                wait(pool, s_cb, it * NS + n + 1)
            plain(pool)
            h = hb[:, s % HR, :]
            pool.tensor_tensor(col(carry, s), h[:, T - 1:T], keep[:, bass.ds(it + 1, 1)], ALU.mult).then_inc(s_carry, 1)
            wait(pool, s_tr, it * UN + s - GR + 1)
            pool.tensor_tensor(hc[:, s % GR, :], h, Cb[:, n, :], ALU.mult).then_inc(s_g, 1)

        def X0(dc):
            return 26 + 4 * dc

        @job("sp", 23, "P")
        def _(sp, it, kind):
            wait(sp, s_zm, (it + 1) * TT)
            sp.dma_start(xnT[:, :, :], xnT_d[bass.ds(it + 1, 1), :, :, :].rearrange("a p k t -> (a p) k t")
                         if not isinstance(it, int) else xnT_d[it + 1]).then_inc(s_xT, 16)

        for dc in range(DC):
            for kc in range(KC):
                @job("pe", X0(dc) + kc, "P")
                def _(pe, it, kind, dc=dc, kc=kc):
                    if kc == 0:
                        if dc == 0:
                            wait(pe, s_xT, 16 * (it + 2))
                        claim(pe, f"X{dc}", "P", it, kind)
                    mm = pe.matmul(bank(f"X{dc}", "P")[:, :], win[:, kc, dc * P:(dc + 1) * P], xnT[:, kc, :],
                                   start=(kc == 0), stop=(kc == KC - 1))
                    if kc == KC - 1:
                        mm.then_inc(s_xp, 1)

            @job("act", X0(dc) + 1, "P")
            def _(act, it, kind, dc=dc):
                j = (it + 1) * DC + dc
                ps, xi = bank(f"X{dc}", "P")[:, :], xin[:, dc % 2, :]
                wait(act, s_halo, j - 1)
                wait(act, s_halo, j - DC + 1)
                act.activation(xi[:, 0:KW - 1], halo[:, dc, :], ACT.Copy).then_inc(s_xe, 1)
                wait(act, s_xp, j + 1)
                act.activation(xi[:, KW - 1:], ps, ACT.Copy).then_inc(s_xe, 1)
                act.activation(ps, ps, ACT.Identity, bias=col(cb, dc), scale=cw[:, dc, KW - 1:KW]).then_inc(s_xe, 1)

            for k in range(KW - 1):
                @job("dve", X0(dc) + 3 + k, "P")
                def _(dve, it, kind, dc=dc, k=k):
                    j = (it + 1) * DC + dc
                    ps, xi = bank(f"X{dc}", "P")[:, :], xin[:, dc % 2, :]
                    if k == 0:
                        wait(dve, s_xe, j * 3 + 3)
                    if k == KW - 2 and dc == 0:
                        wait(dve, s_delta, 2 * (it + 1))
                    wait(dve, s_cv, j * 3 + k)
                    dve.scalar_tensor_tensor(out=u[:, dc, :] if k == KW - 2 else ps, in0=xi[:, k:k + T],
                                             scalar=cw[:, dc, k:k + 1], in1=ps, op0=ALU.mult,
                                             op1=ALU.add).then_inc(s_cv, 1)
                    if k == KW - 2:
                        dve.tensor_tensor(halo[:, dc, :], xi[:, T:T + KW - 1],
                                          keep[:, bass.ds(it + 2, 1)].to_broadcast([P, KW - 1]),
                                          ALU.mult).then_inc(s_halo, 1)

        @job("act", 44, "P")
        def _(act, it, kind):
            wait(act, s_cv, (it + 2) * DC * 3)
            act.activation(u[:, :, :], u[:, :, :], ACT.Silu).then_inc(s_u, 1)

        for dc in range(DC):
            @job("pe", 45 + dc, "P")
            def _(pe, it, kind, dc=dc):
                if dc == 0:
                    claim(pe, "XD", "P", it, kind)
                    wait(pe, s_u, it + 2)
                mm = pe.matmul(bank("XD", "P")[:, :], wxd[:, dc, :], u[:, dc, :], start=(dc == 0), stop=(dc == DC - 1))
                if dc == DC - 1:
                    mm.then_inc(s_xd, 1)

        @job("dve", 49, "P")
        def _(dve, it, kind):
            p, ps = it + 1, bank("XD", "P")
            wait(dve, s_xd, p + 1)
            wait(dve, s_cb, p * NS)
            wait(dve, s_stack, p)
            wait(dve, s_dm, p * DC)
            dve.tensor_copy(xr[32:48, :], ps[32:48, :]).then_inc(s_stk, 1)
            dve.tensor_copy(stackN[:, :], ps[:, :]).then_inc(s_stk, 1)
            wait(dve, s_stk, p * 6 + 2)
            dve.tensor_tensor(xr[64:128, :], ps[64:128, :], stackN[64:128, :], ALU.subtract).then_inc(s_stk, 1)

        @job("dve", 50, "P")
        def _(dve, it, kind):
            p = it + 1
            wait(dve, s_stk, p * 6 + 3)
            dve.tensor_copy(stackN[64:128, :], xr[64:128, :]).then_inc(s_stk, 1)
            wait(dve, s_stk, p * 6 + 4)
            dve.tensor_tensor(xr[96:128, :], xr[96:128, :], stackN[96:128, :], ALU.subtract).then_inc(s_stk, 1)
            wait(dve, s_stk, p * 6 + 5)
            dve.tensor_copy(stackN[96:128, :], xr[96:128, :]).then_inc(s_stk, 1)

        def delta_jobs(family, pair, slot, chunk):
            for dc in (2 * pair, 2 * pair + 1):
                @job("pe", slot + dc % 2, family)
                def _(pe, it, kind, dc=dc):
                    p = chunk(it)
                    ps = claim(pe, f"D{dc}", family, it, kind)
                    wait(pe, s_stk, p * 6 + 1)
                    pe.matmul(ps[:, :], wdt[32:48, dc * P:(dc + 1) * P], xr[32:48, :],
                              start=True, stop=True).then_inc(s_dm, 1)

                @job("act", slot + dc % 2 + 1, family)
                def _(act, it, kind, dc=dc):
                    p = chunk(it)
                    ps = bank(f"D{dc}", family)
                    wait(act, s_dm, p * DC + dc + 1)
                    wait(act, s_delta, p * 2 + pair)
                    act.activation(tmpA[:, dc % 2, :], ps[:, :], ACT.Abs, bias=col(bdt, dc)).then_inc(s_ab, 1)
                    act.activation(delta[:, dc, :], ps[:, :], ACT.Relu, bias=col(bdt, dc)).then_inc(s_dl, 1)

            @job("act", slot + 2, family)
            def _(act, it, kind):
                q = chunk(it) * 2 + pair
                wait(act, s_ab, 2 * q + 2)
                act.activation(tmpA[:, :, :], tmpA[:, :, :], ACT.Exp, scale=-1.0).then_inc(s_ln, 1)
                wait(act, s_ln, 2 * q + 1)
                act.activation(tmpA[:, :, :], tmpA[:, :, :], ACT.Ln, bias=1.0).then_inc(s_ln, 1)

            @job("pool", slot + 3, family)
            def _(pool, it, kind):
                q = chunk(it) * 2 + pair
                d, uu = delta[:, 2 * pair:2 * pair + 2, :], u[:, 2 * pair:2 * pair + 2, :]
                wait(pool, s_ln, 2 * q + 2)
                pool.tensor_tensor(d, d, tmpA[:, :, :], ALU.add).then_inc(s_dadd, 1)
                wait(pool, s_dadd, q + 1)
                pool.tensor_tensor(du[:, 2 * pair:2 * pair + 2, :], d, uu, ALU.mult).then_inc(s_delta, 1)

        delta_jobs("P", 0, 50, lambda it: it + 1)
        delta_jobs("W", 1, 3, lambda it: it)

        @job("act", 55, "P")
        def _(act, it, kind):
            p = it + 1
            wait(act, s_tr, p * UN - NS + 1)
            for dc in range(DC):
                act.activation(Du[:, dc, :], u[:, dc, :], ACT.Copy, scale=col(dsk, dc)).then_inc(s_Du, 1)

        def c_jobs(n, slot, family, chunk):
            @job("pe", slot, family)
            def _(pe, it, kind):
                ps = claim(pe, f"C{n}", family, it, kind)
                wait(pe, s_stk, chunk(it) * 6 + 6)
                bcast(pe, ps[:, :], stackN, NS + n).then_inc(s_cm, 1)

            @job("act", slot, family)
            def _(act, it, kind):
                p = chunk(it)
                wait(act, s_cm, p * NS + n + 1)
                wait(act, s_g, p * UN - NS + n + 1)
                act.activation(Cb[:, n, :], bank(f"C{n}", family)[:, :], ACT.Copy).then_inc(s_cb, 1)

        for n in range(13):
            c_jobs(n, 51 + n, "P", lambda it: it + 1)
        for n in range(13, NS):
            c_jobs(n, n - 13, "W", lambda it: it)

        for tt in range(TT):
            for kc in range(KC):
                @job("pe", 15 + 2 * tt + kc, "Z")
                def _(pe, it, kind, tt=tt, kc=kc):
                    if kc == 0:
                        claim(pe, f"Z{tt}", "Z", it, kind)
                    mm = pe.matmul(bank(f"Z{tt}", "Z")[:, :], xnT[:, kc, tt * P:(tt + 1) * P], win[:, kc, DI:],
                                   start=(kc == 0), stop=(kc == KC - 1))
                    if kc == KC - 1:
                        mm.then_inc(s_zm, 1)

            @job("act", 16 + 2 * tt, "Z")
            def _(act, it, kind, tt=tt):
                wait(act, s_zm, it * TT + tt + 1)
                act.activation(zs[:, tt, :], bank(f"Z{tt}", "Z")[:, :], ACT.Copy).then_inc(s_zc, 1)

        @job("act", 23, "Z")
        def _(act, it, kind):
            wait(act, s_zc, (it + 1) * TT)
            act.activation(zs[:, :, :], zs[:, :, :], ACT.Silu).then_inc(s_z, 1)

        def gate(dve, it, dc):
            wait(dve, s_z, it + 1)
            wait(dve, s_tr, it * UN + (dc + 1) * NS)
            z = zs[:, :, dc * P:(dc + 1) * P]
            dve.tensor_tensor(z, z, psY[dc % 2][:, :].rearrange("p (a b) -> p a b", a=TT), ALU.mult).then_inc(s_gate, 1)

        for dc, slot in ((0, 25), (1, 37), (2, 53)):
            job("dve", slot, "Z")(lambda dve, it, kind, dc=dc: gate(dve, it, dc))
        job("dve", 5, "E")(lambda dve, it, kind: gate(dve, it - 1, DC - 1))

        for tt in range(TT):
            @job("pe", 6 + 2 * tt, "E")
            def _(pe, it, kind, tt=tt):
                ps = claim(pe, f"ET{tt}", "E", it, kind)
                wait(pe, s_gate, it * DC)
                for dc in range(DC):
                    mm = pe.matmul(ps[:, dc * P:(dc + 1) * P], zs[:, tt, dc * P:(dc + 1) * P], ident[:, :],
                                   start=True, stop=True, is_transpose=True)
                mm.then_inc(s_etm, 1)

            @job("act", 6 + 2 * tt, "E")
            def _(act, it, kind, tt=tt):
                j = (it - 1) * TT + tt
                wait(act, s_etm, j + 1)
                wait(act, s_eom, (it - 1) * TT + max(tt - 1, 0))
                act.activation(ygT[:, tt % 2, :, :], bank(f"ET{tt}", "E")[:, :].rearrange("p (a b) -> p a b", a=DC),
                               ACT.Copy).then_inc(s_et, 1)

            @job("pe", 7 + 2 * tt, "E")
            def _(pe, it, kind, tt=tt):
                ps = claim(pe, f"EO{tt}", "E", it, kind)
                wait(pe, s_et, (it - 1) * TT + tt + 1)
                for dc in range(DC):
                    mm = pe.matmul(ps[:, 0:D], ygT[:, tt % 2, dc, :], wout[:, dc, :], start=(dc == 0), stop=(dc == DC - 1))
                mm.then_inc(s_eom, 1)

            @job("act", 8 + 2 * tt, "E")
            def _(act, it, kind, tt=tt):
                wait(act, s_eom, (it - 1) * TT + tt + 1)
                if tt == 0:
                    wait(act, s_om, 16 * (it - 1))
                act.activation(om[:, tt, :], bank(f"EO{tt}", "E")[:, 0:D], ACT.Copy).then_inc(s_eo, 1)

        @job("sp", 15, "E")
        def _(sp, it, kind):
            wait(sp, s_eo, it * TT)
            sp.dma_start(om_d[bass.ds((it - 1) * T, T), :].rearrange("(a p) d -> p a d", p=P), om[:, :, :]).then_inc(s_om, 16)

        for i in range(TILES):
            @job("sp", min(2 * i, 22) if i < 12 else 2 * i - 2, "S")
            def _(sp, it, kind, i=i):
                r = i % 4
                wait(sp, s_sc[r], 32 * (i // 4))
                sp.dma_start(xsrc[:, r, :], xn_d[i * P:(i + 1) * P, :]).then_inc(s_scl[r], 16)
            for k in range(2):
                @job("pool", 2 * i + k, "S")
                def _(pool, it, kind, i=i, k=k):
                    r = i % 4
                    wait(pool, s_scl[r], 16 * (i // 4 + 1))
                    if i == 0 and k == 0:
                        wait(pool, s_zero, 16)
                    pool.indirect_dma_start(
                        out=xs_d[:, :], out_offset=bass.IndirectOffsetOnAxis(ap=slots[:, k, i:i + 1], axis=0),
                        in_=xsrc[:, r, :], in_offset=None).then_inc(s_sc[r], 16)

        def in_kind(q, kind):
            return kind == MID or q * GT < MT - (NC - 2) * NG * GT

        for q in range(NG):
            b0 = 21 * q

            def group(it, q=q):
                return (it - 1) * NG + q

            def tile0(it, q=q):
                return (it - 1) * (NG * GT) + q * GT

            def mjob(engine, slot, q=q):
                def add(fn):
                    def run(eng, it, kind):
                        if in_kind(q, kind):
                            fn(eng, it)
                    job(engine, slot, "M")(run)
                return add

            def pair0(it, q=q):
                return (it - 1) * (NG * GT // 2) + q * (GT // 2)

            @mjob("sp", b0)
            def _(sp, it, group=group, tile0=tile0, pair0=pair0, q=q):
                if q == 0:
                    for r in range(4):
                        wait(sp, s_sc[r], 32 * (TILES // 4))
                wait(sp, s_t1, pair0(it))
                sp.dma_start(xg[:, :, :], xs_d[bass.ds(tile0(it) * P, GT * P), :].rearrange("(a p) d -> p a d", p=P)).then_inc(s_xg, 16)
                for j in range(GT):
                    e = sp.value_load(etab[0:1, bass.ds(tile0(it) + j, 1)], min_val=0, max_val=E - 1)
                    if j == 0:
                        wait(sp, s_m2, pair0(it))
                    sp.dma_start(w2r[:, j, :, :], W2[bass.ds(e, 1), :, :].rearrange("a (k p) o -> p (a k) o", p=P)).then_inc(s_w2, 16)

            for h in range(GT // 2):
                c0 = b0 + 1 + 6 * h

                @mjob("pe", c0)
                def _(pe, it, h=h, group=group, pair0=pair0):
                    pr = pair0(it) + h
                    if h == 0:
                        wait(pe, s_xg, 16 * (group(it) + 1))
                        wait(pe, s_my, pr)
                    else:
                        wait(pe, s_mn, pr)
                    for a in range(2):
                        for kc in range(KC):
                            mm = pe.matmul(psE[:, (a * KC + kc) * P:(a * KC + kc + 1) * P],
                                           xg[:, 2 * h + a, kc * P:(kc + 1) * P], ident[:, :],
                                           start=True, stop=True, is_transpose=True)
                    mm.then_inc(s_t1, 1)

                @mjob("act", c0)
                def _(act, it, h=h, pair0=pair0):
                    wait(act, s_t1, pair0(it) + h + 1)
                    act.activation(xgT[:, :, :, :], psE[:, :].rearrange("p (a k t) -> p a k t", a=2, k=KC), ACT.Copy).then_inc(s_mx, 1)

                for a in range(2):
                    @mjob("pe", c0 + 1 + a)
                    def _(pe, it, h=h, a=a, pair0=pair0, tile0=tile0):
                        if a == 0:
                            wait(pe, s_mx, pair0(it) + h + 1)
                            plain(pe)
                        e = pe.value_load(etab[0:1, bass.ds(tile0(it) + 2 * h + a, 1)], min_val=0, max_val=E - 1)
                        dst = psE[:, a * D:(a + 1) * D]
                        for kc in range(KC):
                            pe.matmul(dst, xgT[:, a, kc, :], w1[:, bass.ds(e, 1), kc, :].rearrange("p a d -> p (a d)"),
                                      start=(kc == 0), stop=False)
                        mm = pe.matmul(dst, pick6[:, 0, :], bias6[:, bass.ds(e * D, D)], start=False, stop=True)
                        if a == 1:
                            mm.then_inc(s_m1, 1)

                @mjob("dve", c0 + 3)
                def _(dve, it, h=h, pair0=pair0):
                    pr = pair0(it) + h
                    wait(dve, s_m1, pr + 1)
                    for a in range(2):
                        dve.bn_stats(st[:, 0, a, :], psE[:, a * D:(a + 1) * D]).then_inc(s_mbn, 1)
                    wait(dve, s_mbn, 2 * pr + 2)
                    plain(dve)
                    for a in range(2):
                        dve.bn_aggr(mv[:, 0, a, :], st[:, 0, a, :]).then_inc(s_mag, 1)

                @mjob("pool", c0 + 2)
                def _(pool, it, h=h, pair0=pair0):
                    pr = pair0(it) + h
                    wait(pool, s_mag, 2 * pr + 2)
                    plain(pool)
                    pool.tensor_scalar(ve[:, 0, 0:2], mv[:, 0, 0:2, 1], EPS, None, ALU.add).then_inc(s_mve, 1)
                    wait(pool, s_mve, pr + 1)
                    pool.tensor_tensor(rstd[:, 0, 0:2], ve[:, 0, 0:2], mhalf[:, 0:2], ALU.pow).then_inc(s_mrs, 1)

                @mjob("dve", c0 + 4)
                def _(dve, it, h=h, pair0=pair0):
                    wait(dve, s_mrs, pair0(it) + h + 1)
                    for a in range(2):
                        dve.tensor_scalar(hn[:, a, :], psE[:, a * D:(a + 1) * D], mv[:, 0, a, 0:1], rstd[:, 0, a:a + 1],
                                          ALU.subtract, ALU.mult).then_inc(s_mh, 1)

                @mjob("pe", c0 + 5)
                def _(pe, it, h=h, pair0=pair0):
                    wait(pe, s_mh, 2 * (pair0(it) + h) + 2)
                    for a in range(2):
                        for kc in range(KC):
                            mm = pe.matmul(psE[:, (a * KC + kc) * P:(a * KC + kc + 1) * P],
                                           hn[:, a, kc * P:(kc + 1) * P], ident[:, :],
                                           start=True, stop=True, is_transpose=True)
                    mm.then_inc(s_t2, 1)

                @mjob("act", c0 + 5)
                def _(act, it, h=h, pair0=pair0):
                    pr = pair0(it) + h
                    wait(act, s_t2, pr + 1)
                    if h == 0:
                        wait(act, s_m2, pr)
                    act.activation(hnT[:, 2 * h:2 * h + 2, :, :], psE[:, :].rearrange("p (a k t) -> p a k t", a=2, k=KC),
                                   ACT.Copy).then_inc(s_mn, 1)

            @mjob("act", b0 + 14)
            def _(act, it, tile0=tile0, pair0=pair0):
                t = tile0(it)
                wait(act, s_mn, pair0(it) + 2)
                for j in range(GT):
                    e = act.value_load(etab[0:1, bass.ds(t + j, 1)], min_val=0, max_val=E - 1)
                    for kc in range(KC):
                        ins = act.activation(hnT[:, j, kc, :], hnT[:, j, kc, :], ACT.Gelu,
                                             scale=g1t[:, bass.ds(e, 1), kc], bias=be1t[:, bass.ds(e, 1), kc])
                    ins.then_inc(s_mg, 1)

            for j in range(GT):
                @mjob("pe", b0 + 15 + j)
                def _(pe, it, j=j, tile0=tile0, group=group, pair0=pair0):
                    t, h, a = tile0(it), j // 2, j % 2
                    wait(pe, s_mg, t + j + 1)
                    if j == 0:
                        wait(pe, s_w2, 16 * GT * (group(it) + 1))
                    elif j == 2:
                        wait(pe, s_my, pair0(it) + 1)
                    plain(pe)
                    e = pe.value_load(etab[0:1, bass.ds(t + j, 1)], min_val=0, max_val=E - 1)
                    dst = psE[:, a * D:(a + 1) * D]
                    for kc in range(KC):
                        pe.matmul(dst, hnT[:, j, kc, :], w2r[:, j, kc, :], start=(kc == 0), stop=False)
                    mm = pe.matmul(dst, pick6[:, 1, :], bias6[:, bass.ds(e * D, D)], start=False, stop=True)
                    if a == 1:
                        mm.then_inc(s_m2, 1)

            for h in range(GT // 2):
                @mjob("act", b0 + 16 + 2 * h)
                def _(act, it, h=h, pair0=pair0, group=group):
                    wait(act, s_m2, pair0(it) + h + 1)
                    if h == 0:
                        wait(act, s_ys, 16 * group(it))
                    act.activation(yo[:, 2 * h:2 * h + 2, :], psE[:, :].rearrange("p (a d) -> p a d", a=2), ACT.Copy).then_inc(s_my, 1)

            @mjob("sp", b0 + 20)
            def _(sp, it, tile0=tile0, pair0=pair0):
                wait(sp, s_my, pair0(it) + 2)
                sp.dma_start(ys_d[bass.ds(tile0(it) * P, GT * P), :].rearrange("(a p) d -> p a d", p=P), yo[:, :, :]).then_inc(s_ys, 16)

        units = {
            "pe": [(pe_unit, LEAD_B), (pe_sum, -LAG)],
            "act": [(act_unit, LEAD_A)],
            "dve": [(dve_product, 0), (dve_scan, -1)],
            "pool": [(pool_unit, 0)],
            "sp": [],
        }

        def unit_steps(name, eng, it, kind, slot):
            for fn, off in units[name]:
                s = slot + off
                if 0 <= s < UN:
                    fn(eng, it, s)
                elif s >= UN and kind != LAST:
                    fn(eng, it + 1, s - UN)
                elif s < 0 and kind != FIRST:
                    fn(eng, it - 1, s + UN)

        def side(name, eng, it, kind, slot):
            for family, fn in jobs[name][slot]:
                if present(family, kind):
                    fn(eng, it, kind)

        def body(name, eng, it, kind):
            if name == "dve":
                wait(eng, s_stk, it * 6 + 6)
                wait(eng, s_bbc, it * UN)
                eng.tensor_copy(stack[:, :], stackN[:, :]).then_inc(s_stack, 1)
            for s in range(UN):
                unit_steps(name, eng, it, kind, s)
                side(name, eng, it, kind, s)

        def chunks(name, eng):
            for s in range(UN):
                side(name, eng, -1, "pre", s)
            for s in range(-LEAD_A, 0):
                for fn, off in units[name]:
                    if s + off >= 0:
                        fn(eng, 0, s + off)
            body(name, eng, 0, FIRST)
            with eng.Fori(1, NC - 1) as it:
                body(name, eng, it, MID)
            body(name, eng, NC - 1, LAST)
            for s in range(UN, UN + LAG):
                for fn, off in units[name]:
                    if off < 0 and s + off < UN:
                        fn(eng, NC - 1, s + off)
            for s in range(UN):
                side(name, eng, NC, "post", s)

        NBIG = 2 + 3 + 2 * KC + 4 + 2
        NCONST = 8

        block = ctx.enter_context(nc.Block())

        @block.sync
        def _(sp):
            for s in ahead:
                sp.sem_inc(s, 1)
            xt = x.rearrange("(g a p) d -> g p a d", p=P, a=TT)

            def load_x(g, k):
                sp.dma_start(xraw[k], xt[bass.ds(g, 1)].rearrange("g p a d -> (g p) a d")).then_inc(s_xl[k], 16)

            load_x(0, 0)
            load_x(1, 1)
            sp.dma_start(wr[:, :, :], Wr.rearrange("(k p) e -> p k e", p=P)).then_inc(s_w["early"], 16)
            sp.dma_start(brr[:, :], br.rearrange("(a e) -> a e", a=1)).then_inc(s_w["early"], 16)
            sp.wait_ge(s_rt, 5)
            for b in range(2):
                for k in range(3):
                    sp.dma_start(b_d[3 * b + k, :].rearrange("(p d) -> p d", d=64), bparts[k][64 * b:64 * b + 64, :]).then_inc(s_w["bst"], 16)

            def norm_stores(i, more):
                for k in range(2):
                    wait(sp, s_xn, i * (2 * TT) + (k + 1) * TT)
                    sp.dma_start(xn_d[bass.ds((2 * i + k) * T, T), :].rearrange("(a p) d -> p a d", p=P), xnb[k]).then_inc(s_xst[k], 16)
                    if more:
                        load_x(2 * i + k + 2, k)
                    wait(sp, s_te, i * 4 + 2 * k + 2)
                    sp.dma_start(xnT_d[bass.ds(2 * i + k, 1)].rearrange("g p k t -> (g p) k t"), xnTg[k]).then_inc(s_tst[k], 16)

            with sp.Fori(0, NC // 2 - 1) as i:
                norm_stores(i, True)
            norm_stores(NC // 2 - 1, False)
            wait(sp, s_route, 1)
            for k in range(2):
                wait(sp, s_xst[k], 16 * (NC // 2))
                wait(sp, s_tst[k], 16 * (NC // 2))
            chunks("sp", sp)

            wait(sp, s_om, 16 * NC)
            with sp.Fori(0, NC // 2) as i:
                for k in range(2):
                    g = 2 * i + k
                    wait(sp, s_fo[k], 16 * i)
                    sp.dma_start(half(u, k), xt[bass.ds(g, 1)].rearrange("g p a d -> (g p) a d")).then_inc(s_fx[k], 16)
                    sp.dma_start(half(Du, k), om_d[bass.ds(g * T, T), :].rearrange("(a p) d -> p a d", p=P)).then_inc(s_fx[k], 16)
                for k in range(2):
                    g = 2 * i + k
                    wait(sp, s_fa, (g + 1) * (3 * TT))
                    sp.dma_start(out[bass.ds(g * T, T), :].rearrange("(a p) d -> p a d", p=P), half(u, k)).then_inc(s_fo[k], 16)
            for k in range(2):
                wait(sp, s_fo[k], 16 * (NC // 2))
            wait(sp, s_om, 16 * NC)
            wait(sp, s_ys, 16 * (MT // GT))

        @block.gpsimd
        def _(pool):
            pool.memset(ident[:, :], 0.0).then_inc(s_const, 1)
            pool.memset(upper[:, :], 0.0).then_inc(s_const, 1)
            pool.memset(sel[:, :], 0.0).then_inc(s_const, 1)
            pool.memset(pick6[:, :, :], 1.0).then_inc(s_const, 1)
            pool.memset(reset, 1.0).then_inc(s_const, 1)
            pool.wait_ge(s_const, 5)
            ev = reset.rearrange("p (e i) -> p e i", i=TILES)
            pool.affine_select(out=ident[:, :], in_=ident[:, :], compare_op=ALU.not_equal, fill=1.0,
                               base=0, pattern=[[-1, P]], channel_multiplier=1).then_inc(s_const, 1)
            pool.affine_select(out=upper[:, :], in_=upper[:, :], compare_op=ALU.is_ge, fill=1.0,
                               base=0, pattern=[[-1, P]], channel_multiplier=1).then_inc(s_const, 1)
            pool.affine_select(out=ev, in_=ev, compare_op=ALU.not_equal, fill=0.0,
                               base=0, pattern=[[0, E], [1, TILES]], channel_multiplier=0).then_inc(s_const, 1)
            pool.affine_select(out=pick6[:, 0, :], in_=pick6[:, 0, :], compare_op=ALU.is_ge, fill=0.0,
                               base=2, pattern=[[0, P]], channel_multiplier=-1).then_inc(s_const, 1)
            pool.affine_select(out=pick6[:, 1, :], in_=pick6[:, 1, :], compare_op=ALU.is_ge, fill=0.0,
                               base=-3, pattern=[[0, P]], channel_multiplier=1).then_inc(s_const, 1)
            for k, q in enumerate((0, 2, 3)):
                pool.affine_select(out=sel[:, :], in_=sel[:, :], compare_op=ALU.not_equal, fill=1.0,
                                   base=-32 * q, pattern=[[-1, 2 * NS]], channel_multiplier=1).then_inc(s_const, 1)
                pool.wait_ge(s_const, 11 + k)
            kw = dict(channel_multiplier=0, allow_small_or_imprecise_dtypes=True)
            pool.iota(iotaE.rearrange("p (i e) -> p i e", e=E), pattern=[[0, TILES], [1, E]], base=-E, **kw).then_inc(s_const, 1)
            pool.iota(iotaJ.rearrange("p (e j) -> p e j", e=E), pattern=[[0, E], [P, TILES]], base=0, **kw).then_inc(s_const, 1)
            pool.iota(iotaT.rearrange("p (j e) -> p j e", e=E), pattern=[[1, MT], [0, E]], base=0, **kw).then_inc(s_const, 1)
            pool.wait_ge(s_cdve, NCONST)
            with pool.Fori(0, NC // 2) as i:
                for k in range(2):
                    wait(pool, s_mv, i * (2 * TT) + (k + 1) * TT)
                    plain(pool)
                    pool.tensor_scalar(ve[:, k, :], mv[:, k, :, 1], EPS, None, ALU.add).then_inc(s_ve, 1)
                    wait(pool, s_ve, i * 2 + k + 1)
                    pool.tensor_tensor(rstd[:, k, :], ve[:, k, :], mhalf[:, :], ALU.pow).then_inc(s_rs, 1)
            wait(pool, s_route, 1)
            chunks("pool", pool)

            wait(pool, s_ys, 16 * (MT // GT))
            with pool.Fori(0, NC // 2) as i:
                for k in range(2):
                    g = 2 * i + k
                    wait(pool, s_fa, i * (6 * TT))
                    for e in range(2):
                        pool.tensor_copy(idx[:, k, e * TT:(e + 1) * TT], slots[:, e, bass.ds(g * TT, TT)]).then_inc(s_fi, 1)
                    wait(pool, s_fi, (g + 1) * 2)
                    plain(pool)
                    for e in range(2):
                        for tt in range(TT):
                            pool.indirect_dma_start(
                                out=half((delta, du)[e], k)[:, tt, :], out_offset=None, in_=ys_d[:, :],
                                in_offset=bass.IndirectOffsetOnAxis(ap=idx[:, k, e * TT + tt:e * TT + tt + 1], axis=0),
                            ).then_inc(s_fg[k], 16)

        @block.scalar
        def _(act):
            bts = [b1.rearrange("e (a d) -> (e a) d", d=64), b2.rearrange("e (a d) -> (e a) d", d=64)]
            for b in range(2):
                act.dma_start(om[64 * b:64 * b + 64, 0, 0:64], bts[b]).then_inc(s_w["bias"], 16)
            act.dma_start(aneg[:, :, :], A_log.rearrange("(c p) n -> p c n", p=P)).then_inc(s_a, 16)
            act.dma_start(win[:, :, :], W_in.rearrange("(k p) e -> p k e", p=P)).then_inc(s_w["big"], 16)
            act.dma_start(cw[:, :, :], conv_w.rearrange("(c p) a k -> p c (a k)", p=P)).then_inc(s_w["big"], 16)
            with nc.allow_non_contiguous_dma(reason="a few hundred scalars by channel"):
                for dst, src in ((cb, conv_b), (bdt, b_dt), (dsk, D_skip)):
                    act.dma_start(dst[:, :], src.rearrange("(c p) -> p c", p=P)).then_inc(s_w["big"], 16)
                for dst, src in ((g1t, g1), (be1t, be1)):
                    for kc in range(KC):
                        act.dma_start(dst[:, :, kc], src[:, kc * P:(kc + 1) * P].rearrange("e p -> p e")).then_inc(s_w["big"], 16)
            wx = W_xproj.rearrange("(c p) m -> p c m", p=P)
            act.wait_ge(s_wz, 1)
            act.dma_start(wxd[:, :, 32:48], wx[:, :, 0:R]).then_inc(s_w["big"], 16)
            for q in (0, 2, 3):
                act.dma_start(wxd[:, :, 32 * q:32 * q + 32], wx[:, :, R:]).then_inc(s_w["big"], 16)
            act.dma_start(wdt[32:48, :], W_dt).then_inc(s_w["big"], 16)
            act.dma_start(wout[:, :, :], W_out.rearrange("(c p) o -> p c o", p=P)).then_inc(s_w["big"], 16)
            act.wait_ge(s_cdve, 1)
            act.dma_start(xs_d.rearrange("(p a b) d -> p a (b d)", p=P, a=MT * D // (HR * T)),
                          hb[:, :, :].rearrange("p (o a) b -> p o (a b)", o=1).to_broadcast([P, MT * D // (HR * T), HR * T])
                          ).then_inc(s_zero, 16)
            act.wait_ge(s_w["bst"], 16 * 6)
            act.dma_start(bias6[:, :], b_d[:, :]).then_inc(s_w["bias"], 16)
            act.dma_start(w1[:, :, :, :], W1.rearrange("e (k p) h -> p e k h", p=P)).then_inc(s_w["w1"], 16)
            with act.Fori(0, NC // 2) as i:
                for k in range(2):
                    wait(act, s_tst[k], 16 * i)
                    for kc in range(KC):
                        wait(act, s_tp, i * 4 + 2 * k + kc + 1)
                        act.activation(xnTg[k][:, kc, :], (psB + psY)[2 * k + kc][:, :], ACT.Copy).then_inc(s_te, 1)
            act.wait_ge(s_a, 16)
            act.activation(aneg[:, :, :], aneg[:, :, :], ACT.Exp).then_inc(s_a, 1)
            act.wait_ge(s_rtd, 1)
            act.activation(Cb[:, 7, :], Cb[:, 6, :], ACT.Exp).then_inc(s_rte, 1)
            act.wait_ge(s_w["big"], 16 * NBIG)
            wait(act, s_route, 1)
            act.wait_ge(s_zero, 16)
            chunks("act", act)

        @block.tensor
        def _(pe):
            pe.wait_ge(s_const, 16)
            pe.wait_ge(s_cdve, NCONST)
            pe.wait_ge(s_w["early"], 32)
            with pe.Fori(0, NC // 2) as i:
                for k in range(2):
                    wait(pe, s_xn, i * (2 * TT) + (k + 1) * TT)
                    for kc in range(KC):
                        wait(pe, s_te, i * 4)
                        for tt in range(TT):
                            mm = pe.matmul((psB + psY)[2 * k + kc][:, tt * P:(tt + 1) * P],
                                           xnb[k][:, tt, kc * P:(kc + 1) * P], ident[:, :],
                                           start=True, stop=True, is_transpose=True)
                        mm.then_inc(s_tp, 1)
                    wait(pe, s_te, i * 4 + 2 * k + 2)
                    wait(pe, s_lg, i * 2)
                    for tt in range(TT):
                        dst = psP[k][:, tt * E:(tt + 1) * E]
                        for kc in range(KC):
                            pe.matmul(dst, xnTg[k][:, kc, tt * P:(tt + 1) * P], wr[:, kc, :], start=(kc == 0), stop=False)
                        mm = pe.matmul(dst, ones1[:, :], brr[:, :], start=False, stop=True)
                    mm.then_inc(s_lm, 1)
            pe.wait_ge(s_rtd, 2)
            Mb = Cb[:, 8, 0:T // 2].bitcast(BF16)
            pe.matmul(psB[0][:, :], upper[:, :], Mb, start=True, stop=True).then_inc(s_rank, 1)
            pe.matmul(psB[1][:, :], onesb[:, :], Mb, start=True, stop=True).then_inc(s_rank, 1)
            pe.wait_ge(s_w["big"], 16 * NBIG)
            pe.wait_ge(s_w["w1"], 16)
            pe.wait_ge(s_w["bias"], 48)
            wait(pe, s_route, 1)
            chunks("pe", pe)

        @block.vector
        def _(dve):
            def const(ins):
                ins.then_inc(s_cdve, 1)

            const(dve.memset(hb[:, :, :], 0.0))
            dve.memset(wxd[:, :, :], 0.0).then_inc(s_wz, 1)
            const(dve.memset(onesb[:, :], 1.0))
            const(dve.memset(ones1[:, :], 1.0))
            const(dve.memset(mhalf[:, :], -0.5))
            const(dve.memset(carry[:, :], 0.0))
            const(dve.memset(halo[:, :, :], 0.0))
            const(dve.memset(keep[:, :], 1.0))
            dve.wait_ge(s_cdve, 7)
            const(dve.memset(keep[:, 0:NC + 1:CPB], 0.0))

            bf = om[:, 0, 0:64]
            dve.wait_ge(s_w["bias"], 32)
            chain = [0]

            def link(ins):
                chain[0] += 1
                ins.then_inc(s_rt, 1)
                dve.wait_ge(s_rt, chain[0])

            link(dve.tensor_copy(bparts[0], bf))
            link(dve.tensor_tensor(bf, bf, bparts[0], ALU.subtract))
            link(dve.tensor_copy(bparts[1], bf))
            link(dve.tensor_tensor(bf, bf, bparts[1], ALU.subtract))
            link(dve.tensor_copy(bparts[2], bf))

            with dve.Fori(0, NC // 2) as i:
                for k in range(2):
                    wait(dve, s_xl[k], 16 * (i + 1))
                    for tt in range(TT):
                        dve.bn_stats(st[:, k, tt, :], xraw[k][:, tt, :]).then_inc(s_bn, 1)
                    for tt in range(TT):
                        wait(dve, s_bn, i * (2 * TT) + k * TT + tt + 1)
                        plain(dve)
                        dve.bn_aggr(mv[:, k, tt, :], st[:, k, tt, :]).then_inc(s_mv, 1)
                    wait(dve, s_rs, i * 2 + k + 1)
                    wait(dve, s_xst[k], 16 * i)
                    wait(dve, s_tp, i * 4)
                    for tt in range(TT):
                        dve.tensor_scalar(xnb[k][:, tt, :], xraw[k][:, tt, :], mv[:, k, tt, 0:1], rstd[:, k, tt:tt + 1],
                                          ALU.subtract, ALU.mult).then_inc(s_xn, 1)
                    wait(dve, s_lm, i * 2 + k + 1)
                    dve.tensor_copy(lg[:, bass.ds((2 * i + k) * (TT * E), TT * E)], psP[k][:, 0:TT * E]).then_inc(s_lg, 1)

            dve.wait_ge(s_a, 17)
            link(dve.tensor_scalar(aneg[:, :, :], aneg[:, :, :], -1.0, None, ALU.mult))

            def row(k):
                return Cb[:, k, :]

            def ie(ap):
                return ap.rearrange("p (i e) -> p i e", e=E)

            def ei(ap):
                return ap.rearrange("p (e i) -> p e i", e=E)

            def over_e(ap):
                return ap.unsqueeze(2).to_broadcast([P, TILES, E])

            def s32(k):
                return small[:, k, :]

            def s16(k):
                return small[:, k, 0:E]

            dve.wait_ge(s_const, 16)
            wait(dve, s_lg, NC)
            logits = lg

            def onehot(src, top, first, oh, t0, t1):
                link(dve.tensor_reduce(top, ie(src), AX.X, ALU.max))
                link(dve.tensor_tensor(ie(t0), ie(src), over_e(top), ALU.is_equal))
                link(dve.tensor_tensor(t1, t0, iotaE, ALU.mult))
                link(dve.tensor_reduce(first, ie(t1), AX.X, ALU.min))
                link(dve.tensor_tensor(ie(oh), ie(iotaE), over_e(first), ALU.is_equal))

            oh1, oh2 = row(2), row(5)
            onehot(logits, s32(0), s32(1), oh1, row(0), row(1))
            dve.tensor_tensor(ie(row(6)), ie(logits), over_e(s32(0)), ALU.subtract).then_inc(s_rtd, 1)
            link(dve.tensor_scalar(row(3), oh1, -2 * BIG, BIG, ALU.mult, ALU.add))
            link(dve.tensor_tensor(row(4), logits, row(3), ALU.min))
            onehot(row(4), s32(2), s32(3), oh2, row(0), row(1))
            dve.tensor_tensor(Cb[:, 8, 0:T // 2].bitcast(BF16), oh1, oh2, ALU.add).then_inc(s_rtd, 1)
            dve.wait_ge(s_rte, 1)
            link(dve.tensor_reduce(s32(4), ie(row(7)), AX.X, ALU.add))
            link(dve.reciprocal(s32(4), s32(4)))
            for k, oh in enumerate((oh1, oh2)):
                link(dve.tensor_tensor(row(0), row(7), oh, ALU.mult))
                link(dve.tensor_reduce(s32(5 + k), ie(row(0)), AX.X, ALU.add))
                link(dve.tensor_tensor(s32(5 + k), s32(5 + k), s32(4), ALU.mult))
            link(dve.tensor_tensor(s32(7), s32(5), s32(6), ALU.add))
            link(dve.tensor_scalar(s32(7), s32(7), 1e-9, None, ALU.max))
            link(dve.reciprocal(s32(7), s32(7)))
            for k in range(2):
                link(dve.tensor_tensor(wk[:, k, :], s32(5 + k), s32(7), ALU.mult))
            dve.wait_ge(s_rank, 2)
            link(dve.tensor_copy(ei(row(9)), psB[1][:, :].rearrange("p (i e) -> p e i", e=E)))
            link(dve.tensor_tensor_scan(row(11), reset, row(9), 0.0, ALU.mult, ALU.add))
            link(dve.tensor_tensor(row(12), row(11), row(9), ALU.subtract))
            count = ei(row(11))[:, :, TILES - 1]
            link(dve.tensor_tensor(ei(row(13)), count.unsqueeze(2).to_broadcast([P, E, TILES]), ei(iotaJ), ALU.is_gt))
            link(dve.tensor_reduce(s16(8), ei(row(13)), AX.X, ALU.add))
            link(dve.memset(s16(11), 1.0))
            link(dve.tensor_tensor_scan(s16(9), s16(11), s16(8), 0.0, ALU.mult, ALU.add))
            link(dve.tensor_tensor(s16(10), s16(9), s16(8), ALU.subtract))
            link(dve.tensor_scalar(s16(10), s16(10), float(P), None, ALU.mult))
            link(dve.tensor_tensor(ei(row(14)), ei(row(12)), s16(10).unsqueeze(2).to_broadcast([P, E, TILES]), ALU.add))
            link(dve.tensor_tensor(ie(row(15)), ie(psB[0][:, :]), row(14).rearrange("p (e i) -> p i e", e=E), ALU.add))
            for k, oh in enumerate((oh1, oh2)):
                link(dve.tensor_tensor(row(0), row(15), oh, ALU.mult))
                link(dve.tensor_reduce(s32(5), ie(row(0)), AX.X, ALU.add))
                link(dve.tensor_copy(slots[:, k, :], s32(5)))
            cmp_t = Cb_flat[:, 0:MT * E].rearrange("p (j e) -> p j e", e=E)
            link(dve.tensor_tensor(cmp_t, s16(9).unsqueeze(1).to_broadcast([P, MT, E]),
                                   iotaT.rearrange("p (j e) -> p j e", e=E), ALU.is_le))
            tf = Cb_flat[:, 2048:2048 + MT]
            link(dve.tensor_reduce(tf, cmp_t, AX.X, ALU.add))
            link(dve.tensor_scalar(tf, tf, float(E - 1), None, ALU.min))
            link(dve.tensor_copy(etab[:, :], tf))
            for k in range(2):
                wait(dve, s_xst[k], 16 * (NC // 2))
                wait(dve, s_tst[k], 16 * (NC // 2))
                dve.wait_ge(s_xl[k], 16 * (NC // 2))
            dve.memset(small[:, 0, 0:1], 0.0).then_inc(s_route, 1)
            chunks("dve", dve)

            with dve.Fori(0, NC // 2) as i:
                for k in range(2):
                    g = 2 * i + k
                    wait(dve, s_fx[k], 32 * (i + 1))
                    for tt in range(TT):
                        o = half(u, k)[:, tt, :]
                        dve.tensor_tensor(o, o, half(Du, k)[:, tt, :], ALU.add).then_inc(s_fa, 1)
                    for e in range(2):
                        if e == 0:
                            wait(dve, s_fg[k], 16 * 2 * TT * (i + 1))
                        for tt in range(TT):
                            o = half(u, k)[:, tt, :]
                            wait(dve, s_fa, g * (3 * TT) + e * TT + tt + 1)
                            dve.scalar_tensor_tensor(out=o, in0=half((delta, du)[e], k)[:, tt, :],
                                                     scalar=wk[:, e, bass.ds(g * TT + tt, 1)], in1=o,
                                                     op0=ALU.mult, op1=ALU.add).then_inc(s_fa, 1)


_INS = ["L0_attn_x", "L0_attn_W_in", "L0_attn_conv_w", "L0_attn_conv_b", "L0_attn_W_xproj", "L0_attn_W_dt",
        "L0_attn_b_dt", "L0_attn_A_log", "L0_attn_D_skip", "L0_attn_W_out", "L0_ffn_Wr", "L0_ffn_br",
        "L0_ffn_W1", "L0_ffn_b1", "L0_ffn_g1", "L0_ffn_be1", "L0_ffn_W2", "L0_ffn_b2"]


def kernel(**inputs):
    import numpy as np
    import concourse.bacc as bacc
    from concourse.bass_utils import run_bass_kernel_spmd as run

    nc = bacc.Bacc("TRN2", target_bir_lowering=False, num_devices=1)
    arrays, args = {}, []
    for name in _INS:
        a = np.ascontiguousarray(inputs[name])
        if name == "L0_attn_x":
            a = a.reshape(NT, D)
        arrays[f"in_{name}"] = a
        args.append(nc.dram_tensor(f"in_{name}", a.shape, mybir.dt.from_np(a.dtype), kind="ExternalInput").ap())
    args.append(nc.dram_tensor("out", (NT, D), F32, kind="ExternalOutput").ap())
    build(nc, *args)
    r = run(nc, [arrays], core_ids=[0])
    return r.results[0]["out"].reshape(NB, L, D)
```

```python
from contextlib import ExitStack

import concourse.bass as bass
from concourse import mybir

F32, BF16, I32 = mybir.dt.float32, mybir.dt.bfloat16, mybir.dt.int32
ALU, ACT, AX = mybir.AluOpType, mybir.ActivationFunctionType, mybir.AxisListType

P = 128
NB, L, D = 2, 2048, 256
DI, NS, R = 512, 16, 16
KW = 4
E = 16
NT = NB * L
TILES = NT // P
T = 512
TT = T // P
NC = NT // T
CPB = L // T
DC = DI // P
KC = D // P
UN = DC * NS
GT = 4
NG = 3
MT = 80
EPS = 1e-5
MIX = 10
LAG = 4
LEAD_B = 2
LEAD_A = 4
HR = 8
GR = 4
NK = 4
BIG = 1e38

HC_DVE = {
    "first": list(range(1, UN, 2)),
    "last": list(range(50, UN)),
}

AT = {
    "g_get": [50, 50, 50, 51, 51, 52, 52, 53, 53, 53, 54, 54, 55, 55, 56, 56, 57, 57, 57, 58, 58, 59, 59, 60, 60,
              60, 61, 61, 62, 62, 63, 63],
    "x_load": [23],
    "x_mm": [27, 27, 27, 30, 33, 35, 39, 40],
    "x_copy": [26, 37, 37, 40],
    "x_tap": [29, 32, 32, 36, 36, 37, 40, 40, 42, 42, 43, 43],
    "x_silu": [44],
    "xd_mm": [45, 45, 46, 48],
    "stack": [49, 49],
    "d_mm": [49, 50, 2, 4],
    "d_abs": [52, 52, 4, 4],
    "d_ln": [52, 10],
    "d_sum": [53, 12],
    "du_skip": [45, 47, 50, 55],
    "c_mm": [50, 51, 52, 52, 52, 55, 59, 59, 60, 61, 61, 61, 62, 0, 0, 3],
    "c_copy": [52, 52, 52, 52, 55, 57, 58, 58, 60, 60, 61, 61, 62, 0, 0, 3],
    "z_mm": [14, 14, 14, 14, 18, 21, 22, 24],
    "z_copy": [17, 18, 20, 24],
    "z_silu": [25],
    "gate": [32, 36, 57, 5],
    "e_tr": [6, 6, 8, 11],
    "e_trc": [4, 4, 7, 12],
    "e_mm": [7, 11, 12, 13],
    "e_copy": [7, 10, 13, 13],
    "e_store": [37],
    "s_load": [0, 2, 4, 6, 8, 10, 12, 14, 16, 18, 20, 22, 22, 24, 26, 28, 30, 32, 34, 36, 38, 40, 42, 44, 46, 48,
               50, 52, 54, 56, 58, 60],
    "s_put": [0, 1, 2, 3, 4, 5, 6, 7, 8, 9, 10, 11, 12, 13, 14, 15, 16, 17, 18, 19, 20, 21, 22, 23, 24, 25, 26,
              27, 28, 29, 30, 31, 32, 33, 34, 35, 36, 37, 38, 39, 40, 41, 42, 43, 44, 45, 46, 47, 48, 49, 50, 51,
              52, 53, 54, 55, 56, 57, 58, 59, 60, 61, 62, 63],
    "m_load": [4, 21, 42],
    "m_t1": [2, 8, 19, 30, 43, 48],
    "m_t1c": [2, 6, 21, 28, 43, 51],
    "m_w1": [3, 3, 8, 9, 24, 26, 31, 31, 44, 44, 50, 50],
    "m_bn": [4, 10, 26, 33, 45, 53],
    "m_rstd": [2, 8, 25, 32, 44, 52],
    "m_hn": [6, 13, 28, 35, 47, 54],
    "m_t2": [7, 12, 29, 35, 47, 53],
    "m_t2c": [6, 15, 26, 37, 49, 55],
    "m_gelu": [15, 38, 56],
    "m_w2": [15, 15, 17, 17, 38, 40, 42, 42, 56, 56, 58, 59],
    "m_yo": [15, 18, 39, 42, 56, 59],
    "m_store": [23, 52, 52],
}
assert UN % 3 == 1
assert MT >= 2 * NT // P + E - 1 and MT % GT == 0


def build(nc, x, W_in, conv_w, conv_b, W_xproj, W_dt, b_dt, A_log, D_skip, W_out,
          Wr, br, W1, b1, g1, be1, W2, b2, out):
    ctx = ExitStack()
    with ctx:
        def sb(name, shape, dt=F32):
            return ctx.enter_context(nc.sbuf_tensor(name, shape, dt))

        def psum(name):
            return ctx.enter_context(nc.psum_tensor(name, [P, 512], F32))

        def sem(name):
            return ctx.enter_context(nc.semaphore(name))

        def dram(name, shape, dt=F32):
            return nc.dram_tensor(name, shape, dt, kind="Internal").ap()

        xn_d = dram("xn_d", (NT, D))
        xnT_d = dram("xnT_d", (NC, P, KC, T))
        xs_d = dram("xs_d", (MT * P, D))
        ys_d = dram("ys_d", (MT * P, D))
        om_d = dram("om_d", (NT, D))
        b_d = dram("b_d", (6, E * D), BF16)

        w1 = sb("w1", [P, E, KC, D])
        w2r = sb("w2r", [P, GT, KC, D])
        win = sb("win", [P, KC, 2 * DI])
        wout = sb("wout", [P, DC, D])
        wxd = sb("wxd", [P, DC, P])
        wdt = sb("wdt", [P, DI])
        wr = sb("wr", [P, KC, E])
        brr = sb("brr", [1, E])
        cw = sb("cw", [P, DC, KW])
        cb = sb("cb", [P, DC])
        bdt = sb("bdt", [P, DC])
        dsk = sb("dsk", [P, DC])
        aneg = sb("aneg", [P, DC, NS])
        g1t = sb("g1t", [P, E, KC])
        be1t = sb("be1t", [P, E, KC])
        bias6 = sb("bias6", [6, E * D], BF16)
        ident = sb("ident", [P, P])
        upper = sb("upper", [P, P], BF16)
        onesb = sb("onesb", [P, P], BF16)
        ones1 = sb("ones1", [1, P])
        pick6 = sb("pick6", [6, 2, P], BF16)
        sel = sb("sel", [P, 2 * NS], BF16)
        keep = sb("keep", [P, NC + 1])
        mhalf = sb("mhalf", [P, TT])
        xnT = sb("xnT", [P, KC, T])
        xin = sb("xin", [P, 2, T + KW - 1])
        halo = sb("halo", [P, DC, KW - 1])
        u = sb("u", [P, DC, T])
        Du = sb("Du", [P, DC, T])
        delta = sb("delta", [P, DC, T])
        du = sb("du", [P, DC, T])
        tmpA = sb("tmpA", [P, 2, T])
        xr = sb("xr", [P, T])
        stackN = sb("stackN", [P, T], BF16)
        stack = sb("stack", [P, T], BF16)
        Cb = sb("Cb", [P, NS, T])
        hb = sb("hb", [P, HR, T])
        hc = sb("hc", [P, GR, T])
        carry = sb("carry", [P, UN])
        zs = sb("zs", [P, TT, DI])
        ygT = sb("ygT", [P, 2, DC, P])
        om = sb("om", [P, TT, D])
        xg = sb("xg", [P, GT, D])
        xgT = sb("xgT", [P, 2, KC, P])
        hn = sb("hn", [P, 2, D])
        hnT = sb("hnT", [P, GT, KC, P])
        yo = sb("yo", [P, GT, D])
        st = sb("st", [P, 2, TT, 6])
        mv = sb("mv", [P, 2, TT, 2])
        ve = sb("ve", [P, 2, TT])
        rstd = sb("rstd", [P, 2, TT])
        slots = sb("slots", [P, 2, TILES], I32)
        wk = sb("wk", [P, 2, TILES])
        etab = sb("etab", [P, MT], I32)
        small = sb("small", [P, 12, TILES])

        def group_of(t, k):
            return t[:, 2 * k:2 * k + 2, :].rearrange("p a (b d) -> p (a b) d", d=D)

        xraw = [group_of(Cb, k) for k in range(NK)]
        xnTg = [Cb[:, 2 * (NK + k):2 * (NK + k) + 2, :] for k in range(NK)]
        xnb = [group_of(hb, k) for k in range(NK)]
        lg = zs[:, 3, :]
        iotaE, reset, iotaJ = zs[:, 0, :], zs[:, 1, :], zs[:, 2, :]
        iotaT = w2r[:, :, :, :].rearrange("p a b c -> p (a b c)")[:, 0:MT * E]
        w1_flat = w1[:, :, :, :].rearrange("p a b c -> p (a b c)")
        scratch = w1_flat.rearrange("p (a b) -> p a b", b=T)
        bparts = [om[:, 1, 32 * k:32 * k + 32].bitcast(BF16) for k in range(3)]
        xsrc = xg
        zero = ygT[:, :, :, :].rearrange("p a b c -> p (a b c)")

        w2r_flat = w2r[:, :, :, :].rearrange("p a b c -> p (a b) c")
        fx = [w2r_flat[:, 0:TT, :], w2r_flat[:, TT:2 * TT, :], xg[:, :, :],
              hnT[:, :, :, :].rearrange("p a k t -> p a (k t)")]
        fm = [group_of(t, k) for t in (delta, du) for k in range(2)]
        fy = [[group_of(t[:, 4 * g:4 * g + 4, :], e) for e in range(2)] for t in (scratch, Cb) for g in range(NC // 2)]

        psB = [psum(f"psB{i}") for i in range(3)]
        psY = [psum(f"psY{i}") for i in range(2)]
        psP = [psum(f"psP{i}") for i in range(2)]
        psE = psum("psE")

        s_w = {k: sem(f"s_w_{k}") for k in ("early", "w1", "bias", "bst", "big")}
        s_plain = sem("s_plain")
        s_zero, s_wz = sem("s_zero"), sem("s_wz")
        s_const, s_cdve, s_a = sem("s_const"), sem("s_cdve"), sem("s_a")
        s_xl = [sem(f"s_xl{k}") for k in range(NK)]
        s_xst = [sem(f"s_xst{k}") for k in range(NK)]
        s_tst = [sem(f"s_tst{k}") for k in range(NK)]
        s_bn, s_mv, s_ve, s_rs, s_xn = sem("s_bn"), sem("s_mv"), sem("s_ve"), sem("s_rs"), sem("s_xn")
        s_tp, s_te, s_lm, s_lg = sem("s_tp"), sem("s_te"), sem("s_lm"), sem("s_lg")
        s_rt, s_rtd, s_rte, s_rank = sem("s_rt"), sem("s_rtd"), sem("s_rte"), sem("s_rank")
        s_route = sem("s_route")
        s_bbc, s_dbu, s_exp, s_scan, s_carry, s_g, s_tr = (sem(n) for n in (
            "s_bbc", "s_dbu", "s_exp", "s_scan", "s_carry", "s_g", "s_tr"))
        s_xT, s_xp, s_xe, s_cv, s_halo, s_u, s_xd, s_stk, s_stack = (sem(n) for n in (
            "s_xT", "s_xp", "s_xe", "s_cv", "s_halo", "s_u", "s_xd", "s_stk", "s_stack"))
        s_dm, s_dl, s_ab, s_ln, s_dadd, s_delta, s_Du = (sem(n) for n in (
            "s_dm", "s_dl", "s_ab", "s_ln", "s_dadd", "s_delta", "s_Du"))
        s_cm, s_cb = sem("s_cm"), sem("s_cb")
        s_zm, s_zc, s_z, s_gate = sem("s_zm"), sem("s_zc"), sem("s_z"), sem("s_gate")
        s_etm, s_et, s_eom, s_eo, s_om = sem("s_etm"), sem("s_et"), sem("s_eom"), sem("s_eo"), sem("s_om")
        s_scl = [sem(f"s_scl{k}") for k in range(4)]
        s_sc = [sem(f"s_sc{k}") for k in range(4)]
        s_xg, s_w2, s_ys = sem("s_xg"), sem("s_w2"), sem("s_ys")
        s_t1, s_mx, s_m1, s_mbn, s_mag, s_mve, s_mrs, s_mh, s_t2, s_mn, s_mg, s_m2, s_my = (sem(n) for n in (
            "s_t1", "s_mx", "s_m1", "s_mbn", "s_mag", "s_mve", "s_mrs", "s_mh", "s_t2", "s_mn", "s_mg",
            "s_m2", "s_my"))
        s_fx = [sem(f"s_fx{k}") for k in range(NK)]
        s_fg = [sem(f"s_fg{g}") for g in range(NC)]
        s_fo = [sem(f"s_fo{k}") for k in range(NK)]
        s_fd = [sem(f"s_fd{k}") for k in range(NK)]
        s_fa, s_gv = sem("s_fa"), sem("s_gv")

        ahead = [s_carry, s_eom, s_lg, s_m2, s_my, s_om, s_t1, s_te, s_tp, s_ys,
                 *s_fo, *s_fd, *s_tst, *s_xst]

        def wait(eng, s, value):
            if isinstance(value, int) and value <= 0:
                return
            value = value + 1 if any(s is a for a in ahead) else value
            assert isinstance(value, int) or value.min_val > 0
            eng.wait_ge(s, value)

        def col(ap, i):
            return ap[:, i:i + 1]

        def plain(eng):
            eng.sem_inc(s_plain, 1)

        FIRST, MID, LAST = "first", "mid", "last"

        def ring3(s):
            return s % 3 if s < UN - 1 else 1

        def before3(s):
            return {0: -4, 1: -1, 2: -2, UN - 1: UN - 3}.get(s, s - 3)

        jobs = {e: [[] for _ in range(UN)] for e in ("pe", "act", "dve", "pool", "sp")}

        def job(engine, step, family, k=0):
            def add(fn):
                jobs[engine][AT[step][k]].append((family, fn))
            return add

        def present(family, kind):
            return {"P": kind in ("pre", FIRST, MID), "W": kind in (FIRST, MID, LAST),
                    "Z": kind in (FIRST, MID, LAST), "E": kind in (MID, LAST, "post"),
                    "M": kind in (MID, LAST), "S": kind == FIRST, "G": kind == LAST}[family]

        uses, uses_at = [], []

        def use(name, family, step, k, released):
            uses.append((name, family, released))
            uses_at.append(AT[step][k])

        order = ["pre", FIRST, MID, LAST, "post"]

        def bank(name, family):
            return psP[place[name, family] % 2]

        def claim(pe, name, family, it, kind):
            k = place[name, family]
            same = [u for u in in_order[k % 2:k:2] if present(u[1], kind)]
            if same:
                s, v = same[-1][2](it)
            elif kind == "pre":
                return bank(name, family)
            else:
                before = order[order.index(kind) - 1]
                s, v = [u for u in in_order[k % 2::2] if present(u[1], before)][-1][2](it - 1)
            wait(pe, s, v)
            return bank(name, family)

        def bcast(pe, dst, st_, r):
            return pe.matmul(dst, sel[:, r:r + 1].to_broadcast([P, P]), st_[:, :], start=True, stop=True)

        def pe_unit(pe, it, s):
            if s == 0:
                wait(pe, s_stack, it + 1)
            wait(pe, s_scan, it * UN + before3(s) + 1)
            bcast(pe, psB[ring3(s)][:, :], stack, s % NS).then_inc(s_bbc, 1)

        def pe_sum(pe, it, s):
            dc, n = divmod(s, NS)
            y = psY[dc % 2]
            if n == 0:
                wait(pe, s_Du, it * DC + dc + 1)
                wait(pe, s_gate, it * DC + dc - 1)
                for tt in range(TT):
                    pe.matmul(y[:, tt * P:(tt + 1) * P], Du[:, dc, tt * P:(tt + 1) * P], ident[:, :],
                              start=(tt == 0), stop=False, is_transpose=True, skip_group_check=True)
            wait(pe, s_g, it * UN + s + 1)
            for tt in range(TT):
                mm = pe.matmul(y[:, tt * P:(tt + 1) * P], hc[:, s % GR, tt * P:(tt + 1) * P], ident[:, :],
                               start=False, stop=(n == NS - 1), is_transpose=True, skip_group_check=True)
            mm.then_inc(s_tr, 1)

        def act_unit(act, it, s):
            dc, n = divmod(s, NS)
            if n == 0:
                wait(act, s_delta, it * 2 + dc // 2 + 1)
            wait(act, s_g, it * UN + s - HR + 1)
            act.activation(hb[:, s % HR, :], delta[:, dc, :], ACT.Exp, scale=aneg[:, dc, n:n + 1]).then_inc(s_exp, 1)

        def dve_product(dve, it, s):
            dc, n = divmod(s, NS)
            if n == 0:
                wait(dve, s_delta, it * 2 + dc // 2 + 1)
            wait(dve, s_bbc, it * UN + s + 1)
            b = psB[ring3(s)][:, :]
            dve.tensor_tensor(b, du[:, dc, :], b, ALU.mult).then_inc(s_dbu, 1)

        def hc_turn(it, s):
            if not isinstance(it, int) or it not in (0, NC - 1):
                return 0
            mine = HC_DVE["last" if it else "first"]
            return mine.index(s) + 1 + (len(HC_DVE["first"]) if it else 0) if s in mine else 0

        def dve_hc(dve, it, s):
            turn = hc_turn(it, s)
            if turn:
                wait(dve, s_scan, it * UN + s + 1)
                if s < NS:
                    wait(dve, s_cb, it * NS + s % NS + 1)
                wait(dve, s_tr, it * UN + s - GR + 1)
                dve.tensor_tensor(hc[:, s % GR, :], hb[:, s % HR, :], Cb[:, s % NS, :], ALU.mult).then_inc(s_gv, 1)

        def dve_scan(dve, it, s):
            wait(dve, s_dbu, it * UN + s + 1)
            wait(dve, s_exp, it * UN + s + 1)
            h = hb[:, s % HR, :]
            dve.tensor_tensor_scan(h, h, psB[ring3(s)][:, :], col(carry, s), ALU.mult, ALU.add).then_inc(s_scan, 1)

        def pool_unit(pool, it, s):
            dc, n = divmod(s, NS)
            wait(pool, s_scan, it * UN + s + 1)
            if dc == 0:
                wait(pool, s_cb, it * NS + n + 1)
            turn = hc_turn(it, s)
            if turn:
                wait(pool, s_gv, turn)
            plain(pool)
            h = hb[:, s % HR, :]
            pool.tensor_tensor(col(carry, s), h[:, T - 1:T], keep[:, bass.ds(it + 1, 1)], ALU.mult).then_inc(s_g if turn else s_carry, 1)
            if turn:
                return
            wait(pool, s_tr, it * UN + s - GR + 1)
            pool.tensor_tensor(hc[:, s % GR, :], h, Cb[:, n, :], ALU.mult).then_inc(s_g, 1)

        @job("sp", "x_load", "P")
        def _(sp, it, kind):
            wait(sp, s_zm, (it + 1) * TT)
            sp.dma_start(xnT[:, :, :], xnT_d[bass.ds(it + 1, 1), :, :, :].rearrange("a p k t -> (a p) k t")
                         if not isinstance(it, int) else xnT_d[it + 1]).then_inc(s_xT, 16)

        for dc in range(DC):
            use(f"X{dc}", "P", "x_mm", dc * KC, lambda it, dc=dc: (s_cv, ((it + 1) * DC + dc) * 3 + 3))
            for kc in range(KC):
                @job("pe", "x_mm", "P", dc * KC + kc)
                def _(pe, it, kind, dc=dc, kc=kc):
                    if kc == 0:
                        if dc == 0:
                            wait(pe, s_xT, 16 * (it + 2))
                        claim(pe, f"X{dc}", "P", it, kind)
                    mm = pe.matmul(bank(f"X{dc}", "P")[:, :], win[:, kc, dc * P:(dc + 1) * P], xnT[:, kc, :],
                                   start=(kc == 0), stop=(kc == KC - 1))
                    if kc == KC - 1:
                        mm.then_inc(s_xp, 1)

            @job("act", "x_copy", "P", dc)
            def _(act, it, kind, dc=dc):
                j = (it + 1) * DC + dc
                ps, xi = bank(f"X{dc}", "P")[:, :], xin[:, dc % 2, :]
                wait(act, s_halo, j - 1)
                wait(act, s_halo, j - DC + 1)
                act.activation(xi[:, 0:KW - 1], halo[:, dc, :], ACT.Copy).then_inc(s_xe, 1)
                wait(act, s_xp, j + 1)
                act.activation(xi[:, KW - 1:], ps, ACT.Copy).then_inc(s_xe, 1)
                act.activation(ps, ps, ACT.Identity, bias=col(cb, dc), scale=cw[:, dc, KW - 1:KW]).then_inc(s_xe, 1)

            for k in range(KW - 1):
                @job("dve", "x_tap", "P", dc * (KW - 1) + k)
                def _(dve, it, kind, dc=dc, k=k):
                    j = (it + 1) * DC + dc
                    ps, xi = bank(f"X{dc}", "P")[:, :], xin[:, dc % 2, :]
                    if k == 0:
                        wait(dve, s_xe, j * 3 + 3)
                    if k == KW - 2 and dc == 0:
                        wait(dve, s_delta, 2 * (it + 1))
                    wait(dve, s_cv, j * 3 + k)
                    dve.scalar_tensor_tensor(out=u[:, dc, :] if k == KW - 2 else ps, in0=xi[:, k:k + T],
                                             scalar=cw[:, dc, k:k + 1], in1=ps, op0=ALU.mult,
                                             op1=ALU.add).then_inc(s_cv, 1)
                    if k == KW - 2:
                        dve.tensor_tensor(halo[:, dc, :], xi[:, T:T + KW - 1],
                                          keep[:, bass.ds(it + 2, 1)].to_broadcast([P, KW - 1]),
                                          ALU.mult).then_inc(s_halo, 1)

        @job("act", "x_silu", "P")
        def _(act, it, kind):
            wait(act, s_cv, (it + 2) * DC * 3)
            act.activation(u[:, :, :], u[:, :, :], ACT.Silu).then_inc(s_u, 1)

        use("XD", "P", "xd_mm", 0, lambda it: (s_stk, (it + 1) * 6 + 3))
        for dc in range(DC):
            @job("pe", "xd_mm", "P", dc)
            def _(pe, it, kind, dc=dc):
                if dc == 0:
                    claim(pe, "XD", "P", it, kind)
                    wait(pe, s_u, it + 2)
                mm = pe.matmul(bank("XD", "P")[:, :], wxd[:, dc, :], u[:, dc, :], start=(dc == 0), stop=(dc == DC - 1))
                if dc == DC - 1:
                    mm.then_inc(s_xd, 1)

        @job("dve", "stack", "P", 0)
        def _(dve, it, kind):
            p, ps = it + 1, bank("XD", "P")
            wait(dve, s_xd, p + 1)
            wait(dve, s_cb, p * NS)
            wait(dve, s_stack, p)
            wait(dve, s_dm, p * DC)
            dve.tensor_copy(xr[32:48, :], ps[32:48, :]).then_inc(s_stk, 1)
            dve.tensor_copy(stackN[:, :], ps[:, :]).then_inc(s_stk, 1)
            wait(dve, s_stk, p * 6 + 2)
            dve.tensor_tensor(xr[64:128, :], ps[64:128, :], stackN[64:128, :], ALU.subtract).then_inc(s_stk, 1)

        @job("dve", "stack", "P", 1)
        def _(dve, it, kind):
            p = it + 1
            wait(dve, s_stk, p * 6 + 3)
            dve.tensor_copy(stackN[64:128, :], xr[64:128, :]).then_inc(s_stk, 1)
            wait(dve, s_stk, p * 6 + 4)
            dve.tensor_tensor(xr[96:128, :], xr[96:128, :], stackN[96:128, :], ALU.subtract).then_inc(s_stk, 1)
            wait(dve, s_stk, p * 6 + 5)
            dve.tensor_copy(stackN[96:128, :], xr[96:128, :]).then_inc(s_stk, 1)

        def delta_jobs(family, pair, chunk):
            for dc in (2 * pair, 2 * pair + 1):
                use(f"D{dc}", family, "d_mm", dc, lambda it, dc=dc: (s_dl, chunk(it) * DC + dc + 1))

                @job("pe", "d_mm", family, dc)
                def _(pe, it, kind, dc=dc):
                    p = chunk(it)
                    ps = claim(pe, f"D{dc}", family, it, kind)
                    wait(pe, s_stk, p * 6 + 1)
                    pe.matmul(ps[:, :], wdt[32:48, dc * P:(dc + 1) * P], xr[32:48, :],
                              start=True, stop=True).then_inc(s_dm, 1)

                @job("act", "d_abs", family, dc)
                def _(act, it, kind, dc=dc):
                    p = chunk(it)
                    ps = bank(f"D{dc}", family)
                    wait(act, s_dm, p * DC + dc + 1)
                    wait(act, s_delta, p * 2 + pair)
                    act.activation(tmpA[:, dc % 2, :], ps[:, :], ACT.Abs, bias=col(bdt, dc)).then_inc(s_ab, 1)
                    act.activation(delta[:, dc, :], ps[:, :], ACT.Relu, bias=col(bdt, dc)).then_inc(s_dl, 1)

            @job("act", "d_ln", family, pair)
            def _(act, it, kind):
                q = chunk(it) * 2 + pair
                wait(act, s_ab, 2 * q + 2)
                act.activation(tmpA[:, :, :], tmpA[:, :, :], ACT.Exp, scale=-1.0).then_inc(s_ln, 1)
                wait(act, s_ln, 2 * q + 1)
                act.activation(tmpA[:, :, :], tmpA[:, :, :], ACT.Ln, bias=1.0).then_inc(s_ln, 1)

            @job("pool", "d_sum", family, pair)
            def _(pool, it, kind):
                q = chunk(it) * 2 + pair
                d, uu = delta[:, 2 * pair:2 * pair + 2, :], u[:, 2 * pair:2 * pair + 2, :]
                wait(pool, s_ln, 2 * q + 2)
                pool.tensor_tensor(d, d, tmpA[:, :, :], ALU.add).then_inc(s_dadd, 1)
                wait(pool, s_dadd, q + 1)
                pool.tensor_tensor(du[:, 2 * pair:2 * pair + 2, :], d, uu, ALU.mult).then_inc(s_delta, 1)

        delta_jobs("P", 0, lambda it: it + 1)
        delta_jobs("W", 1, lambda it: it)

        for dc in range(DC):
            @job("act", "du_skip", "P", dc)
            def _(act, it, kind, dc=dc):
                wait(act, s_u, it + 2)
                wait(act, s_tr, it * UN + dc * NS + 1)
                act.activation(Du[:, dc, :], u[:, dc, :], ACT.Copy, scale=col(dsk, dc)).then_inc(s_Du, 1)

        def c_jobs(n, family, chunk):
            use(f"C{n}", family, "c_mm", n, lambda it: (s_cb, chunk(it) * NS + n + 1))

            @job("pe", "c_mm", family, n)
            def _(pe, it, kind):
                ps = claim(pe, f"C{n}", family, it, kind)
                wait(pe, s_stk, chunk(it) * 6 + 6)
                bcast(pe, ps[:, :], stackN, NS + n).then_inc(s_cm, 1)

            @job("act", "c_copy", family, n)
            def _(act, it, kind):
                p = chunk(it)
                wait(act, s_cm, p * NS + n + 1)
                wait(act, s_g, p * UN - NS + n + 1)
                act.activation(Cb[:, n, :], bank(f"C{n}", family)[:, :], ACT.Copy).then_inc(s_cb, 1)

        for n in range(13):
            c_jobs(n, "P", lambda it: it + 1)
        for n in range(13, NS):
            c_jobs(n, "W", lambda it: it)

        for tt in range(TT):
            use(f"Z{tt}", "Z", "z_mm", tt * KC, lambda it, tt=tt: (s_zc, it * TT + tt + 1))
            for kc in range(KC):
                @job("pe", "z_mm", "Z", tt * KC + kc)
                def _(pe, it, kind, tt=tt, kc=kc):
                    if kc == 0:
                        claim(pe, f"Z{tt}", "Z", it, kind)
                    mm = pe.matmul(bank(f"Z{tt}", "Z")[:, :], xnT[:, kc, tt * P:(tt + 1) * P], win[:, kc, DI:],
                                   start=(kc == 0), stop=(kc == KC - 1))
                    if kc == KC - 1:
                        mm.then_inc(s_zm, 1)

            @job("act", "z_copy", "Z", tt)
            def _(act, it, kind, tt=tt):
                wait(act, s_zm, it * TT + tt + 1)
                act.activation(zs[:, tt, :], bank(f"Z{tt}", "Z")[:, :], ACT.Copy).then_inc(s_zc, 1)

        @job("act", "z_silu", "Z")
        def _(act, it, kind):
            wait(act, s_zc, (it + 1) * TT)
            act.activation(zs[:, :, :], zs[:, :, :], ACT.Silu).then_inc(s_z, 1)

        def gate(dve, it, dc):
            wait(dve, s_z, it + 1)
            wait(dve, s_tr, it * UN + (dc + 1) * NS)
            z = zs[:, :, dc * P:(dc + 1) * P]
            dve.tensor_tensor(z, z, psY[dc % 2][:, :].rearrange("p (a b) -> p a b", a=TT), ALU.mult).then_inc(s_gate, 1)

        for dc in range(DC - 1):
            job("dve", "gate", "Z", dc)(lambda dve, it, kind, dc=dc: gate(dve, it, dc))
        job("dve", "gate", "E", DC - 1)(lambda dve, it, kind: gate(dve, it - 1, DC - 1))

        for tt in range(TT):
            use(f"ET{tt}", "E", "e_tr", tt, lambda it, tt=tt: (s_et, (it - 1) * TT + tt + 1))
            use(f"EO{tt}", "E", "e_mm", tt, lambda it, tt=tt: (s_eo, (it - 1) * TT + tt + 1))

            @job("pe", "e_tr", "E", tt)
            def _(pe, it, kind, tt=tt):
                ps = claim(pe, f"ET{tt}", "E", it, kind)
                wait(pe, s_gate, it * DC)
                for dc in range(DC):
                    mm = pe.matmul(ps[:, dc * P:(dc + 1) * P], zs[:, tt, dc * P:(dc + 1) * P], ident[:, :],
                                   start=True, stop=True, is_transpose=True)
                mm.then_inc(s_etm, 1)

            @job("act", "e_trc", "E", tt)
            def _(act, it, kind, tt=tt):
                j = (it - 1) * TT + tt
                wait(act, s_etm, j + 1)
                if tt == 0:
                    wait(act, s_zero, 16)
                wait(act, s_eom, (it - 1) * TT + max(tt - 1, 0))
                act.activation(ygT[:, tt % 2, :, :], bank(f"ET{tt}", "E")[:, :].rearrange("p (a b) -> p a b", a=DC),
                               ACT.Copy).then_inc(s_et, 1)

            @job("pe", "e_mm", "E", tt)
            def _(pe, it, kind, tt=tt):
                ps = claim(pe, f"EO{tt}", "E", it, kind)
                wait(pe, s_et, (it - 1) * TT + tt + 1)
                for dc in range(DC):
                    mm = pe.matmul(ps[:, 0:D], ygT[:, tt % 2, dc, :], wout[:, dc, :], start=(dc == 0), stop=(dc == DC - 1))
                mm.then_inc(s_eom, 1)

            @job("act", "e_copy", "E", tt)
            def _(act, it, kind, tt=tt):
                wait(act, s_eom, (it - 1) * TT + tt + 1)
                if tt == 0:
                    wait(act, s_om, 16 * (it - 1))
                act.activation(om[:, tt, :], bank(f"EO{tt}", "E")[:, 0:D], ACT.Copy).then_inc(s_eo, 1)

        @job("sp", "e_store", "E")
        def _(sp, it, kind):
            wait(sp, s_eo, it * TT)
            sp.dma_start(om_d[bass.ds((it - 1) * T, T), :].rearrange("(a p) d -> p a d", p=P), om[:, :, :]).then_inc(s_om, 16)

        for i in range(TILES):
            @job("sp", "s_load", "S", i)
            def _(sp, it, kind, i=i):
                r = i % 4
                wait(sp, s_sc[r], 32 * (i // 4))
                sp.dma_start(xsrc[:, r, :], xn_d[i * P:(i + 1) * P, :]).then_inc(s_scl[r], 16)
            for k in range(2):
                @job("pool", "s_put", "S", 2 * i + k)
                def _(pool, it, kind, i=i, k=k):
                    r = i % 4
                    wait(pool, s_scl[r], 16 * (i // 4 + 1))
                    if i == 0 and k == 0:
                        wait(pool, s_zero, 16)
                    pool.indirect_dma_start(
                        out=xs_d[:, :], out_offset=bass.IndirectOffsetOnAxis(ap=slots[:, k, i:i + 1], axis=0),
                        in_=xsrc[:, r, :], in_offset=None).then_inc(s_sc[r], 16)

        def get_rows(pool, g, e, tt):
            i = g * TT + tt
            pool.indirect_dma_start(
                out=fy[g][e][:, tt, :], out_offset=None, in_=ys_d[:, :],
                in_offset=bass.IndirectOffsetOnAxis(ap=slots[:, e, i:i + 1], axis=0)).then_inc(s_fg[g], 16)

        for j in range(NC // 2 * 2 * TT):
            @job("pool", "g_get", "G", j)
            def _(pool, it, kind, j=j):
                if j == 0:
                    wait(pool, s_ys, 16 * (MT // GT))
                    wait(pool, s_m1, MT // 2)
                get_rows(pool, j // (2 * TT), j // TT % 2, j % TT)

        def in_kind(q, kind):
            return kind == MID or q * GT < MT - (NC - 2) * NG * GT

        for q in range(NG):
            def group(it, q=q):
                return (it - 1) * NG + q

            def tile0(it, q=q):
                return (it - 1) * (NG * GT) + q * GT

            def mjob(engine, step, k=0, n=1, q=q):
                def add(fn):
                    def run(eng, it, kind):
                        if in_kind(q, kind):
                            fn(eng, it)
                    job(engine, step, "M", q * n + k)(run)
                return add

            def pair0(it, q=q):
                return (it - 1) * (NG * GT // 2) + q * (GT // 2)

            @mjob("sp", "m_load")
            def _(sp, it, group=group, tile0=tile0, pair0=pair0, q=q):
                if q == 0:
                    for r in range(4):
                        wait(sp, s_sc[r], 32 * (TILES // 4))
                wait(sp, s_t1, pair0(it))
                sp.dma_start(xg[:, :, :], xs_d[bass.ds(tile0(it) * P, GT * P), :].rearrange("(a p) d -> p a d", p=P)).then_inc(s_xg, 16)
                for j in range(GT):
                    e = sp.value_load(etab[0:1, bass.ds(tile0(it) + j, 1)], min_val=0, max_val=E - 1)
                    if j == 0:
                        wait(sp, s_m2, pair0(it))
                    sp.dma_start(w2r[:, j, :, :], W2[bass.ds(e, 1), :, :].rearrange("a (k p) o -> p (a k) o", p=P)).then_inc(s_w2, 16)

            for h in range(GT // 2):
                @mjob("pe", "m_t1", h, 2)
                def _(pe, it, h=h, group=group, pair0=pair0):
                    pr = pair0(it) + h
                    if h == 0:
                        pe.wait_ge(s_w["w1"], 16)
                        pe.wait_ge(s_w["bias"], 48)
                        wait(pe, s_xg, 16 * (group(it) + 1))
                        wait(pe, s_my, pr)
                    else:
                        wait(pe, s_mn, pr)
                    for a in range(2):
                        for kc in range(KC):
                            mm = pe.matmul(psE[:, (a * KC + kc) * P:(a * KC + kc + 1) * P],
                                           xg[:, 2 * h + a, kc * P:(kc + 1) * P], ident[:, :],
                                           start=True, stop=True, is_transpose=True)
                    mm.then_inc(s_t1, 1)

                @mjob("act", "m_t1c", h, 2)
                def _(act, it, h=h, pair0=pair0):
                    wait(act, s_t1, pair0(it) + h + 1)
                    act.activation(xgT[:, :, :, :], psE[:, :].rearrange("p (a k t) -> p a k t", a=2, k=KC), ACT.Copy).then_inc(s_mx, 1)

                for a in range(2):
                    @mjob("pe", "m_w1", 2 * h + a, 4)
                    def _(pe, it, h=h, a=a, pair0=pair0, tile0=tile0):
                        if a == 0:
                            wait(pe, s_mx, pair0(it) + h + 1)
                            plain(pe)
                        e = pe.value_load(etab[0:1, bass.ds(tile0(it) + 2 * h + a, 1)], min_val=0, max_val=E - 1)
                        dst = psE[:, a * D:(a + 1) * D]
                        for kc in range(KC):
                            pe.matmul(dst, xgT[:, a, kc, :], w1[:, bass.ds(e, 1), kc, :].rearrange("p a d -> p (a d)"),
                                      start=(kc == 0), stop=False)
                        mm = pe.matmul(dst, pick6[:, 0, :], bias6[:, bass.ds(e * D, D)], start=False, stop=True)
                        if a == 1:
                            mm.then_inc(s_m1, 1)

                @mjob("dve", "m_bn", h, 2)
                def _(dve, it, h=h, pair0=pair0):
                    pr = pair0(it) + h
                    wait(dve, s_m1, pr + 1)
                    for a in range(2):
                        dve.bn_stats(st[:, 0, a, :], psE[:, a * D:(a + 1) * D]).then_inc(s_mbn, 1)
                    wait(dve, s_mbn, 2 * pr + 2)
                    plain(dve)
                    for a in range(2):
                        dve.bn_aggr(mv[:, 0, a, :], st[:, 0, a, :]).then_inc(s_mag, 1)

                @mjob("pool", "m_rstd", h, 2)
                def _(pool, it, h=h, pair0=pair0):
                    pr = pair0(it) + h
                    wait(pool, s_mag, 2 * pr + 2)
                    plain(pool)
                    pool.tensor_scalar(ve[:, 0, 0:2], mv[:, 0, 0:2, 1], EPS, None, ALU.add).then_inc(s_mve, 1)
                    wait(pool, s_mve, pr + 1)
                    pool.tensor_tensor(rstd[:, 0, 0:2], ve[:, 0, 0:2], mhalf[:, 0:2], ALU.pow).then_inc(s_mrs, 1)

                @mjob("dve", "m_hn", h, 2)
                def _(dve, it, h=h, pair0=pair0):
                    wait(dve, s_mrs, pair0(it) + h + 1)
                    for a in range(2):
                        dve.tensor_scalar(hn[:, a, :], psE[:, a * D:(a + 1) * D], mv[:, 0, a, 0:1], rstd[:, 0, a:a + 1],
                                          ALU.subtract, ALU.mult).then_inc(s_mh, 1)

                @mjob("pe", "m_t2", h, 2)
                def _(pe, it, h=h, pair0=pair0):
                    wait(pe, s_mh, 2 * (pair0(it) + h) + 2)
                    for a in range(2):
                        for kc in range(KC):
                            mm = pe.matmul(psE[:, (a * KC + kc) * P:(a * KC + kc + 1) * P],
                                           hn[:, a, kc * P:(kc + 1) * P], ident[:, :],
                                           start=True, stop=True, is_transpose=True)
                    mm.then_inc(s_t2, 1)

                @mjob("act", "m_t2c", h, 2)
                def _(act, it, h=h, pair0=pair0):
                    pr = pair0(it) + h
                    wait(act, s_t2, pr + 1)
                    if h == 0:
                        wait(act, s_m2, pr)
                    act.activation(hnT[:, 2 * h:2 * h + 2, :, :], psE[:, :].rearrange("p (a k t) -> p a k t", a=2, k=KC),
                                   ACT.Copy).then_inc(s_mn, 1)

            @mjob("act", "m_gelu")
            def _(act, it, tile0=tile0, pair0=pair0):
                t = tile0(it)
                wait(act, s_mn, pair0(it) + 2)
                for j in range(GT):
                    e = act.value_load(etab[0:1, bass.ds(t + j, 1)], min_val=0, max_val=E - 1)
                    for kc in range(KC):
                        ins = act.activation(hnT[:, j, kc, :], hnT[:, j, kc, :], ACT.Gelu,
                                             scale=g1t[:, bass.ds(e, 1), kc], bias=be1t[:, bass.ds(e, 1), kc])
                    ins.then_inc(s_mg, 1)

            for j in range(GT):
                @mjob("pe", "m_w2", j, 4)
                def _(pe, it, j=j, tile0=tile0, group=group, pair0=pair0):
                    t, h, a = tile0(it), j // 2, j % 2
                    wait(pe, s_mg, t + j + 1)
                    if j == 0:
                        wait(pe, s_w2, 16 * GT * (group(it) + 1))
                    elif j == 2:
                        wait(pe, s_my, pair0(it) + 1)
                    plain(pe)
                    e = pe.value_load(etab[0:1, bass.ds(t + j, 1)], min_val=0, max_val=E - 1)
                    dst = psE[:, a * D:(a + 1) * D]
                    for kc in range(KC):
                        pe.matmul(dst, hnT[:, j, kc, :], w2r[:, j, kc, :], start=(kc == 0), stop=False)
                    mm = pe.matmul(dst, pick6[:, 1, :], bias6[:, bass.ds(e * D, D)], start=False, stop=True)
                    if a == 1:
                        mm.then_inc(s_m2, 1)

            for h in range(GT // 2):
                @mjob("act", "m_yo", h, 2)
                def _(act, it, h=h, pair0=pair0, group=group):
                    wait(act, s_m2, pair0(it) + h + 1)
                    if h == 0:
                        wait(act, s_ys, 16 * group(it))
                    act.activation(yo[:, 2 * h:2 * h + 2, :], psE[:, :].rearrange("p (a d) -> p a d", a=2), ACT.Copy).then_inc(s_my, 1)

            @mjob("sp", "m_store")
            def _(sp, it, tile0=tile0, pair0=pair0):
                wait(sp, s_my, pair0(it) + 2)
                sp.dma_start(ys_d[bass.ds(tile0(it) * P, GT * P), :].rearrange("(a p) d -> p a d", p=P), yo[:, :, :]).then_inc(s_ys, 16)

        in_order = [uses[j] for j in sorted(range(len(uses)), key=lambda j: uses_at[j])]
        place = {u[:2]: j for j, u in enumerate(in_order)}

        units = {
            "pe": [(pe_unit, LEAD_B), (pe_sum, -LAG)],
            "act": [(act_unit, LEAD_A)],
            "dve": [(dve_product, 0), (dve_scan, 0)],
            "pool": [(pool_unit, 0)],
            "sp": [],
        }

        def unit_steps(name, eng, it, kind, slot):
            for fn, off in units[name]:
                s = slot + off
                if 0 <= s < UN:
                    fn(eng, it, s)
                elif s >= UN and kind != LAST:
                    fn(eng, it + 1, s - UN)
                elif s < 0 and kind != FIRST:
                    fn(eng, it - 1, s + UN)

        def side(name, eng, it, kind, slot):
            for family, fn in jobs[name][slot]:
                if present(family, kind):
                    fn(eng, it, kind)

        def next_stack(dve, it):
            wait(dve, s_stk, it * 6 + 6)
            wait(dve, s_bbc, it * UN)
            dve.tensor_copy(stack[:, :], stackN[:, :]).then_inc(s_stack, 1)

        def body(name, eng, it, kind):
            for s in range(UN):
                if name != "dve":
                    unit_steps(name, eng, it, kind, s)
                    side(name, eng, it, kind, s)
                elif s % 2 == 0:
                    for fn in (dve_product, dve_scan, dve_hc):
                        if fn is dve_hc and s == UN - 2 and kind != LAST:
                            next_stack(eng, it + 1)
                        fn(eng, it, s)
                        fn(eng, it, s + 1)
                    for k in (s, s + 1):
                        side(name, eng, it, kind, k)

        def prologue(name, eng, first=0, last=None):
            todo = [fn for s in range(UN) for family, fn in jobs[name][s] if present(family, "pre")]
            for fn in todo[first:last]:
                fn(eng, -1, "pre")

        def chunks(name, eng):
            if name == "dve":
                next_stack(dve=eng, it=0)
            for s in range(-LEAD_A, 0):
                for fn, off in units[name]:
                    if s + off >= 0:
                        fn(eng, 0, s + off)
            body(name, eng, 0, FIRST)
            with eng.Fori(1, NC - 1) as it:
                body(name, eng, it, MID)
            body(name, eng, NC - 1, LAST)
            for s in range(UN, UN + LAG):
                for fn, off in units[name]:
                    if off < 0 and s + off < UN:
                        fn(eng, NC - 1, s + off)

        def epilogue(name, eng):
            for s in range(UN):
                side(name, eng, NC, "post", s)

        NBIG = 2 + 3 + 2 * KC + 4 + 2
        NCONST = 8

        block = ctx.enter_context(nc.Block())

        @block.sync
        def _(sp):
            for s in ahead:
                sp.sem_inc(s, 1)
            xt = x.rearrange("(g a p) d -> g p a d", p=P, a=TT)

            def load_x(g, k):
                sp.dma_start(xraw[k], xt[bass.ds(g, 1)].rearrange("g p a d -> (g p) a d")).then_inc(s_xl[k], 16)

            load_x(0, 0)
            sp.dma_start(wr[:, :, :], Wr.rearrange("(k p) e -> p k e", p=P)).then_inc(s_w["early"], 16)
            sp.dma_start(brr[:, :], br.rearrange("(a e) -> a e", a=1)).then_inc(s_w["early"], 16)
            for k in range(1, NK):
                load_x(k, k)

            def norm_stores(i, more):
                for k in range(NK):
                    wait(sp, s_xn, i * (NK * TT) + (k + 1) * TT)
                    if more:
                        load_x(NK * i + k + NK, k)
                    sp.dma_start(xn_d[bass.ds((NK * i + k) * T, T), :].rearrange("(a p) d -> p a d", p=P), xnb[k]).then_inc(s_xst[k], 16)
                    wait(sp, s_te, i * (2 * NK) + 2 * k + 2)
                    sp.dma_start(xnT_d[bass.ds(NK * i + k, 1)].rearrange("g p k t -> (g p) k t"), xnTg[k]).then_inc(s_tst[k], 16)

            with sp.Fori(0, NC // NK - 1) as i:
                norm_stores(i, True)
            norm_stores(NC // NK - 1, False)
            wait(sp, s_tst[0], 16)
            prologue("sp", sp)
            sp.wait_ge(s_rt, 5)
            for b in range(2):
                for k in range(3):
                    sp.dma_start(b_d[3 * b + k, :].rearrange("(p d) -> p d", d=64), bparts[k][64 * b:64 * b + 64, :]).then_inc(s_w["bst"], 16)
            for k in range(NK):
                wait(sp, s_xst[k], 16 * (NC // NK))
                wait(sp, s_tst[k], 16 * (NC // NK))
            chunks("sp", sp)

            def load_x(g, k):
                sp.dma_start(fx[k], xt[bass.ds(g, 1)].rearrange("g p a d -> (g p) a d")).then_inc(s_fx[k], 16)

            def load_m(g, k):
                wait(sp, s_om, 16 * (g + 1))
                sp.dma_start(fm[k], om_d[bass.ds(g * T, T), :].rearrange("(a p) d -> p a d", p=P)).then_inc(s_fx[k], 16)

            wait(sp, s_m2, MT // 2)
            for k in range(NK):
                load_x(k, k)
            wait(sp, s_g, NC * UN)
            for k in range(NK):
                load_m(k, k)
            epilogue("sp", sp)

            def out_stores(i, more):
                for k in range(NK):
                    wait(sp, s_fd[k], (i + 1) * TT)
                    sp.dma_start(out[bass.ds((NK * i + k) * T, T), :].rearrange("(a p) d -> p a d", p=P), fx[k]).then_inc(s_fo[k], 16)
                if more:
                    for k in range(NK):
                        wait(sp, s_fo[k], 16 * (i + 1))
                        load_x(NK * i + k + NK, k)
                        load_m(NK * i + k + NK, k)

            with sp.Fori(0, NC // NK - 1) as i:
                out_stores(i, True)
            out_stores(NC // NK - 1, False)
            for k in range(NK):
                wait(sp, s_fo[k], 16 * (NC // NK))
            wait(sp, s_ys, 16 * (MT // GT))

        @block.gpsimd
        def _(pool):
            pool.memset(ident[:, :], 0.0).then_inc(s_const, 1)
            pool.memset(upper[:, :], 0.0).then_inc(s_const, 1)
            pool.memset(sel[:, :], 0.0).then_inc(s_const, 1)
            pool.memset(pick6[:, :, :], 1.0).then_inc(s_const, 1)
            pool.memset(reset, 1.0).then_inc(s_const, 1)
            pool.wait_ge(s_const, 5)
            ev = reset.rearrange("p (e i) -> p e i", i=TILES)
            pool.affine_select(out=ident[:, :], in_=ident[:, :], compare_op=ALU.not_equal, fill=1.0,
                               base=0, pattern=[[-1, P]], channel_multiplier=1).then_inc(s_const, 1)
            pool.affine_select(out=upper[:, :], in_=upper[:, :], compare_op=ALU.is_ge, fill=1.0,
                               base=0, pattern=[[-1, P]], channel_multiplier=1).then_inc(s_const, 1)
            pool.affine_select(out=ev, in_=ev, compare_op=ALU.not_equal, fill=0.0,
                               base=0, pattern=[[0, E], [1, TILES]], channel_multiplier=0).then_inc(s_const, 1)
            pool.affine_select(out=pick6[:, 0, :], in_=pick6[:, 0, :], compare_op=ALU.is_ge, fill=0.0,
                               base=2, pattern=[[0, P]], channel_multiplier=-1).then_inc(s_const, 1)
            pool.affine_select(out=pick6[:, 1, :], in_=pick6[:, 1, :], compare_op=ALU.is_ge, fill=0.0,
                               base=-3, pattern=[[0, P]], channel_multiplier=1).then_inc(s_const, 1)
            for k, q in enumerate((0, 2, 3)):
                pool.affine_select(out=sel[:, :], in_=sel[:, :], compare_op=ALU.not_equal, fill=1.0,
                                   base=-32 * q, pattern=[[-1, 2 * NS]], channel_multiplier=1).then_inc(s_const, 1)
                pool.wait_ge(s_const, 11 + k)
            kw = dict(channel_multiplier=0, allow_small_or_imprecise_dtypes=True)
            pool.iota(iotaE.rearrange("p (i e) -> p i e", e=E), pattern=[[0, TILES], [1, E]], base=-E, **kw).then_inc(s_const, 1)
            pool.iota(iotaJ.rearrange("p (e j) -> p e j", e=E), pattern=[[0, E], [P, TILES]], base=0, **kw).then_inc(s_const, 1)
            pool.iota(iotaT.rearrange("p (j e) -> p j e", e=E), pattern=[[1, MT], [0, E]], base=0, **kw).then_inc(s_const, 1)
            pool.wait_ge(s_cdve, NCONST)
            with pool.Fori(0, NC // 2) as i:
                for k in range(2):
                    wait(pool, s_mv, i * (2 * TT) + (k + 1) * TT)
                    plain(pool)
                    pool.tensor_scalar(ve[:, k, :], mv[:, k, :, 1], EPS, None, ALU.add).then_inc(s_ve, 1)
                    wait(pool, s_ve, i * 2 + k + 1)
                    pool.tensor_tensor(rstd[:, k, :], ve[:, k, :], mhalf[:, :], ALU.pow).then_inc(s_rs, 1)
            prologue("pool", pool)
            wait(pool, s_route, 1)
            chunks("pool", pool)

            wait(pool, s_g, NC * UN)
            for g in range(NC // 2, NC):
                for e in range(2):
                    for tt in range(TT):
                        get_rows(pool, g, e, tt)

        @block.scalar
        def _(act):
            bts = [b1.rearrange("e (a d) -> (e a) d", d=64), b2.rearrange("e (a d) -> (e a) d", d=64)]
            for b in range(2):
                act.dma_start(om[64 * b:64 * b + 64, 0, 0:64], bts[b]).then_inc(s_w["bias"], 16)
            act.dma_start(aneg[:, :, :], A_log.rearrange("(c p) n -> p c n", p=P)).then_inc(s_a, 16)
            act.dma_start(win[:, :, :], W_in.rearrange("(k p) e -> p k e", p=P)).then_inc(s_w["big"], 16)
            act.dma_start(cw[:, :, :], conv_w.rearrange("(c p) a k -> p c (a k)", p=P)).then_inc(s_w["big"], 16)
            with nc.allow_non_contiguous_dma(reason="a few hundred scalars by channel"):
                for dst, src in ((cb, conv_b), (bdt, b_dt), (dsk, D_skip)):
                    act.dma_start(dst[:, :], src.rearrange("(c p) -> p c", p=P)).then_inc(s_w["big"], 16)
                for dst, src in ((g1t, g1), (be1t, be1)):
                    for kc in range(KC):
                        act.dma_start(dst[:, :, kc], src[:, kc * P:(kc + 1) * P].rearrange("e p -> p e")).then_inc(s_w["big"], 16)
            wx = W_xproj.rearrange("(c p) m -> p c m", p=P)
            act.wait_ge(s_wz, 1)
            act.dma_start(wxd[:, :, 32:48], wx[:, :, 0:R]).then_inc(s_w["big"], 16)
            for q in (0, 2, 3):
                act.dma_start(wxd[:, :, 32 * q:32 * q + 32], wx[:, :, R:]).then_inc(s_w["big"], 16)
            act.dma_start(wdt[32:48, :], W_dt).then_inc(s_w["big"], 16)
            act.dma_start(wout[:, :, :], W_out.rearrange("(c p) o -> p c o", p=P)).then_inc(s_w["big"], 16)
            with act.Fori(0, NC // NK) as i:
                for k in range(NK):
                    wait(act, s_tst[k], 16 * i)
                    for kc in range(KC):
                        wait(act, s_tp, i * (2 * NK) + 2 * k + kc + 1)
                        act.activation(xnTg[k][:, kc, :], (psB + psY)[2 * (k % 2) + kc][:, :], ACT.Copy).then_inc(s_te, 1)
                    wait(act, s_lm, i * NK + k + 1)
                    act.activation(lg[:, bass.ds((NK * i + k) * (TT * E), TT * E)], psP[k % 2][:, 0:TT * E], ACT.Copy).then_inc(s_lg, 1)
            act.wait_ge(s_cdve, 1)
            act.dma_start(xs_d.rearrange("(p a b) d -> p a (b d)", p=P, b=4),
                          zero.unsqueeze(1).to_broadcast([P, MT // 4, 4 * D])).then_inc(s_zero, 16)
            act.wait_ge(s_a, 16)
            act.activation(aneg[:, :, :], aneg[:, :, :], ACT.Exp).then_inc(s_a, 1)
            act.wait_ge(s_w["big"], 16 * NBIG)
            prologue("act", act, 0, 2)
            act.wait_ge(s_rtd, 1)
            act.activation(scratch[:, 7, :], scratch[:, 6, :], ACT.Exp).then_inc(s_rte, 1)
            prologue("act", act, 2)
            act.wait_ge(s_w["bst"], 16 * 6)
            act.dma_start(bias6[:, :], b_d[:, :]).then_inc(s_w["bias"], 16)
            wait(act, s_route, 1)
            act.dma_start(w1[:, :, :, :], W1.rearrange("e (k p) h -> p e k h", p=P)).then_inc(s_w["w1"], 16)
            chunks("act", act)
            epilogue("act", act)

        @block.tensor
        def _(pe):
            pe.wait_ge(s_const, 16)
            pe.wait_ge(s_cdve, NCONST)
            pe.wait_ge(s_w["early"], 32)
            with pe.Fori(0, NC // NK) as i:
                for k in range(NK):
                    g = NK * i + k
                    wait(pe, s_xn, (g + 1) * TT)
                    for kc in range(KC):
                        for tt in range(TT):
                            mm = pe.matmul((psB + psY)[2 * (k % 2) + kc][:, tt * P:(tt + 1) * P],
                                           xnb[k][:, tt, kc * P:(kc + 1) * P], ident[:, :],
                                           start=True, stop=True, is_transpose=True)
                        mm.then_inc(s_tp, 1)
                    wait(pe, s_te, g * 2 + 2)
                    for tt in range(TT):
                        dst = psP[k % 2][:, tt * E:(tt + 1) * E]
                        for kc in range(KC):
                            pe.matmul(dst, xnTg[k][:, kc, tt * P:(tt + 1) * P], wr[:, kc, :], start=(kc == 0), stop=False)
                        mm = pe.matmul(dst, ones1[:, :], brr[:, :], start=False, stop=True)
                    mm.then_inc(s_lm, 1)
            pe.wait_ge(s_w["big"], 16 * NBIG)
            wait(pe, s_lg, NC)
            prologue("pe", pe, 0, 2 * KC)
            pe.wait_ge(s_rtd, 2)
            Mb = scratch[:, 8, 0:T // 2].bitcast(BF16)
            pe.matmul(psB[0][:, :], upper[:, :], Mb, start=True, stop=True).then_inc(s_rank, 1)
            pe.matmul(psB[1][:, :], onesb[:, :], Mb, start=True, stop=True).then_inc(s_rank, 1)
            prologue("pe", pe, 2 * KC)
            wait(pe, s_route, 1)
            chunks("pe", pe)
            epilogue("pe", pe)

        @block.vector
        def _(dve):
            def const(ins):
                ins.then_inc(s_cdve, 1)

            const(dve.memset(zero, 0.0))
            dve.memset(wxd[:, :, :], 0.0).then_inc(s_wz, 1)
            const(dve.memset(onesb[:, :], 1.0))
            const(dve.memset(ones1[:, :], 1.0))
            const(dve.memset(mhalf[:, :], -0.5))
            const(dve.memset(carry[:, :], 0.0))
            const(dve.memset(halo[:, :, :], 0.0))
            const(dve.memset(keep[:, :], 1.0))
            dve.wait_ge(s_cdve, 7)
            const(dve.memset(keep[:, 0:NC + 1:CPB], 0.0))

            bf = om[:, 0, 0:64]
            dve.wait_ge(s_w["bias"], 32)
            chain = [0]

            pre_done = [0]

            def link(ins):
                chain[0] += 1
                ins.then_inc(s_rt, 1)
                if chain[0] >= MIX and chain[0] % 2 == 0:
                    prologue("dve", dve, pre_done[0], pre_done[0] + 1)
                    pre_done[0] += 1
                dve.wait_ge(s_rt, chain[0])

            link(dve.tensor_copy(bparts[0], bf))
            link(dve.tensor_tensor(bf, bf, bparts[0], ALU.subtract))
            link(dve.tensor_copy(bparts[1], bf))
            link(dve.tensor_tensor(bf, bf, bparts[1], ALU.subtract))
            link(dve.tensor_copy(bparts[2], bf))

            with dve.Fori(0, NC // NK) as i:
                for pair in range(0, NK, 2):
                    for k in (pair, pair + 1):
                        wait(dve, s_xl[k], 16 * (i + 1))
                        for tt in range(TT):
                            dve.bn_stats(st[:, k % 2, tt, :], xraw[k][:, tt, :]).then_inc(s_bn, 1)
                        wait(dve, s_bn, i * (NK * TT) + (k + 1) * TT)
                        plain(dve)
                        for tt in range(TT):
                            dve.bn_aggr(mv[:, k % 2, tt, :], st[:, k % 2, tt, :]).then_inc(s_mv, 1)
                    for k in (pair, pair + 1):
                        wait(dve, s_rs, i * NK + k + 1)
                        wait(dve, s_xst[k], 16 * i)
                        wait(dve, s_tst[k], 16 * i)
                        for tt in range(TT):
                            dve.tensor_scalar(xnb[k][:, tt, :], xraw[k][:, tt, :], mv[:, k % 2, tt, 0:1],
                                              rstd[:, k % 2, tt:tt + 1], ALU.subtract, ALU.mult).then_inc(s_xn, 1)

            dve.wait_ge(s_a, 17)
            link(dve.tensor_scalar(aneg[:, :, :], aneg[:, :, :], -1.0, None, ALU.mult))

            def row(k):
                return scratch[:, k, :]

            def ie(ap):
                return ap.rearrange("p (i e) -> p i e", e=E)

            def ei(ap):
                return ap.rearrange("p (e i) -> p e i", e=E)

            def over_e(ap):
                return ap.unsqueeze(2).to_broadcast([P, TILES, E])

            def s32(k):
                return small[:, k, :]

            def s16(k):
                return small[:, k, 0:E]

            dve.wait_ge(s_const, 16)
            wait(dve, s_lg, NC)
            logits = lg

            def onehot(src, top, first, oh, t0, t1):
                link(dve.tensor_reduce(top, ie(src), AX.X, ALU.max))
                link(dve.tensor_tensor(ie(t0), ie(src), over_e(top), ALU.is_equal))
                link(dve.tensor_tensor(t1, t0, iotaE, ALU.mult))
                link(dve.tensor_reduce(first, ie(t1), AX.X, ALU.min))
                link(dve.tensor_tensor(ie(oh), ie(iotaE), over_e(first), ALU.is_equal))

            oh1, oh2 = row(2), row(5)
            onehot(logits, s32(0), s32(1), oh1, row(0), row(1))
            dve.tensor_tensor(ie(row(6)), ie(logits), over_e(s32(0)), ALU.subtract).then_inc(s_rtd, 1)
            link(dve.tensor_scalar(row(3), oh1, -2 * BIG, BIG, ALU.mult, ALU.add))
            link(dve.tensor_tensor(row(4), logits, row(3), ALU.min))
            onehot(row(4), s32(2), s32(3), oh2, row(0), row(1))
            dve.tensor_tensor(scratch[:, 8, 0:T // 2].bitcast(BF16), oh1, oh2, ALU.add).then_inc(s_rtd, 1)
            dve.wait_ge(s_rte, 1)
            link(dve.tensor_reduce(s32(4), ie(row(7)), AX.X, ALU.add))
            link(dve.reciprocal(s32(4), s32(4)))
            for k, oh in enumerate((oh1, oh2)):
                link(dve.tensor_tensor(row(0), row(7), oh, ALU.mult))
                link(dve.tensor_reduce(s32(5 + k), ie(row(0)), AX.X, ALU.add))
                link(dve.tensor_tensor(s32(5 + k), s32(5 + k), s32(4), ALU.mult))
            link(dve.tensor_tensor(s32(7), s32(5), s32(6), ALU.add))
            link(dve.tensor_scalar(s32(7), s32(7), 1e-9, None, ALU.max))
            link(dve.reciprocal(s32(7), s32(7)))
            for k in range(2):
                link(dve.tensor_tensor(wk[:, k, :], s32(5 + k), s32(7), ALU.mult))
            dve.wait_ge(s_rank, 2)
            link(dve.tensor_copy(ei(row(9)), psB[1][:, :].rearrange("p (i e) -> p e i", e=E)))
            link(dve.tensor_tensor_scan(row(11), reset, row(9), 0.0, ALU.mult, ALU.add))
            link(dve.tensor_tensor(row(12), row(11), row(9), ALU.subtract))
            count = ei(row(11))[:, :, TILES - 1]
            link(dve.tensor_tensor(ei(row(13)), count.unsqueeze(2).to_broadcast([P, E, TILES]), ei(iotaJ), ALU.is_gt))
            link(dve.tensor_reduce(s16(8), ei(row(13)), AX.X, ALU.add))
            link(dve.memset(s16(11), 1.0))
            link(dve.tensor_tensor_scan(s16(9), s16(11), s16(8), 0.0, ALU.mult, ALU.add))
            link(dve.tensor_tensor(s16(10), s16(9), s16(8), ALU.subtract))
            link(dve.tensor_scalar(s16(10), s16(10), float(P), None, ALU.mult))
            link(dve.tensor_tensor(ei(row(14)), ei(row(12)), s16(10).unsqueeze(2).to_broadcast([P, E, TILES]), ALU.add))
            link(dve.tensor_tensor(ie(row(15)), ie(psB[0][:, :]), row(14).rearrange("p (e i) -> p i e", e=E), ALU.add))
            for k, oh in enumerate((oh1, oh2)):
                link(dve.tensor_tensor(row(0), row(15), oh, ALU.mult))
                link(dve.tensor_reduce(s32(5), ie(row(0)), AX.X, ALU.add))
                link(dve.tensor_copy(slots[:, k, :], s32(5)))
            cmp_t = w1_flat[:, 0:MT * E].rearrange("p (j e) -> p j e", e=E)
            link(dve.tensor_tensor(cmp_t, s16(9).unsqueeze(1).to_broadcast([P, MT, E]),
                                   iotaT.rearrange("p (j e) -> p j e", e=E), ALU.is_le))
            tf = w1_flat[:, 2048:2048 + MT]
            link(dve.tensor_reduce(tf, cmp_t, AX.X, ALU.add))
            link(dve.tensor_scalar(tf, tf, float(E - 1), None, ALU.min))
            link(dve.tensor_copy(etab[:, :], tf))
            prologue("dve", dve, pre_done[0])
            for k in range(NK):
                wait(dve, s_xst[k], 16 * (NC // NK))
                wait(dve, s_tst[k], 16 * (NC // NK))
            dve.memset(small[:, 0, 0:1], 0.0).then_inc(s_route, 1)
            chunks("dve", dve)

            epilogue("dve", dve)

            for g in range(NC):
                k = g % NK
                wait(dve, s_fx[k], 32 * (g // NK + 1))
                dve.tensor_tensor(fx[k], fx[k], fm[k], ALU.add).then_inc(s_fa, 1)
                wait(dve, s_fg[g], 16 * 2 * TT)
                for e in range(2):
                    for tt in range(TT):
                        o = fx[k][:, tt, :]
                        wait(dve, s_fa, g * (1 + TT) + 1 + (0 if e == 0 else tt + 1))
                        dve.scalar_tensor_tensor(out=o, in0=fy[g][e][:, tt, :],
                                                 scalar=col(wk[:, e, :], g * TT + tt), in1=o,
                                                 op0=ALU.mult, op1=ALU.add).then_inc(s_fa if e == 0 else s_fd[k], 1)


_INS = ["L0_attn_x", "L0_attn_W_in", "L0_attn_conv_w", "L0_attn_conv_b", "L0_attn_W_xproj", "L0_attn_W_dt",
        "L0_attn_b_dt", "L0_attn_A_log", "L0_attn_D_skip", "L0_attn_W_out", "L0_ffn_Wr", "L0_ffn_br",
        "L0_ffn_W1", "L0_ffn_b1", "L0_ffn_g1", "L0_ffn_be1", "L0_ffn_W2", "L0_ffn_b2"]


def kernel(**inputs):
    import numpy as np
    import concourse.bacc as bacc
    from concourse.bass_utils import run_bass_kernel_spmd as run

    nc = bacc.Bacc("TRN2", target_bir_lowering=False, num_devices=1)
    arrays, args = {}, []
    for name in _INS:
        a = np.ascontiguousarray(inputs[name])
        if name == "L0_attn_x":
            a = a.reshape(NT, D)
        arrays[f"in_{name}"] = a
        args.append(nc.dram_tensor(f"in_{name}", a.shape, mybir.dt.from_np(a.dtype), kind="ExternalInput").ap())
    args.append(nc.dram_tensor("out", (NT, D), F32, kind="ExternalOutput").ap())
    build(nc, *args)
    r = run(nc, [arrays], core_ids=[0])
    return r.results[0]["out"].reshape(NB, L, D)
```

```python
from contextlib import ExitStack

import concourse.bass as bass
from concourse import mybir

F32, BF16, I32 = mybir.dt.float32, mybir.dt.bfloat16, mybir.dt.int32
ALU, ACT, AX = mybir.AluOpType, mybir.ActivationFunctionType, mybir.AxisListType

P = 128
NB, L, D = 2, 2048, 256
DI, NS, R = 512, 16, 16
KW = 4
E = 16
NT = NB * L
TILES = NT // P
T = 512
TT = T // P
NC = NT // T
CPB = L // T
DC = DI // P
KC = D // P
UN = DC * NS
GT = 4
NG = 3
MT = 80
EPS = 1e-5
MIX = [15, 18, 19, 20, 21, 22, 24, 24, 25, 25, 26, 27, 27, 37]
LAG = 3
LEAD_B = 2
LEAD_A = 3
HR = 8
GR = 4
NK = 4
BIG = 1e38

HC_DVE = {
    "first": [2, 6, 7, 8, 9, 10, 13, 14, 15, 16, 17, 18, 19, 20, 22, 23, 26, 29, 30, 31, 34, 40, 44, 45, 50, 52,
              54, 55, 56, 57, 58, 59, 61, 62],
    "last": [14, 19, 20, 22, 44, 45, 46, 47, 48, 50, 51, 52, 53, 55, 56, 57, 58, 59, 60, 61, 62, 63],
}

AT = {
    "g_get": [42, 42, 44, 45, 46, 46, 46, 47, 47, 47, 49, 49, 50, 50, 51, 53, 55, 55, 55, 55, 56, 57, 57, 58, 58,
              58, 59, 60, 60, 61, 61, 63],
    "x_load": [27],
    "x_mm": [27, 27, 29, 31, 34, 34, 39, 40],
    "x_copy": [26, 33, 37, 41],
    "x_tap": [29, 31, 32, 34, 37, 37, 37, 38, 40, 41, 42, 43],
    "x_silu": [44],
    "xd_mm": [45, 46, 47, 47],
    "stack": [48, 51],
    "d_mm": [49, 49, 2, 4],
    "d_abs": [52, 52, 3, 5],
    "d_ln": [52, 10],
    "d_sum": [54, 15],
    "du_skip": [45, 46, 46, 55],
    "c_mm": [51, 51, 52, 52, 53, 56, 57, 59, 61, 61, 61, 61, 62, 0, 0, 9],
    "c_copy": [52, 52, 52, 52, 56, 57, 57, 60, 60, 60, 60, 61, 61, 0, 1, 9],
    "z_mm": [13, 14, 16, 16, 21, 22, 22, 23],
    "z_copy": [17, 22, 24, 24],
    "z_silu": [24],
    "gate": [33, 38, 57, 2],
    "e_tr": [4, 5, 7, 11],
    "e_trc": [5, 6, 7, 11],
    "e_mm": [6, 11, 12, 15],
    "e_copy": [7, 10, 16, 19],
    "e_store": [27],
    "s_load": [0, 0, 1, 4, 5, 9, 10, 14, 16, 16, 20, 22, 22, 24, 24, 28, 31, 31, 33, 36, 38, 41, 42, 42, 46, 48,
               50, 53, 54, 57, 60, 63],
    "s_put": [0, 1, 2, 4, 4, 6, 6, 7, 7, 9, 10, 11, 12, 13, 14, 15, 15, 16, 17, 18, 19, 20, 21, 22, 23, 24, 25,
              26, 27, 28, 29, 30, 30, 31, 33, 33, 34, 35, 36, 37, 37, 37, 37, 41, 42, 43, 44, 45, 45, 47, 47, 49,
              49, 50, 51, 52, 53, 54, 56, 56, 57, 57, 59, 60],
    "m_load": [1, 11, 45],
    "m_t1": [2, 8, 21, 30, 42, 48],
    "m_t1c": [1, 7, 23, 29, 43, 51],
    "m_w1": [3, 3, 9, 9, 26, 26, 31, 31, 44, 44, 50, 50],
    "m_bn": [4, 11, 26, 32, 45, 53],
    "m_rstd": [2, 11, 25, 32, 42, 50],
    "m_hn": [4, 12, 28, 34, 46, 55],
    "m_t2": [6, 14, 29, 35, 47, 54],
    "m_t2c": [6, 17, 29, 37, 49, 56],
    "m_gelu": [17, 37, 56],
    "m_w2": [17, 17, 19, 19, 38, 38, 41, 41, 56, 56, 57, 59],
    "m_yo": [17, 19, 38, 42, 56, 59],
    "m_store": [15, 56, 62],
}
assert UN % 3 == 1
assert MT >= 2 * NT // P + E - 1 and MT % GT == 0


def build(nc, x, W_in, conv_w, conv_b, W_xproj, W_dt, b_dt, A_log, D_skip, W_out,
          Wr, br, W1, b1, g1, be1, W2, b2, out):
    ctx = ExitStack()
    with ctx:
        def sb(name, shape, dt=F32):
            return ctx.enter_context(nc.sbuf_tensor(name, shape, dt))

        def psum(name):
            return ctx.enter_context(nc.psum_tensor(name, [P, 512], F32))

        def sem(name):
            return ctx.enter_context(nc.semaphore(name))

        def dram(name, shape, dt=F32):
            return nc.dram_tensor(name, shape, dt, kind="Internal").ap()

        xn_d = dram("xn_d", (NT, D))
        xnT_d = dram("xnT_d", (NC, P, KC, T))
        xs_d = dram("xs_d", (MT * P, D))
        ys_d = dram("ys_d", (MT * P, D))
        om_d = dram("om_d", (NT, D))
        b_d = dram("b_d", (6, E * D), BF16)

        w1 = sb("w1", [P, E, KC, D])
        w2r = sb("w2r", [P, GT, KC, D])
        win = sb("win", [P, KC, 2 * DI])
        wout = sb("wout", [P, DC, D])
        wxd = sb("wxd", [P, DC, P])
        wdt = sb("wdt", [P, DI])
        wr = sb("wr", [P, KC, E])
        brc = sb("brc", [E, 1])
        cw = sb("cw", [P, DC, KW])
        cb = sb("cb", [P, DC])
        bdt = sb("bdt", [P, DC])
        dsk = sb("dsk", [P, DC])
        aneg = sb("aneg", [P, DC, NS])
        g1t = sb("g1t", [P, E, KC])
        be1t = sb("be1t", [P, E, KC])
        bias6 = sb("bias6", [6, E * D], BF16)
        ident = sb("ident", [P, P])
        upper = sb("upper", [P, P], BF16)
        onesb = sb("onesb", [P, P], BF16)
        pick6 = sb("pick6", [6, 2, P], BF16)
        sel = sb("sel", [P, 2 * NS], BF16)
        keep = sb("keep", [P, NC + 1])
        mhalf = sb("mhalf", [P, TT])
        xnT = sb("xnT", [P, KC, T])
        xin = sb("xin", [P, 2, T + KW - 1])
        halo = sb("halo", [P, DC, KW - 1])
        u = sb("u", [P, DC, T])
        Du = sb("Du", [P, DC, T])
        delta = sb("delta", [P, DC, T])
        du = sb("du", [P, DC, T])
        tmpA = sb("tmpA", [P, 2, T])
        xr = sb("xr", [P, T])
        stackN = sb("stackN", [P, T], BF16)
        stack = sb("stack", [P, T], BF16)
        Cb = sb("Cb", [P, NS, T])
        hb = sb("hb", [P, HR, T])
        hc = sb("hc", [P, GR, T])
        carry = sb("carry", [P, UN])
        zs = sb("zs", [P, TT, DI])
        ygT = sb("ygT", [P, 2, DC, P])
        om = sb("om", [P, TT, D])
        xg = sb("xg", [P, GT, D])
        xgT = sb("xgT", [P, 2, KC, P])
        hn = sb("hn", [P, 2, D])
        hnT = sb("hnT", [P, GT, KC, P])
        yo = sb("yo", [P, GT, D])
        st = sb("st", [P, 2, TT, 6])
        mv = sb("mv", [P, 2, TT, 2])
        ve = sb("ve", [P, 2, TT])
        rstd = sb("rstd", [P, 2, TT])
        slots = sb("slots", [P, 2, TILES], I32)
        wk = sb("wk", [P, 2, TILES])
        etab = sb("etab", [P, MT], I32)
        small = sb("small", [P, 12, TILES])

        def group_of(t, k):
            return t[:, 2 * k:2 * k + 2, :].rearrange("p a (b d) -> p (a b) d", d=D)

        xraw = [group_of(Cb, k) for k in range(NK)]
        xnTg = [Cb[:, 2 * (NK + k):2 * (NK + k) + 2, :] for k in range(NK)]
        xnb = [group_of(hb, k) for k in range(NK)]
        lg = zs[:, 3, :]
        lgT = [hc[0:E, k, :] for k in range(2)]
        iotaE, reset, iotaJ = zs[:, 0, :], zs[:, 1, :], zs[:, 2, :]
        iotaT = w2r[:, :, :, :].rearrange("p a b c -> p (a b c)")[:, 0:MT * E]
        w1_flat = w1[:, :, :, :].rearrange("p a b c -> p (a b c)")
        scratch = w1_flat.rearrange("p (a b) -> p a b", b=T)
        bparts = [om[:, 1, 32 * k:32 * k + 32].bitcast(BF16) for k in range(3)]
        xsrc = xg
        zero = ygT[:, :, :, :].rearrange("p a b c -> p (a b c)")

        w2r_flat = w2r[:, :, :, :].rearrange("p a b c -> p (a b) c")
        fx = [w2r_flat[:, 0:TT, :], w2r_flat[:, TT:2 * TT, :], xg[:, :, :],
              hnT[:, :, :, :].rearrange("p a k t -> p a (k t)"), *(group_of(hb, k) for k in range(NC // 2))]
        fm = [group_of(t, k) for t in (delta, du, u, Du) for k in range(2)]
        fy = [[group_of(t[:, 4 * g:4 * g + 4, :], e) for e in range(2)] for t in (scratch, Cb) for g in range(NC // 2)]

        psB = [psum(f"psB{i}") for i in range(3)]
        psY = [psum(f"psY{i}") for i in range(2)]
        psP = [psum(f"psP{i}") for i in range(2)]
        psE = psum("psE")

        s_w = {k: sem(f"s_w_{k}") for k in ("early", "w1", "bias", "bst", "big")}
        s_plain = sem("s_plain")
        s_zero, s_wz = sem("s_zero"), sem("s_wz")
        s_const, s_cdve, s_a = sem("s_const"), sem("s_cdve"), sem("s_a")
        s_xl = [sem(f"s_xl{k}") for k in range(NK)]
        s_xst = [sem(f"s_xst{k}") for k in range(NK)]
        s_tst = [sem(f"s_tst{k}") for k in range(NK)]
        s_bn, s_mv, s_ve, s_rs, s_xn = sem("s_bn"), sem("s_mv"), sem("s_ve"), sem("s_rs"), sem("s_xn")
        s_tp, s_te, s_lm, s_lc, s_lv, s_lg = (sem(n) for n in ("s_tp", "s_te", "s_lm", "s_lc", "s_lv", "s_lg"))
        s_rt, s_rtd, s_rte, s_rank = sem("s_rt"), sem("s_rtd"), sem("s_rte"), sem("s_rank")
        s_route = sem("s_route")
        s_bbc, s_dbu, s_exp, s_scan, s_carry, s_g, s_tr = (sem(n) for n in (
            "s_bbc", "s_dbu", "s_exp", "s_scan", "s_carry", "s_g", "s_tr"))
        s_xT, s_xp, s_xe, s_cv, s_halo, s_u, s_xd, s_stk, s_stack = (sem(n) for n in (
            "s_xT", "s_xp", "s_xe", "s_cv", "s_halo", "s_u", "s_xd", "s_stk", "s_stack"))
        s_dm, s_dl, s_ab, s_ln, s_dadd, s_delta, s_Du = (sem(n) for n in (
            "s_dm", "s_dl", "s_ab", "s_ln", "s_dadd", "s_delta", "s_Du"))
        s_cm, s_cb = sem("s_cm"), sem("s_cb")
        s_zm, s_zc, s_z, s_gate = sem("s_zm"), sem("s_zc"), sem("s_z"), sem("s_gate")
        s_etm, s_et, s_eom, s_eo, s_om = sem("s_etm"), sem("s_et"), sem("s_eom"), sem("s_eo"), sem("s_om")
        s_scl = [sem(f"s_scl{k}") for k in range(4)]
        s_sc = [sem(f"s_sc{k}") for k in range(4)]
        s_xg, s_w2, s_ys = sem("s_xg"), sem("s_w2"), sem("s_ys")
        s_t1, s_mx, s_m1, s_mbn, s_mag, s_mve, s_mrs, s_mh, s_t2, s_mn, s_mg, s_m2, s_my = (sem(n) for n in (
            "s_t1", "s_mx", "s_m1", "s_mbn", "s_mag", "s_mve", "s_mrs", "s_mh", "s_t2", "s_mn", "s_mg",
            "s_m2", "s_my"))
        s_fx = [sem(f"s_fx{g}") for g in range(NC)]
        s_fg = [sem(f"s_fg{g}") for g in range(NC)]
        s_fd, s_fo = sem("s_fd"), sem("s_fo")
        s_fa, s_fs, s_gv = sem("s_fa"), sem("s_fs"), sem("s_gv")

        ahead = [s_eom, s_lg, s_m2, s_my, s_om, s_t1, s_te, s_tp, s_ys,
                 *s_tst, *s_xst]

        def wait(eng, s, value):
            if isinstance(value, int) and value <= 0:
                return
            value = value + 1 if any(s is a for a in ahead) else value
            assert isinstance(value, int) or value.min_val > 0
            eng.wait_ge(s, value)

        def col(ap, i):
            return ap[:, i:i + 1]

        def plain(eng):
            eng.sem_inc(s_plain, 1)

        FIRST, MID, LAST = "first", "mid", "last"

        def ring3(s):
            return s % 3 if s < UN - 1 else 1

        def before3(s):
            return {0: -4, 1: -1, 2: -2, UN - 1: UN - 3}.get(s, s - 3)

        jobs = {e: [[] for _ in range(UN)] for e in ("pe", "act", "dve", "pool", "sp")}

        def job(engine, step, family, k=0):
            def add(fn):
                jobs[engine][AT[step][k]].append((family, fn))
            return add

        def present(family, kind):
            return {"P": kind in ("pre", FIRST, MID), "W": kind in (FIRST, MID, LAST),
                    "Z": kind in (FIRST, MID, LAST), "E": kind in (MID, LAST, "post"),
                    "M": kind in (MID, LAST), "S": kind == FIRST, "G": kind == LAST}[family]

        uses, uses_at = [], []

        def use(name, family, step, k, released):
            uses.append((name, family, released))
            uses_at.append(AT[step][k])

        order = ["pre", FIRST, MID, LAST, "post"]

        def bank(name, family):
            return psP[place[name, family] % 2]

        def claim(pe, name, family, it, kind):
            k = place[name, family]
            same = [u for u in in_order[k % 2:k:2] if present(u[1], kind)]
            if same:
                s, v = same[-1][2](it)
            elif kind == "pre":
                return bank(name, family)
            else:
                before = order[order.index(kind) - 1]
                s, v = [u for u in in_order[k % 2::2] if present(u[1], before)][-1][2](it - 1)
            wait(pe, s, v)
            return bank(name, family)

        def bcast(pe, dst, st_, r):
            return pe.matmul(dst, sel[:, r:r + 1].to_broadcast([P, P]), st_[:, :], start=True, stop=True)

        def pe_unit(pe, it, s):
            if s == 0:
                wait(pe, s_stack, it + 1)
            wait(pe, s_scan, it * UN + before3(s) + 1)
            bcast(pe, psB[ring3(s)][:, :], stack, s % NS).then_inc(s_bbc, 1)

        def pe_sum(pe, it, s):
            dc, n = divmod(s, NS)
            y = psY[dc % 2]
            if n == 0:
                wait(pe, s_Du, it * DC + dc + 1)
                wait(pe, s_gate, it * DC + dc - 1)
                for tt in range(TT):
                    pe.matmul(y[:, tt * P:(tt + 1) * P], Du[:, dc, tt * P:(tt + 1) * P], ident[:, :],
                              start=(tt == 0), stop=False, is_transpose=True, skip_group_check=True)
            wait(pe, s_g, it * UN + s + 1)
            for tt in range(TT):
                mm = pe.matmul(y[:, tt * P:(tt + 1) * P], hc[:, s % GR, tt * P:(tt + 1) * P], ident[:, :],
                               start=False, stop=(n == NS - 1), is_transpose=True, skip_group_check=True)
            mm.then_inc(s_tr, 1)

        def act_unit(act, it, s):
            dc, n = divmod(s, NS)
            if n == 0:
                wait(act, s_delta, it * 2 + dc // 2 + 1)
            wait(act, s_g, it * UN + s - HR + 1)
            act.activation(hb[:, s % HR, :], delta[:, dc, :], ACT.Exp, scale=aneg[:, dc, n:n + 1]).then_inc(s_exp, 1)

        def dve_product(dve, it, s):
            dc, n = divmod(s, NS)
            if n == 0:
                wait(dve, s_delta, it * 2 + dc // 2 + 1)
            wait(dve, s_bbc, it * UN + s + 1)
            b = psB[ring3(s)][:, :]
            dve.tensor_tensor(b, du[:, dc, :], b, ALU.mult).then_inc(s_dbu, 1)

        def hc_turn(it, s):
            if not isinstance(it, int) or it not in (0, NC - 1):
                return 0
            mine = HC_DVE["last" if it else "first"]
            return mine.index(s) + 1 + (len(HC_DVE["first"]) if it else 0) if s in mine else 0

        def dve_hc(dve, it, s):
            turn = hc_turn(it, s)
            if turn:
                wait(dve, s_scan, it * UN + s + 1)
                if s < NS:
                    wait(dve, s_cb, it * NS + s % NS + 1)
                wait(dve, s_tr, it * UN + s - GR + 1)
                dve.tensor_tensor(hc[:, s % GR, :], hb[:, s % HR, :], Cb[:, s % NS, :], ALU.mult).then_inc(s_gv, 1)

        def dve_scan(dve, it, s):
            wait(dve, s_dbu, it * UN + s + 1)
            wait(dve, s_exp, it * UN + s + 1)
            h = hb[:, s % HR, :]
            dve.tensor_tensor_scan(h, h, psB[ring3(s)][:, :], col(carry, s), ALU.mult, ALU.add).then_inc(s_scan, 1)

        def pool_units(pool, it, s):
            turns = [hc_turn(it, s), hc_turn(it, s + 1)]

            def carries(ours):
                plain(pool)
                ins = pool.tensor_tensor(carry[:, s:s + 2], hb[:, s % HR:s % HR + 2, T - 1],
                                         keep[:, bass.ds(it + 1, 1)].to_broadcast([P, 2]), ALU.mult)
                ins.then_inc(s_g if ours else s_carry, ours or 1)

            def product(s, count):
                n = s % NS
                if s < NS:
                    wait(pool, s_cb, it * NS + n + 1)
                wait(pool, s_tr, it * UN + s - GR + 1)
                pool.tensor_tensor(hc[:, s % GR, :], hb[:, s % HR, :], Cb[:, n, :], ALU.mult).then_inc(s_g, count)

            wait(pool, s_scan, it * UN + s + 2)
            if any(turns):
                wait(pool, s_gv, max(turns))
                carries(2 if all(turns) else 1 if turns[0] else 0)
                if turns[1] and not turns[0]:
                    product(s, 2)
                elif not turns[1]:
                    product(s + 1, 1)
            else:
                if not (isinstance(it, int) and it == NC - 1):
                    carries(0)
                product(s, 1)
                product(s + 1, 1)

        @job("sp", "x_load", "P")
        def _(sp, it, kind):
            wait(sp, s_zm, (it + 1) * TT)
            sp.dma_start(xnT[:, :, :], xnT_d[bass.ds(it + 1, 1), :, :, :].rearrange("a p k t -> (a p) k t")
                         if not isinstance(it, int) else xnT_d[it + 1]).then_inc(s_xT, 16)

        for dc in range(DC):
            use(f"X{dc}", "P", "x_mm", dc * KC, lambda it, dc=dc: (s_cv, ((it + 1) * DC + dc) * 3 + 3))
            for kc in range(KC):
                @job("pe", "x_mm", "P", dc * KC + kc)
                def _(pe, it, kind, dc=dc, kc=kc):
                    if kc == 0:
                        if dc == 0:
                            wait(pe, s_xT, 16 * (it + 2))
                        claim(pe, f"X{dc}", "P", it, kind)
                    mm = pe.matmul(bank(f"X{dc}", "P")[:, :], win[:, kc, dc * P:(dc + 1) * P], xnT[:, kc, :],
                                   start=(kc == 0), stop=(kc == KC - 1))
                    if kc == KC - 1:
                        mm.then_inc(s_xp, 1)

            @job("act", "x_copy", "P", dc)
            def _(act, it, kind, dc=dc):
                j = (it + 1) * DC + dc
                ps, xi = bank(f"X{dc}", "P")[:, :], xin[:, dc % 2, :]
                wait(act, s_halo, j - 1)
                wait(act, s_halo, j - DC + 1)
                act.activation(xi[:, 0:KW - 1], halo[:, dc, :], ACT.Copy).then_inc(s_xe, 1)
                wait(act, s_xp, j + 1)
                act.activation(xi[:, KW - 1:], ps, ACT.Copy).then_inc(s_xe, 1)
                act.activation(ps, ps, ACT.Identity, bias=col(cb, dc), scale=cw[:, dc, KW - 1:KW]).then_inc(s_xe, 1)

            for k in range(KW - 1):
                @job("dve", "x_tap", "P", dc * (KW - 1) + k)
                def _(dve, it, kind, dc=dc, k=k):
                    j = (it + 1) * DC + dc
                    ps, xi = bank(f"X{dc}", "P")[:, :], xin[:, dc % 2, :]
                    if k == 0:
                        wait(dve, s_xe, j * 3 + 3)
                    if k == KW - 2 and dc == 0:
                        wait(dve, s_delta, 2 * (it + 1))
                    wait(dve, s_cv, j * 3 + k)
                    dve.scalar_tensor_tensor(out=u[:, dc, :] if k == KW - 2 else ps, in0=xi[:, k:k + T],
                                             scalar=cw[:, dc, k:k + 1], in1=ps, op0=ALU.mult,
                                             op1=ALU.add).then_inc(s_cv, 1)
                    if k == KW - 2:
                        dve.tensor_tensor(halo[:, dc, :], xi[:, T:T + KW - 1],
                                          keep[:, bass.ds(it + 2, 1)].to_broadcast([P, KW - 1]),
                                          ALU.mult).then_inc(s_halo, 1)

        @job("act", "x_silu", "P")
        def _(act, it, kind):
            wait(act, s_cv, (it + 2) * DC * 3)
            act.activation(u[:, :, :], u[:, :, :], ACT.Silu).then_inc(s_u, 1)

        use("XD", "P", "xd_mm", 0, lambda it: (s_stk, (it + 1) * 6 + 3))
        for dc in range(DC):
            @job("pe", "xd_mm", "P", dc)
            def _(pe, it, kind, dc=dc):
                if dc == 0:
                    claim(pe, "XD", "P", it, kind)
                    wait(pe, s_u, it + 2)
                mm = pe.matmul(bank("XD", "P")[:, :], wxd[:, dc, :], u[:, dc, :], start=(dc == 0), stop=(dc == DC - 1))
                if dc == DC - 1:
                    mm.then_inc(s_xd, 1)

        @job("dve", "stack", "P", 0)
        def _(dve, it, kind):
            p, ps = it + 1, bank("XD", "P")
            wait(dve, s_xd, p + 1)
            wait(dve, s_cb, p * NS)
            wait(dve, s_stack, p)
            wait(dve, s_dm, p * DC)
            dve.tensor_copy(xr[32:48, :], ps[32:48, :]).then_inc(s_stk, 1)
            dve.tensor_copy(stackN[:, :], ps[:, :]).then_inc(s_stk, 1)
            wait(dve, s_stk, p * 6 + 2)
            dve.tensor_tensor(xr[64:128, :], ps[64:128, :], stackN[64:128, :], ALU.subtract).then_inc(s_stk, 1)

        @job("dve", "stack", "P", 1)
        def _(dve, it, kind):
            p = it + 1
            wait(dve, s_stk, p * 6 + 3)
            dve.tensor_copy(stackN[64:128, :], xr[64:128, :]).then_inc(s_stk, 1)
            wait(dve, s_stk, p * 6 + 4)
            dve.tensor_tensor(xr[96:128, :], xr[96:128, :], stackN[96:128, :], ALU.subtract).then_inc(s_stk, 1)
            wait(dve, s_stk, p * 6 + 5)
            dve.tensor_copy(stackN[96:128, :], xr[96:128, :]).then_inc(s_stk, 1)

        def delta_jobs(family, pair, chunk):
            for dc in (2 * pair, 2 * pair + 1):
                use(f"D{dc}", family, "d_mm", dc, lambda it, dc=dc: (s_dl, chunk(it) * DC + dc + 1))

                @job("pe", "d_mm", family, dc)
                def _(pe, it, kind, dc=dc):
                    p = chunk(it)
                    ps = claim(pe, f"D{dc}", family, it, kind)
                    wait(pe, s_stk, p * 6 + 1)
                    pe.matmul(ps[:, :], wdt[32:48, dc * P:(dc + 1) * P], xr[32:48, :],
                              start=True, stop=True).then_inc(s_dm, 1)

                @job("act", "d_abs", family, dc)
                def _(act, it, kind, dc=dc):
                    p = chunk(it)
                    ps = bank(f"D{dc}", family)
                    wait(act, s_dm, p * DC + dc + 1)
                    wait(act, s_delta, p * 2 + pair)
                    act.activation(tmpA[:, dc % 2, :], ps[:, :], ACT.Abs, bias=col(bdt, dc)).then_inc(s_ab, 1)
                    act.activation(delta[:, dc, :], ps[:, :], ACT.Relu, bias=col(bdt, dc)).then_inc(s_dl, 1)

            @job("act", "d_ln", family, pair)
            def _(act, it, kind):
                q = chunk(it) * 2 + pair
                wait(act, s_ab, 2 * q + 2)
                act.activation(tmpA[:, :, :], tmpA[:, :, :], ACT.Exp, scale=-1.0).then_inc(s_ln, 1)
                wait(act, s_ln, 2 * q + 1)
                act.activation(tmpA[:, :, :], tmpA[:, :, :], ACT.Ln, bias=1.0).then_inc(s_ln, 1)

            @job("pool", "d_sum", family, pair)
            def _(pool, it, kind):
                q = chunk(it) * 2 + pair
                d, uu = delta[:, 2 * pair:2 * pair + 2, :], u[:, 2 * pair:2 * pair + 2, :]
                wait(pool, s_ln, 2 * q + 2)
                pool.tensor_tensor(d, d, tmpA[:, :, :], ALU.add).then_inc(s_dadd, 1)
                wait(pool, s_dadd, q + 1)
                pool.tensor_tensor(du[:, 2 * pair:2 * pair + 2, :], d, uu, ALU.mult).then_inc(s_delta, 1)

        delta_jobs("P", 0, lambda it: it + 1)
        delta_jobs("W", 1, lambda it: it)

        for dc in range(DC):
            @job("act", "du_skip", "P", dc)
            def _(act, it, kind, dc=dc):
                wait(act, s_u, it + 2)
                wait(act, s_tr, it * UN + dc * NS + 1)
                act.activation(Du[:, dc, :], u[:, dc, :], ACT.Copy, scale=col(dsk, dc)).then_inc(s_Du, 1)

        def c_jobs(n, family, chunk):
            use(f"C{n}", family, "c_mm", n, lambda it: (s_cb, chunk(it) * NS + n + 1))

            @job("pe", "c_mm", family, n)
            def _(pe, it, kind):
                ps = claim(pe, f"C{n}", family, it, kind)
                wait(pe, s_stk, chunk(it) * 6 + 6)
                bcast(pe, ps[:, :], stackN, NS + n).then_inc(s_cm, 1)

            @job("act", "c_copy", family, n)
            def _(act, it, kind):
                p = chunk(it)
                wait(act, s_cm, p * NS + n + 1)
                wait(act, s_g, p * UN - NS + n + 1)
                act.activation(Cb[:, n, :], bank(f"C{n}", family)[:, :], ACT.Copy).then_inc(s_cb, 1)

        for n in range(13):
            c_jobs(n, "P", lambda it: it + 1)
        for n in range(13, NS):
            c_jobs(n, "W", lambda it: it)

        for tt in range(TT):
            use(f"Z{tt}", "Z", "z_mm", tt * KC, lambda it, tt=tt: (s_zc, it * TT + tt + 1))
            for kc in range(KC):
                @job("pe", "z_mm", "Z", tt * KC + kc)
                def _(pe, it, kind, tt=tt, kc=kc):
                    if kc == 0:
                        claim(pe, f"Z{tt}", "Z", it, kind)
                    mm = pe.matmul(bank(f"Z{tt}", "Z")[:, :], xnT[:, kc, tt * P:(tt + 1) * P], win[:, kc, DI:],
                                   start=(kc == 0), stop=(kc == KC - 1))
                    if kc == KC - 1:
                        mm.then_inc(s_zm, 1)

            @job("act", "z_copy", "Z", tt)
            def _(act, it, kind, tt=tt):
                wait(act, s_zm, it * TT + tt + 1)
                act.activation(zs[:, tt, :], bank(f"Z{tt}", "Z")[:, :], ACT.Copy).then_inc(s_zc, 1)

        @job("act", "z_silu", "Z")
        def _(act, it, kind):
            wait(act, s_zc, (it + 1) * TT)
            act.activation(zs[:, :, :], zs[:, :, :], ACT.Silu).then_inc(s_z, 1)

        def gate(dve, it, dc):
            wait(dve, s_z, it + 1)
            wait(dve, s_tr, it * UN + (dc + 1) * NS)
            z = zs[:, :, dc * P:(dc + 1) * P]
            dve.tensor_tensor(z, z, psY[dc % 2][:, :].rearrange("p (a b) -> p a b", a=TT), ALU.mult).then_inc(s_gate, 1)

        for dc in range(DC - 1):
            job("dve", "gate", "Z", dc)(lambda dve, it, kind, dc=dc: gate(dve, it, dc))
        job("dve", "gate", "E", DC - 1)(lambda dve, it, kind: gate(dve, it - 1, DC - 1))

        for tt in range(TT):
            use(f"ET{tt}", "E", "e_tr", tt, lambda it, tt=tt: (s_et, (it - 1) * TT + tt + 1))
            use(f"EO{tt}", "E", "e_mm", tt, lambda it, tt=tt: (s_eo, (it - 1) * TT + tt + 1))

            @job("pe", "e_tr", "E", tt)
            def _(pe, it, kind, tt=tt):
                ps = claim(pe, f"ET{tt}", "E", it, kind)
                wait(pe, s_gate, it * DC)
                for dc in range(DC):
                    mm = pe.matmul(ps[:, dc * P:(dc + 1) * P], zs[:, tt, dc * P:(dc + 1) * P], ident[:, :],
                                   start=True, stop=True, is_transpose=True)
                mm.then_inc(s_etm, 1)

            @job("act", "e_trc", "E", tt)
            def _(act, it, kind, tt=tt):
                j = (it - 1) * TT + tt
                wait(act, s_etm, j + 1)
                if tt == 0:
                    wait(act, s_zero, 16)
                wait(act, s_eom, (it - 1) * TT + max(tt - 1, 0))
                act.activation(ygT[:, tt % 2, :, :], bank(f"ET{tt}", "E")[:, :].rearrange("p (a b) -> p a b", a=DC),
                               ACT.Copy).then_inc(s_et, 1)

            @job("pe", "e_mm", "E", tt)
            def _(pe, it, kind, tt=tt):
                ps = claim(pe, f"EO{tt}", "E", it, kind)
                wait(pe, s_et, (it - 1) * TT + tt + 1)
                for dc in range(DC):
                    mm = pe.matmul(ps[:, 0:D], ygT[:, tt % 2, dc, :], wout[:, dc, :], start=(dc == 0), stop=(dc == DC - 1))
                mm.then_inc(s_eom, 1)

            @job("act", "e_copy", "E", tt)
            def _(act, it, kind, tt=tt):
                wait(act, s_eom, (it - 1) * TT + tt + 1)
                if tt == 0:
                    wait(act, s_om, 16 * (it - 1))
                act.activation(om[:, tt, :], bank(f"EO{tt}", "E")[:, 0:D], ACT.Copy).then_inc(s_eo, 1)

        @job("sp", "e_store", "E")
        def _(sp, it, kind):
            wait(sp, s_eo, it * TT)
            sp.dma_start(om_d[bass.ds((it - 1) * T, T), :].rearrange("(a p) d -> p a d", p=P), om[:, :, :]).then_inc(s_om, 16)

        for i in range(TILES):
            @job("sp", "s_load", "S", i)
            def _(sp, it, kind, i=i):
                r = i % 4
                wait(sp, s_sc[r], 32 * (i // 4))
                sp.dma_start(xsrc[:, r, :], xn_d[i * P:(i + 1) * P, :]).then_inc(s_scl[r], 16)
            for k in range(2):
                @job("pool", "s_put", "S", 2 * i + k)
                def _(pool, it, kind, i=i, k=k):
                    r = i % 4
                    wait(pool, s_scl[r], 16 * (i // 4 + 1))
                    if i == 0 and k == 0:
                        wait(pool, s_zero, 16)
                    pool.indirect_dma_start(
                        out=xs_d[:, :], out_offset=bass.IndirectOffsetOnAxis(ap=slots[:, k, i:i + 1], axis=0),
                        in_=xsrc[:, r, :], in_offset=None).then_inc(s_sc[r], 16)

        def get_rows(pool, g, e, tt):
            i = g * TT + tt
            pool.indirect_dma_start(
                out=fy[g][e][:, tt, :], out_offset=None, in_=ys_d[:, :],
                in_offset=bass.IndirectOffsetOnAxis(ap=slots[:, e, i:i + 1], axis=0)).then_inc(s_fg[g], 16)

        for j in range(NC // 2 * 2 * TT):
            @job("pool", "g_get", "G", j)
            def _(pool, it, kind, j=j):
                if j == 0:
                    wait(pool, s_ys, 16 * (MT // GT))
                    wait(pool, s_m1, MT // 2)
                get_rows(pool, j // (2 * TT), j // TT % 2, j % TT)

        def in_kind(q, kind):
            return kind == MID or q * GT < MT - (NC - 2) * NG * GT

        for q in range(NG):
            def group(it, q=q):
                return (it - 1) * NG + q

            def tile0(it, q=q):
                return (it - 1) * (NG * GT) + q * GT

            def mjob(engine, step, k=0, n=1, q=q):
                def add(fn):
                    def run(eng, it, kind):
                        if in_kind(q, kind):
                            fn(eng, it)
                    job(engine, step, "M", q * n + k)(run)
                return add

            def pair0(it, q=q):
                return (it - 1) * (NG * GT // 2) + q * (GT // 2)

            @mjob("sp", "m_load")
            def _(sp, it, group=group, tile0=tile0, pair0=pair0, q=q):
                if q == 0:
                    for r in range(4):
                        wait(sp, s_sc[r], 32 * (TILES // 4))
                wait(sp, s_t1, pair0(it))
                sp.dma_start(xg[:, :, :], xs_d[bass.ds(tile0(it) * P, GT * P), :].rearrange("(a p) d -> p a d", p=P)).then_inc(s_xg, 16)
                for j in range(GT):
                    e = sp.value_load(etab[0:1, bass.ds(tile0(it) + j, 1)], min_val=0, max_val=E - 1)
                    if j == 0:
                        wait(sp, s_m2, pair0(it))
                    sp.dma_start(w2r[:, j, :, :], W2[bass.ds(e, 1), :, :].rearrange("a (k p) o -> p (a k) o", p=P)).then_inc(s_w2, 16)

            for h in range(GT // 2):
                @mjob("pe", "m_t1", h, 2)
                def _(pe, it, h=h, group=group, pair0=pair0):
                    pr = pair0(it) + h
                    if h == 0:
                        pe.wait_ge(s_w["w1"], 16)
                        pe.wait_ge(s_w["bias"], 48)
                        wait(pe, s_xg, 16 * (group(it) + 1))
                        wait(pe, s_my, pr)
                    else:
                        wait(pe, s_mn, pr)
                    for a in range(2):
                        for kc in range(KC):
                            mm = pe.matmul(psE[:, (a * KC + kc) * P:(a * KC + kc + 1) * P],
                                           xg[:, 2 * h + a, kc * P:(kc + 1) * P], ident[:, :],
                                           start=True, stop=True, is_transpose=True)
                    mm.then_inc(s_t1, 1)

                @mjob("act", "m_t1c", h, 2)
                def _(act, it, h=h, pair0=pair0):
                    wait(act, s_t1, pair0(it) + h + 1)
                    act.activation(xgT[:, :, :, :], psE[:, :].rearrange("p (a k t) -> p a k t", a=2, k=KC), ACT.Copy).then_inc(s_mx, 1)

                for a in range(2):
                    @mjob("pe", "m_w1", 2 * h + a, 4)
                    def _(pe, it, h=h, a=a, pair0=pair0, tile0=tile0):
                        e = pe.value_load(etab[0:1, bass.ds(tile0(it) + 2 * h + a, 1)], min_val=0, max_val=E - 1)
                        if a == 0:
                            wait(pe, s_mx, pair0(it) + h + 1)
                        dst = psE[:, a * D:(a + 1) * D]
                        for kc in range(KC):
                            pe.matmul(dst, xgT[:, a, kc, :], w1[:, bass.ds(e, 1), kc, :].rearrange("p a d -> p (a d)"),
                                      start=(kc == 0), stop=False)
                        mm = pe.matmul(dst, pick6[:, 0, :], bias6[:, bass.ds(e * D, D)], start=False, stop=True)
                        if a == 1:
                            mm.then_inc(s_m1, 1)

                @mjob("dve", "m_bn", h, 2)
                def _(dve, it, h=h, pair0=pair0):
                    pr = pair0(it) + h
                    wait(dve, s_m1, pr + 1)
                    for a in range(2):
                        dve.bn_stats(st[:, 0, a, :], psE[:, a * D:(a + 1) * D]).then_inc(s_mbn, 1)
                    wait(dve, s_mbn, 2 * pr + 2)
                    plain(dve)
                    for a in range(2):
                        dve.bn_aggr(mv[:, 0, a, :], st[:, 0, a, :]).then_inc(s_mag, 1)

                @mjob("pool", "m_rstd", h, 2)
                def _(pool, it, h=h, pair0=pair0):
                    pr = pair0(it) + h
                    wait(pool, s_mag, 2 * pr + 2)
                    plain(pool)
                    pool.tensor_scalar(ve[:, 0, 0:2], mv[:, 0, 0:2, 1], EPS, None, ALU.add).then_inc(s_mve, 1)
                    wait(pool, s_mve, pr + 1)
                    pool.tensor_tensor(rstd[:, 0, 0:2], ve[:, 0, 0:2], mhalf[:, 0:2], ALU.pow).then_inc(s_mrs, 1)

                @mjob("dve", "m_hn", h, 2)
                def _(dve, it, h=h, pair0=pair0):
                    wait(dve, s_mrs, pair0(it) + h + 1)
                    for a in range(2):
                        dve.tensor_scalar(hn[:, a, :], psE[:, a * D:(a + 1) * D], mv[:, 0, a, 0:1], rstd[:, 0, a:a + 1],
                                          ALU.subtract, ALU.mult).then_inc(s_mh, 1)

                @mjob("pe", "m_t2", h, 2)
                def _(pe, it, h=h, pair0=pair0):
                    wait(pe, s_mh, 2 * (pair0(it) + h) + 2)
                    for a in range(2):
                        for kc in range(KC):
                            mm = pe.matmul(psE[:, (a * KC + kc) * P:(a * KC + kc + 1) * P],
                                           hn[:, a, kc * P:(kc + 1) * P], ident[:, :],
                                           start=True, stop=True, is_transpose=True)
                    mm.then_inc(s_t2, 1)

                @mjob("act", "m_t2c", h, 2)
                def _(act, it, h=h, pair0=pair0):
                    pr = pair0(it) + h
                    wait(act, s_t2, pr + 1)
                    if h == 0:
                        wait(act, s_m2, pr)
                    act.activation(hnT[:, 2 * h:2 * h + 2, :, :], psE[:, :].rearrange("p (a k t) -> p a k t", a=2, k=KC),
                                   ACT.Copy).then_inc(s_mn, 1)

            @mjob("act", "m_gelu")
            def _(act, it, tile0=tile0, pair0=pair0):
                t = tile0(it)
                for j in range(GT):
                    e = act.value_load(etab[0:1, bass.ds(t + j, 1)], min_val=0, max_val=E - 1)
                    if j == 0:
                        wait(act, s_mn, pair0(it) + 2)
                    for kc in range(KC):
                        ins = act.activation(hnT[:, j, kc, :], hnT[:, j, kc, :], ACT.Gelu,
                                             scale=g1t[:, bass.ds(e, 1), kc], bias=be1t[:, bass.ds(e, 1), kc])
                    ins.then_inc(s_mg, 1)

            for j in range(GT):
                @mjob("pe", "m_w2", j, 4)
                def _(pe, it, j=j, tile0=tile0, group=group, pair0=pair0):
                    t, h, a = tile0(it), j // 2, j % 2
                    e = pe.value_load(etab[0:1, bass.ds(t + j, 1)], min_val=0, max_val=E - 1)
                    wait(pe, s_mg, t + j + 1)
                    if j == 0:
                        wait(pe, s_w2, 16 * GT * (group(it) + 1))
                    elif j == 2:
                        wait(pe, s_my, pair0(it) + 1)
                    dst = psE[:, a * D:(a + 1) * D]
                    for kc in range(KC):
                        pe.matmul(dst, hnT[:, j, kc, :], w2r[:, j, kc, :], start=(kc == 0), stop=False)
                    mm = pe.matmul(dst, pick6[:, 1, :], bias6[:, bass.ds(e * D, D)], start=False, stop=True)
                    if a == 1:
                        mm.then_inc(s_m2, 1)

            for h in range(GT // 2):
                @mjob("act", "m_yo", h, 2)
                def _(act, it, h=h, pair0=pair0, group=group):
                    wait(act, s_m2, pair0(it) + h + 1)
                    if h == 0:
                        wait(act, s_ys, 16 * group(it))
                    act.activation(yo[:, 2 * h:2 * h + 2, :], psE[:, :].rearrange("p (a d) -> p a d", a=2), ACT.Copy).then_inc(s_my, 1)

            @mjob("sp", "m_store")
            def _(sp, it, tile0=tile0, pair0=pair0):
                wait(sp, s_my, pair0(it) + 2)
                sp.dma_start(ys_d[bass.ds(tile0(it) * P, GT * P), :].rearrange("(a p) d -> p a d", p=P), yo[:, :, :]).then_inc(s_ys, 16)

        in_order = [uses[j] for j in sorted(range(len(uses)), key=lambda j: uses_at[j])]
        place = {u[:2]: j for j, u in enumerate(in_order)}

        units = {
            "pe": [(pe_unit, LEAD_B), (pe_sum, -LAG)],
            "act": [(act_unit, LEAD_A)],
            "dve": [(dve_product, 0), (dve_scan, 0)],
            "pool": [],
            "sp": [],
        }

        def unit_steps(name, eng, it, kind, slot):
            for fn, off in units[name]:
                s = slot + off
                if 0 <= s < UN:
                    fn(eng, it, s)
                elif s >= UN and kind != LAST:
                    fn(eng, it + 1, s - UN)
                elif s < 0 and kind != FIRST:
                    fn(eng, it - 1, s + UN)

        def side(name, eng, it, kind, slot):
            for family, fn in jobs[name][slot]:
                if present(family, kind):
                    fn(eng, it, kind)

        def next_stack(dve, it):
            wait(dve, s_stk, it * 6 + 6)
            wait(dve, s_bbc, it * UN)
            dve.tensor_copy(stack[:, :], stackN[:, :]).then_inc(s_stack, 1)

        def body(name, eng, it, kind):
            for s in range(UN):
                if name not in ("dve", "pool"):
                    unit_steps(name, eng, it, kind, s)
                    side(name, eng, it, kind, s)
                elif s % 2 == 0 and name == "pool":
                    pool_units(eng, it, s)
                    for k in (s, s + 1):
                        side(name, eng, it, kind, k)
                elif s % 2 == 0:
                    for fn in (dve_product, dve_scan, dve_hc):
                        if fn is dve_hc and s == UN - 2 and kind != LAST:
                            next_stack(eng, it + 1)
                        fn(eng, it, s)
                        fn(eng, it, s + 1)
                    for k in (s, s + 1):
                        side(name, eng, it, kind, k)

        def prologue(name, eng, first=0, last=None):
            todo = [fn for s in range(UN) for family, fn in jobs[name][s] if present(family, "pre")]
            for fn in todo[first:last]:
                fn(eng, -1, "pre")

        def chunks(name, eng):
            if name == "dve":
                next_stack(dve=eng, it=0)
            for s in range(-LEAD_A, 0):
                for fn, off in units[name]:
                    if s + off >= 0:
                        fn(eng, 0, s + off)
            body(name, eng, 0, FIRST)
            with eng.Fori(1, NC - 1) as it:
                body(name, eng, it, MID)
            body(name, eng, NC - 1, LAST)
            for s in range(UN, UN + LAG):
                for fn, off in units[name]:
                    if off < 0 and s + off < UN:
                        fn(eng, NC - 1, s + off)

        def epilogue(name, eng):
            for s in range(UN):
                side(name, eng, NC, "post", s)

        NBIG = 2 + 3 + 2 * KC + 4 + 2
        NCONST = 7

        block = ctx.enter_context(nc.Block())

        @block.sync
        def _(sp):
            for s in ahead:
                sp.sem_inc(s, 1)
            xt = x.rearrange("(g a p) d -> g p a d", p=P, a=TT)

            def load_x(g, k):
                sp.dma_start(xraw[k], xt[bass.ds(g, 1)].rearrange("g p a d -> (g p) a d")).then_inc(s_xl[k], 16)

            load_x(0, 0)
            sp.dma_start(wr[:, :, :], Wr.rearrange("(k p) e -> p k e", p=P)).then_inc(s_w["early"], 16)
            sp.dma_start(brc[:, :], br.rearrange("(e a) -> e a", a=1)).then_inc(s_w["early"], 16)
            for k in range(1, NK):
                load_x(k, k)

            def norm_stores(i, more):
                for k in range(NK):
                    wait(sp, s_xn, i * (NK * TT) + (k + 1) * TT)
                    if more:
                        load_x(NK * i + k + NK, k)
                    sp.dma_start(xn_d[bass.ds((NK * i + k) * T, T), :].rearrange("(a p) d -> p a d", p=P), xnb[k]).then_inc(s_xst[k], 16)
                    wait(sp, s_te, i * (2 * NK) + 2 * k + 2)
                    sp.dma_start(xnT_d[bass.ds(NK * i + k, 1)].rearrange("g p k t -> (g p) k t"), xnTg[k]).then_inc(s_tst[k], 16)

            with sp.Fori(0, NC // NK - 1) as i:
                norm_stores(i, True)
            norm_stores(NC // NK - 1, False)
            wait(sp, s_tst[0], 16)
            prologue("sp", sp)
            sp.wait_ge(s_rt, 5)
            for b in range(2):
                for k in range(3):
                    sp.dma_start(b_d[3 * b + k, :].rearrange("(p d) -> p d", d=64), bparts[k][64 * b:64 * b + 64, :]).then_inc(s_w["bst"], 16)
            for k in range(NK):
                wait(sp, s_xst[k], 16 * (NC // NK))
                wait(sp, s_tst[k], 16 * (NC // NK))
            chunks("sp", sp)

            def load_x(g):
                sp.dma_start(fx[g], xt[g]).then_inc(s_fx[g], 16)

            def load_m(g):
                wait(sp, s_om, 16 * (g + 1))
                sp.dma_start(fm[g], om_d[g * T:(g + 1) * T, :].rearrange("(a p) d -> p a d", p=P)).then_inc(s_fx[g], 16)

            wait(sp, s_m2, MT // 2)
            for g in range(NC // 2):
                load_x(g)
            wait(sp, s_g, NC * UN)
            for g in range(NC - 1):
                load_m(g)
            for g in range(NC // 2, NC):
                load_x(g)
            epilogue("sp", sp)
            load_m(NC - 1)
            for g in range(NC):
                wait(sp, s_fd, g + 1)
                sp.dma_start(out[g * T:(g + 1) * T, :].rearrange("(a p) d -> p a d", p=P), fx[g]).then_inc(s_fo, 16)
            wait(sp, s_fo, 16 * NC)
            wait(sp, s_ys, 16 * (MT // GT))

        @block.gpsimd
        def _(pool):
            pool.memset(ident[:, :], 0.0).then_inc(s_const, 1)
            pool.memset(upper[:, :], 0.0).then_inc(s_const, 1)
            pool.memset(sel[:, :], 0.0).then_inc(s_const, 1)
            pool.memset(pick6[:, :, :], 1.0).then_inc(s_const, 1)
            pool.memset(reset, 1.0).then_inc(s_const, 1)
            pool.wait_ge(s_const, 5)
            ev = reset.rearrange("p (e i) -> p e i", i=TILES)
            pool.affine_select(out=ident[:, :], in_=ident[:, :], compare_op=ALU.not_equal, fill=1.0,
                               base=0, pattern=[[-1, P]], channel_multiplier=1).then_inc(s_const, 1)
            pool.affine_select(out=upper[:, :], in_=upper[:, :], compare_op=ALU.is_ge, fill=1.0,
                               base=0, pattern=[[-1, P]], channel_multiplier=1).then_inc(s_const, 1)
            pool.affine_select(out=ev, in_=ev, compare_op=ALU.not_equal, fill=0.0,
                               base=0, pattern=[[0, E], [1, TILES]], channel_multiplier=0).then_inc(s_const, 1)
            pool.affine_select(out=pick6[:, 0, :], in_=pick6[:, 0, :], compare_op=ALU.is_ge, fill=0.0,
                               base=2, pattern=[[0, P]], channel_multiplier=-1).then_inc(s_const, 1)
            pool.affine_select(out=pick6[:, 1, :], in_=pick6[:, 1, :], compare_op=ALU.is_ge, fill=0.0,
                               base=-3, pattern=[[0, P]], channel_multiplier=1).then_inc(s_const, 1)
            for k, q in enumerate((0, 2, 3)):
                pool.affine_select(out=sel[:, :], in_=sel[:, :], compare_op=ALU.not_equal, fill=1.0,
                                   base=-32 * q, pattern=[[-1, 2 * NS]], channel_multiplier=1).then_inc(s_const, 1)
                pool.wait_ge(s_const, 11 + k)
            kw = dict(channel_multiplier=0, allow_small_or_imprecise_dtypes=True)
            pool.iota(iotaE.rearrange("p (i e) -> p i e", e=E), pattern=[[0, TILES], [1, E]], base=-E, **kw).then_inc(s_const, 1)
            pool.iota(iotaJ.rearrange("p (e j) -> p e j", e=E), pattern=[[0, E], [P, TILES]], base=0, **kw).then_inc(s_const, 1)
            pool.iota(iotaT.rearrange("p (j e) -> p j e", e=E), pattern=[[1, MT], [0, E]], base=0, **kw).then_inc(s_const, 1)
            pool.wait_ge(s_cdve, NCONST)
            with pool.Fori(0, NC // 2) as i:
                for k in range(2):
                    wait(pool, s_mv, i * (2 * TT) + (k + 1) * TT)
                    plain(pool)
                    pool.tensor_scalar(ve[:, k, :], mv[:, k, :, 1], EPS, None, ALU.add).then_inc(s_ve, 1)
                    wait(pool, s_ve, i * 2 + k + 1)
                    pool.tensor_tensor(rstd[:, k, :], ve[:, k, :], mhalf[:, :], ALU.pow).then_inc(s_rs, 1)
            prologue("pool", pool)
            wait(pool, s_route, 1)
            chunks("pool", pool)

            wait(pool, s_g, NC * UN)
            for g in range(NC // 2, NC):
                for e in range(2):
                    for tt in range(TT):
                        get_rows(pool, g, e, tt)

        @block.scalar
        def _(act):
            bts = [b1.rearrange("e (a d) -> (e a) d", d=64), b2.rearrange("e (a d) -> (e a) d", d=64)]
            for b in range(2):
                act.dma_start(om[64 * b:64 * b + 64, 0, 0:64], bts[b]).then_inc(s_w["bias"], 16)
            act.dma_start(aneg[:, :, :], A_log.rearrange("(c p) n -> p c n", p=P)).then_inc(s_a, 16)
            act.dma_start(win[:, :, :], W_in.rearrange("(k p) e -> p k e", p=P)).then_inc(s_w["big"], 16)
            act.dma_start(cw[:, :, :], conv_w.rearrange("(c p) a k -> p c (a k)", p=P)).then_inc(s_w["big"], 16)
            with nc.allow_non_contiguous_dma(reason="a few hundred scalars by channel"):
                for dst, src in ((cb, conv_b), (bdt, b_dt), (dsk, D_skip)):
                    act.dma_start(dst[:, :], src.rearrange("(c p) -> p c", p=P)).then_inc(s_w["big"], 16)
                for dst, src in ((g1t, g1), (be1t, be1)):
                    for kc in range(KC):
                        act.dma_start(dst[:, :, kc], src[:, kc * P:(kc + 1) * P].rearrange("e p -> p e")).then_inc(s_w["big"], 16)
            wx = W_xproj.rearrange("(c p) m -> p c m", p=P)
            act.wait_ge(s_wz, 1)
            act.dma_start(wxd[:, :, 32:48], wx[:, :, 0:R]).then_inc(s_w["big"], 16)
            for q in (0, 2, 3):
                act.dma_start(wxd[:, :, 32 * q:32 * q + 32], wx[:, :, R:]).then_inc(s_w["big"], 16)
            act.dma_start(wdt[32:48, :], W_dt).then_inc(s_w["big"], 16)
            act.dma_start(wout[:, :, :], W_out.rearrange("(c p) o -> p c o", p=P)).then_inc(s_w["big"], 16)
            act.wait_ge(s_a, 16)
            act.activation(aneg[:, :, :], aneg[:, :, :], ACT.Exp).then_inc(s_a, 1)
            with act.Fori(0, NC // NK) as i:
                for pair in range(0, NK, 2):
                    for k in (pair, pair + 1):
                        wait(act, s_tst[k], 16 * i)
                        for kc in range(KC):
                            wait(act, s_tp, i * (2 * NK) + 2 * k + kc + 1)
                            act.activation(xnTg[k][:, kc, :], (psB + psY)[2 * (k % 2) + kc][:, :], ACT.Copy).then_inc(s_te, 1)
                    for k in (pair, pair + 1):
                        wait(act, s_lm, i * NK + k + 1)
                        act.activation(lgT[k % 2], psP[k % 2][0:E, :], ACT.Identity, bias=brc[:, :]).then_inc(s_lc, 1)
                    for k in (pair, pair + 1):
                        wait(act, s_lv, i * NK + k + 1)
                        act.activation(lg[:, bass.ds((NK * i + k) * (TT * E), TT * E)], (psY[1], psE)[k % 2][:, 0:TT * E],
                                       ACT.Copy).then_inc(s_lg, 1)
            act.wait_ge(s_cdve, 1)
            act.dma_start(xs_d.rearrange("(p a b) d -> p a (b d)", p=P, b=4),
                          zero.unsqueeze(1).to_broadcast([P, MT // 4, 4 * D])).then_inc(s_zero, 16)
            act.wait_ge(s_w["big"], 16 * NBIG)
            prologue("act", act, 0, 2)
            act.wait_ge(s_rtd, 1)
            act.activation(scratch[:, 7, :], scratch[:, 6, :], ACT.Exp).then_inc(s_rte, 1)
            prologue("act", act, 2)
            act.wait_ge(s_w["bst"], 16 * 6)
            act.dma_start(bias6[:, :], b_d[:, :]).then_inc(s_w["bias"], 16)
            wait(act, s_route, 1)
            act.dma_start(w1[:, :, :, :], W1.rearrange("e (k p) h -> p e k h", p=P)).then_inc(s_w["w1"], 16)
            chunks("act", act)
            epilogue("act", act)

            for g in range(NC):
                wait(act, s_fg[g], 16 * 2 * TT)
                for tt in range(TT):
                    y = fy[g][0][:, tt, :]
                    ins = act.activation(y, y, ACT.Copy, scale=col(wk[:, 0, :], g * TT + tt))
                ins.then_inc(s_fs, 1)

        @block.tensor
        def _(pe):
            pe.wait_ge(s_const, 16)
            pe.wait_ge(s_cdve, NCONST)
            pe.wait_ge(s_w["early"], 32)
            with pe.Fori(0, NC // NK) as i:
                for pair in range(0, NK, 2):
                    for k in (pair, pair + 1):
                        wait(pe, s_xn, (NK * i + k + 1) * TT)
                        for kc in range(KC):
                            for tt in range(TT):
                                mm = pe.matmul((psB + psY)[2 * (k % 2) + kc][:, tt * P:(tt + 1) * P],
                                               xnb[k][:, tt, kc * P:(kc + 1) * P], ident[:, :],
                                               start=True, stop=True, is_transpose=True)
                            mm.then_inc(s_tp, 1)
                    for k in (pair, pair + 1):
                        wait(pe, s_te, (NK * i + k) * 2 + 2)
                        for kc in range(KC):
                            mm = pe.matmul(psP[k % 2][0:E, :], wr[:, kc, :], xnTg[k][:, kc, :], start=(kc == 0), stop=(kc == KC - 1))
                        mm.then_inc(s_lm, 1)
                    for k in (pair, pair + 1):
                        wait(pe, s_lc, NK * i + k + 1)
                        plain(pe)
                        for tt in range(TT):
                            mm = pe.matmul((psY[1], psE)[k % 2][:, tt * E:(tt + 1) * E], lgT[k % 2][:, tt * P:(tt + 1) * P],
                                           ident[0:E, 0:E], start=True, stop=True, is_transpose=True)
                        mm.then_inc(s_lv, 1)
            pe.wait_ge(s_w["big"], 16 * NBIG)
            wait(pe, s_lg, NC)
            prologue("pe", pe, 0, 2 * KC)
            pe.wait_ge(s_rtd, 2)
            Mb = scratch[:, 8, 0:T // 2].bitcast(BF16)
            pe.matmul(psB[0][:, :], upper[:, :], Mb, start=True, stop=True).then_inc(s_rank, 1)
            pe.matmul(psB[1][:, :], onesb[:, :], Mb, start=True, stop=True).then_inc(s_rank, 1)
            prologue("pe", pe, 2 * KC)
            wait(pe, s_route, 1)
            chunks("pe", pe)
            epilogue("pe", pe)

        @block.vector
        def _(dve):
            def const(ins):
                ins.then_inc(s_cdve, 1)

            const(dve.memset(zero, 0.0))
            dve.memset(wxd[:, :, :], 0.0).then_inc(s_wz, 1)
            const(dve.memset(onesb[:, :], 1.0))
            const(dve.memset(mhalf[:, :], -0.5))
            const(dve.memset(carry[:, :], 0.0))
            const(dve.memset(halo[:, :, :], 0.0))
            const(dve.memset(keep[:, :], 1.0))
            dve.wait_ge(s_cdve, 6)
            const(dve.memset(keep[:, 0:NC + 1:CPB], 0.0))

            bf = om[:, 0, 0:64]
            dve.wait_ge(s_w["bias"], 32)
            chain = [0]

            pre_done = [0]

            def link(ins):
                chain[0] += 1
                ins.then_inc(s_rt, 1)
                for _ in range(MIX.count(chain[0])):
                    prologue("dve", dve, pre_done[0], pre_done[0] + 1)
                    pre_done[0] += 1
                dve.wait_ge(s_rt, chain[0])

            link(dve.tensor_copy(bparts[0], bf))
            link(dve.tensor_tensor(bf, bf, bparts[0], ALU.subtract))
            link(dve.tensor_copy(bparts[1], bf))
            link(dve.tensor_tensor(bf, bf, bparts[1], ALU.subtract))
            link(dve.tensor_copy(bparts[2], bf))

            dve.wait_ge(s_a, 17)
            link(dve.tensor_scalar(aneg[:, :, :], aneg[:, :, :], -1.0, None, ALU.mult))

            with dve.Fori(0, NC // NK) as i:
                for pair in range(0, NK, 2):
                    for k in (pair, pair + 1):
                        wait(dve, s_xl[k], 16 * (i + 1))
                        for tt in range(TT):
                            dve.bn_stats(st[:, k % 2, tt, :], xraw[k][:, tt, :]).then_inc(s_bn, 1)
                        wait(dve, s_bn, i * (NK * TT) + (k + 1) * TT)
                        plain(dve)
                        for tt in range(TT):
                            dve.bn_aggr(mv[:, k % 2, tt, :], st[:, k % 2, tt, :]).then_inc(s_mv, 1)
                    for k in (pair, pair + 1):
                        wait(dve, s_rs, i * NK + k + 1)
                        wait(dve, s_xst[k], 16 * i)
                        wait(dve, s_tst[k], 16 * i)
                        for tt in range(TT):
                            dve.tensor_scalar(xnb[k][:, tt, :], xraw[k][:, tt, :], mv[:, k % 2, tt, 0:1],
                                              rstd[:, k % 2, tt:tt + 1], ALU.subtract, ALU.mult).then_inc(s_xn, 1)

            def row(k):
                return scratch[:, k, :]

            def ie(ap):
                return ap.rearrange("p (i e) -> p i e", e=E)

            def ei(ap):
                return ap.rearrange("p (e i) -> p e i", e=E)

            def over_e(ap):
                return ap.unsqueeze(2).to_broadcast([P, TILES, E])

            def s32(k):
                return small[:, k, :]

            def s16(k):
                return small[:, k, 0:E]

            dve.wait_ge(s_const, 16)
            wait(dve, s_lg, NC)
            logits = lg

            def onehot(src, top, first, oh, t0, t1):
                link(dve.tensor_reduce(top, ie(src), AX.X, ALU.max))
                link(dve.tensor_tensor(ie(t0), ie(src), over_e(top), ALU.is_equal))
                link(dve.tensor_tensor(t1, t0, iotaE, ALU.mult))
                link(dve.tensor_reduce(first, ie(t1), AX.X, ALU.min))
                link(dve.tensor_tensor(ie(oh), ie(iotaE), over_e(first), ALU.is_equal))

            oh1, oh2 = row(2), row(5)
            onehot(logits, s32(0), s32(1), oh1, row(0), row(1))
            dve.tensor_tensor(ie(row(6)), ie(logits), over_e(s32(0)), ALU.subtract).then_inc(s_rtd, 1)
            link(dve.tensor_scalar(row(3), oh1, -2 * BIG, BIG, ALU.mult, ALU.add))
            link(dve.tensor_tensor(row(4), logits, row(3), ALU.min))
            onehot(row(4), s32(2), s32(3), oh2, row(0), row(1))
            dve.tensor_tensor(scratch[:, 8, 0:T // 2].bitcast(BF16), oh1, oh2, ALU.add).then_inc(s_rtd, 1)
            dve.wait_ge(s_rte, 1)
            link(dve.tensor_reduce(s32(4), ie(row(7)), AX.X, ALU.add))
            link(dve.reciprocal(s32(4), s32(4)))
            for k, oh in enumerate((oh1, oh2)):
                link(dve.tensor_tensor(row(0), row(7), oh, ALU.mult))
                link(dve.tensor_reduce(s32(5 + k), ie(row(0)), AX.X, ALU.add))
                link(dve.tensor_tensor(s32(5 + k), s32(5 + k), s32(4), ALU.mult))
            link(dve.tensor_tensor(s32(7), s32(5), s32(6), ALU.add))
            link(dve.tensor_scalar(s32(7), s32(7), 1e-9, None, ALU.max))
            link(dve.reciprocal(s32(7), s32(7)))
            for k in range(2):
                link(dve.tensor_tensor(wk[:, k, :], s32(5 + k), s32(7), ALU.mult))
            dve.wait_ge(s_rank, 2)
            link(dve.tensor_copy(ei(row(9)), psB[1][:, :].rearrange("p (i e) -> p e i", e=E)))
            link(dve.tensor_tensor_scan(row(11), reset, row(9), 0.0, ALU.mult, ALU.add))
            link(dve.tensor_tensor(row(12), row(11), row(9), ALU.subtract))
            count = ei(row(11))[:, :, TILES - 1]
            link(dve.tensor_tensor(ei(row(13)), count.unsqueeze(2).to_broadcast([P, E, TILES]), ei(iotaJ), ALU.is_gt))
            link(dve.tensor_reduce(s16(8), ei(row(13)), AX.X, ALU.add))
            link(dve.memset(s16(11), 1.0))
            link(dve.tensor_tensor_scan(s16(9), s16(11), s16(8), 0.0, ALU.mult, ALU.add))
            link(dve.tensor_tensor(s16(10), s16(9), s16(8), ALU.subtract))
            link(dve.tensor_scalar(s16(10), s16(10), float(P), None, ALU.mult))
            link(dve.tensor_tensor(ei(row(14)), ei(row(12)), s16(10).unsqueeze(2).to_broadcast([P, E, TILES]), ALU.add))
            link(dve.tensor_tensor(ie(row(15)), ie(psB[0][:, :]), row(14).rearrange("p (e i) -> p i e", e=E), ALU.add))
            for k, oh in enumerate((oh1, oh2)):
                link(dve.tensor_tensor(row(0), row(15), oh, ALU.mult))
                link(dve.tensor_reduce(s32(5), ie(row(0)), AX.X, ALU.add))
                link(dve.tensor_copy(slots[:, k, :], s32(5)))
            cmp_t = w1_flat[:, 0:MT * E].rearrange("p (j e) -> p j e", e=E)
            link(dve.tensor_tensor(cmp_t, s16(9).unsqueeze(1).to_broadcast([P, MT, E]),
                                   iotaT.rearrange("p (j e) -> p j e", e=E), ALU.is_le))
            tf = w1_flat[:, 2048:2048 + MT]
            link(dve.tensor_reduce(tf, cmp_t, AX.X, ALU.add))
            link(dve.tensor_scalar(tf, tf, float(E - 1), None, ALU.min))
            link(dve.tensor_copy(etab[:, :], tf))
            prologue("dve", dve, pre_done[0])
            for k in range(NK):
                wait(dve, s_xst[k], 16 * (NC // NK))
                wait(dve, s_tst[k], 16 * (NC // NK))
            dve.memset(small[:, 0, 0:1], 0.0).then_inc(s_route, 1)
            chunks("dve", dve)

            epilogue("dve", dve)

            def add_first(g):
                wait(dve, s_fs, g + 1)
                wait(dve, s_fa, (g + 1) * (1 + TT))
                dve.tensor_tensor(fx[g], fx[g], fy[g][0], ALU.add).then_inc(s_fd, 1)

            for g in range(NC):
                wait(dve, s_fx[g], 32)
                dve.tensor_tensor(fx[g], fx[g], fm[g], ALU.add).then_inc(s_fa, 1)
                wait(dve, s_fg[g], 16 * 2 * TT)
                wait(dve, s_fa, g * (1 + TT) + 1)
                for tt in range(TT):
                    o = fx[g][:, tt, :]
                    dve.scalar_tensor_tensor(out=o, in0=fy[g][1][:, tt, :], scalar=col(wk[:, 1, :], g * TT + tt), in1=o,
                                             op0=ALU.mult, op1=ALU.add).then_inc(s_fa, 1)
                if g >= 2:
                    add_first(g - 2)
            for g in (NC - 2, NC - 1):
                add_first(g)


_INS = ["L0_attn_x", "L0_attn_W_in", "L0_attn_conv_w", "L0_attn_conv_b", "L0_attn_W_xproj", "L0_attn_W_dt",
        "L0_attn_b_dt", "L0_attn_A_log", "L0_attn_D_skip", "L0_attn_W_out", "L0_ffn_Wr", "L0_ffn_br",
        "L0_ffn_W1", "L0_ffn_b1", "L0_ffn_g1", "L0_ffn_be1", "L0_ffn_W2", "L0_ffn_b2"]


def kernel(**inputs):
    import numpy as np
    import concourse.bacc as bacc
    from concourse.bass_utils import run_bass_kernel_spmd as run

    nc = bacc.Bacc("TRN2", target_bir_lowering=False, num_devices=1)
    arrays, args = {}, []
    for name in _INS:
        a = np.ascontiguousarray(inputs[name])
        if name == "L0_attn_x":
            a = a.reshape(NT, D)
        arrays[f"in_{name}"] = a
        args.append(nc.dram_tensor(f"in_{name}", a.shape, mybir.dt.from_np(a.dtype), kind="ExternalInput").ap())
    args.append(nc.dram_tensor("out", (NT, D), F32, kind="ExternalOutput").ap())
    build(nc, *args)
    r = run(nc, [arrays], core_ids=[0])
    return r.results[0]["out"].reshape(NB, L, D)
```
